# Optimizing a Trainium2 kernel written in Bass

```python
import numpy as np
import jax
import jax.numpy as jnp

def _softmax(x, axis=-1):
    return jax.nn.softmax(x, axis=axis)

def _gelu(x):
    return jax.nn.gelu(x, approximate=True)

def _silu(x):
    return jax.nn.silu(x)

def _sigmoid(x):
    return jax.nn.sigmoid(x)

def _layernorm(x, axis=-1, eps=1e-05):
    m = jnp.mean(x, axis=axis, keepdims=True)
    v = jnp.var(x, axis=axis, keepdims=True)
    return (x - m) / jnp.sqrt(v + eps)

def _scatter_add(tgt, idx, src, axis=0):
    return tgt.at[idx].add(src)

def _segment_sum(src, seg, n):
    return jax.ops.segment_sum(src, seg, n)
kernel_name = 'mk_hybrid_d2_jaxref_r8_d91d5f'

def setup_inputs(seed: int=0):
    np.random.seed(seed)
    _w = jnp.asarray

    def _L0_attn_a_setup():
        import jax, jax.numpy as jnp
        import numpy as np
        D_MODEL = 128
        NUM_HEADS = 16
        MAX_LEN = 256
        BATCH = 2
        SEQ_LEN = 256
        key = jax.random.key(seed)
        ks = jax.random.split(key, 6)
        s = 0.02
        return {'x': jax.random.normal(ks[0], (BATCH, SEQ_LEN, D_MODEL), dtype=jnp.float32), 'Wq': jax.random.normal(ks[1], (D_MODEL, D_MODEL), dtype=jnp.float32) * s, 'bq': jnp.zeros((D_MODEL,), dtype=jnp.float32), 'Wk': jax.random.normal(ks[2], (D_MODEL, D_MODEL), dtype=jnp.float32) * s, 'bk': jnp.zeros((D_MODEL,), dtype=jnp.float32), 'Wv': jax.random.normal(ks[3], (D_MODEL, D_MODEL), dtype=jnp.float32) * s, 'bv': jnp.zeros((D_MODEL,), dtype=jnp.float32), 'rel_emb': jax.random.normal(ks[4], (NUM_HEADS, 2 * MAX_LEN - 1), dtype=jnp.float32)}
    _L0_attn_a_in = _L0_attn_a_setup()

    def _L0_attn_b_setup():
        import jax, jax.numpy as jnp
        import numpy as np
        EMBED_DIM = 128
        NUM_HEADS = 16
        HEAD_DIM = EMBED_DIM // NUM_HEADS
        FEATURE_EPS = 1e-06
        DEN_EPS = 1e-06
        key = jax.random.key(seed)
        k_x, k_qw, k_qb, k_ow, k_ob = jax.random.split(key, 5)
        b, l = (2, 256)
        x = jax.random.normal(k_x, (b, l, EMBED_DIM), dtype=jnp.float32)
        s = 1.0 / np.sqrt(EMBED_DIM)
        qkv_w = jax.random.uniform(k_qw, (3 * EMBED_DIM, EMBED_DIM), minval=-s, maxval=s, dtype=jnp.float32)
        qkv_b = jax.random.uniform(k_qb, (3 * EMBED_DIM,), minval=-s, maxval=s, dtype=jnp.float32)
        out_w = jax.random.uniform(k_ow, (EMBED_DIM, EMBED_DIM), minval=-s, maxval=s, dtype=jnp.float32)
        out_b = jax.random.uniform(k_ob, (EMBED_DIM,), minval=-s, maxval=s, dtype=jnp.float32)
        return {'x': x, 'qkv_w': qkv_w, 'qkv_b': qkv_b, 'out_w': out_w, 'out_b': out_b}
    _L0_attn_b_in = _L0_attn_b_setup()

    def _L0_ffn_setup():
        import jax, jax.numpy as jnp
        import numpy as np
        B, T, D, E, H = (8, 256, 128, 8, 32)
        LN_EPS = 1e-05
        key = jax.random.key(seed)
        ks = jax.random.split(key, 4)
        return {'x': jax.random.normal(ks[0], (B, T, D), dtype=jnp.float32), 'Wg': jax.random.normal(ks[1], (E, D), dtype=jnp.float32) * 0.02, 'ln_scale': jnp.ones((E, D), dtype=jnp.float32), 'ln_bias': jnp.zeros((E, D), dtype=jnp.float32), 'W1': jax.random.normal(ks[2], (E, D, H), dtype=jnp.float32) * 0.02, 'b1': jnp.zeros((E, H), dtype=jnp.float32), 'W2': jax.random.normal(ks[3], (E, H, D), dtype=jnp.float32) * 0.02, 'b2': jnp.zeros((E, D), dtype=jnp.float32)}
    _L0_ffn_in = _L0_ffn_setup()

    def _L1_attn_a_setup():
        import jax, jax.numpy as jnp
        import numpy as np
        import math
        NUM_HEADS = 16
        MAX_REL_POS = 128
        key = jax.random.key(seed)
        ks = jax.random.split(key, 6)
        B, S, H = (4, 128, 128)
        hd = H // NUM_HEADS
        sc = 1.0 / math.sqrt(H)
        return {'x': jax.random.normal(ks[0], (B, S, H), jnp.float32), 'Wq': jax.random.normal(ks[1], (H, H), jnp.float32) * sc, 'bq': jnp.zeros((H,), jnp.float32), 'Wk': jax.random.normal(ks[2], (H, H), jnp.float32) * sc, 'bk': jnp.zeros((H,), jnp.float32), 'Wv': jax.random.normal(ks[3], (H, H), jnp.float32) * sc, 'bv': jnp.zeros((H,), jnp.float32), 'Wo': jax.random.normal(ks[4], (H, H), jnp.float32) * sc, 'bo': jnp.zeros((H,), jnp.float32), 'rel_emb': jax.random.normal(ks[5], (2 * MAX_REL_POS + 1, hd), jnp.float32) * 0.02}
    _L1_attn_a_in = _L1_attn_a_setup()

    def _L1_attn_b_setup():
        import jax, jax.numpy as jnp
        import numpy as np
        D_MODEL, N_HEADS, D_HEAD = (128, 16, 64)
        B, T = (4, 256)
        key = jax.random.key(seed)
        k1, k2, k3 = jax.random.split(key, 3)
        x = jax.random.normal(k1, (B, T, D_MODEL), dtype=jnp.float32)
        w_qkv = jax.random.normal(k2, (3 * N_HEADS * D_HEAD, D_MODEL), dtype=jnp.float32) * 0.02
        w_out = jax.random.normal(k3, (D_MODEL, N_HEADS * D_HEAD), dtype=jnp.float32) * 0.02
        return {'x': x, 'w_qkv': w_qkv, 'w_out': w_out}
    _L1_attn_b_in = _L1_attn_b_setup()

    def _L1_ffn_setup():
        import jax, jax.numpy as jnp
        import numpy as np
        B, T, C, H, E, K = (4, 128, 128, 128, 8, 2)

        def _swiglu(x):
            a, b = jnp.split(x, 2, axis=-1)
            return jax.nn.silu(a) * b
        key = jax.random.key(seed)
        ks = jax.random.split(key, 6)
        s = 0.02
        x = jax.random.normal(ks[0], (B, T, C), jnp.float32)
        w_shared_in = jax.random.normal(ks[1], (C, 2 * H), jnp.float32) * s
        w_shared_out = jax.random.normal(ks[2], (H, C), jnp.float32) * s
        w1_shared = jax.random.normal(ks[3], (C, 2 * H), jnp.float32) * s
        w2 = jax.random.normal(ks[4], (E, H, C), jnp.float32) * s
        w_gate = jax.random.normal(ks[5], (C, E), jnp.float32) * s
        gate_bias = jnp.zeros((E,), jnp.float32)
        return {'x': x, 'w_shared_in': w_shared_in, 'w_shared_out': w_shared_out, 'w1_shared': w1_shared, 'w2': w2, 'w_gate': w_gate, 'gate_bias': gate_bias}
    _L1_ffn_in = _L1_ffn_setup()
    _d = {'L0_attn_a_x': _L0_attn_a_in['x'], 'L0_attn_a_Wq': _L0_attn_a_in['Wq'], 'L0_attn_a_bq': _L0_attn_a_in['bq'], 'L0_attn_a_Wk': _L0_attn_a_in['Wk'], 'L0_attn_a_bk': _L0_attn_a_in['bk'], 'L0_attn_a_Wv': _L0_attn_a_in['Wv'], 'L0_attn_a_bv': _L0_attn_a_in['bv'], 'L0_attn_a_rel_emb': _L0_attn_a_in['rel_emb'], 'L0_attn_b_qkv_w': _L0_attn_b_in['qkv_w'], 'L0_attn_b_qkv_b': _L0_attn_b_in['qkv_b'], 'L0_attn_b_out_w': _L0_attn_b_in['out_w'], 'L0_attn_b_out_b': _L0_attn_b_in['out_b'], 'L0_ffn_Wg': _L0_ffn_in['Wg'], 'L0_ffn_ln_scale': _L0_ffn_in['ln_scale'], 'L0_ffn_ln_bias': _L0_ffn_in['ln_bias'], 'L0_ffn_W1': _L0_ffn_in['W1'], 'L0_ffn_b1': _L0_ffn_in['b1'], 'L0_ffn_W2': _L0_ffn_in['W2'], 'L0_ffn_b2': _L0_ffn_in['b2'], 'L1_attn_a_Wq': _L1_attn_a_in['Wq'], 'L1_attn_a_bq': _L1_attn_a_in['bq'], 'L1_attn_a_Wk': _L1_attn_a_in['Wk'], 'L1_attn_a_bk': _L1_attn_a_in['bk'], 'L1_attn_a_Wv': _L1_attn_a_in['Wv'], 'L1_attn_a_bv': _L1_attn_a_in['bv'], 'L1_attn_a_Wo': _L1_attn_a_in['Wo'], 'L1_attn_a_bo': _L1_attn_a_in['bo'], 'L1_attn_a_rel_emb': _L1_attn_a_in['rel_emb'], 'L1_attn_b_w_qkv': _L1_attn_b_in['w_qkv'], 'L1_attn_b_w_out': _L1_attn_b_in['w_out'], 'L1_ffn_w_shared_in': _L1_ffn_in['w_shared_in'], 'L1_ffn_w_shared_out': _L1_ffn_in['w_shared_out'], 'L1_ffn_w1_shared': _L1_ffn_in['w1_shared'], 'L1_ffn_w2': _L1_ffn_in['w2'], 'L1_ffn_w_gate': _L1_ffn_in['w_gate'], 'L1_ffn_gate_bias': _L1_ffn_in['gate_bias']}
    _x0 = _d['L0_attn_a_x']
    _d['L0_attn_a_x'] = jax.random.normal(jax.random.fold_in(jax.random.key(seed), 1), (32, 256, 128), dtype=_x0.dtype)
    del _x0
    return _d

def reference(L0_attn_a_x, L0_attn_a_Wq, L0_attn_a_bq, L0_attn_a_Wk, L0_attn_a_bk, L0_attn_a_Wv, L0_attn_a_bv, L0_attn_a_rel_emb, L0_attn_b_qkv_w, L0_attn_b_qkv_b, L0_attn_b_out_w, L0_attn_b_out_b, L0_ffn_Wg, L0_ffn_ln_scale, L0_ffn_ln_bias, L0_ffn_W1, L0_ffn_b1, L0_ffn_W2, L0_ffn_b2, L1_attn_a_Wq, L1_attn_a_bq, L1_attn_a_Wk, L1_attn_a_bk, L1_attn_a_Wv, L1_attn_a_bv, L1_attn_a_Wo, L1_attn_a_bo, L1_attn_a_rel_emb, L1_attn_b_w_qkv, L1_attn_b_w_out, L1_ffn_w_shared_in, L1_ffn_w_shared_out, L1_ffn_w1_shared, L1_ffn_w2, L1_ffn_w_gate, L1_ffn_gate_bias):

    def _L0_attn_a_ref(x, Wq, bq, Wk, bk, Wv, bv, rel_emb):
        import jax, jax.numpy as jnp
        import numpy as np
        D_MODEL = 128
        NUM_HEADS = 16
        MAX_LEN = 256
        BATCH = 2
        SEQ_LEN = 256
        B, L, D = x.shape
        H = rel_emb.shape[0]
        dk = D // H

        def heads(y):
            return y.reshape(B, L, H, dk).transpose(0, 2, 1, 3)
        q = heads(x @ Wq + bq)
        k = heads(x @ Wk + bk)
        v = heads(x @ Wv + bv)
        scores = jnp.einsum('bhid,bhjd->bhij', q, k) / jnp.sqrt(jnp.float32(dk))
        pos = jnp.arange(L)
        rel_idx = pos[:, None] - pos[None, :] + (L - 1)
        bias = rel_emb[:, rel_idx]
        attn = jax.nn.softmax(scores + bias[None], axis=-1)
        out = jnp.einsum('bhij,bhjd->bhid', attn, v)
        return out.transpose(0, 2, 1, 3).reshape(B, L, D)

    def _L0_attn_b_ref(x, qkv_w, qkv_b, out_w, out_b):
        import jax, jax.numpy as jnp
        import numpy as np
        EMBED_DIM = 128
        NUM_HEADS = 16
        HEAD_DIM = EMBED_DIM // NUM_HEADS
        FEATURE_EPS = 1e-06
        DEN_EPS = 1e-06
        b, l, e = x.shape
        qkv = (x @ qkv_w.T + qkv_b).reshape(b, l, 3, NUM_HEADS, HEAD_DIM)
        qkv = jnp.transpose(qkv, (2, 0, 3, 1, 4))
        q, k, v = (qkv[0], qkv[1], qkv[2])
        q = jax.nn.relu(q) + FEATURE_EPS
        k = jax.nn.relu(k) + FEATURE_EPS
        kv = jnp.cumsum(jnp.einsum('bhld,bhle->bhlde', k, v), axis=2)
        k_cum = jnp.cumsum(k, axis=2)
        num = jnp.einsum('bhld,bhlde->bhle', q, kv)
        den = jnp.maximum(jnp.einsum('bhld,bhld->bhl', q, k_cum)[..., None], DEN_EPS)
        out = num / den
        out = jnp.transpose(out, (0, 2, 1, 3)).reshape(b, l, e)
        return out @ out_w.T + out_b

    def _L0_ffn_ref(x, Wg, ln_scale, ln_bias, W1, b1, W2, b2):
        import jax, jax.numpy as jnp
        import numpy as np
        B, T, D, E, H = (8, 256, 128, 8, 32)
        LN_EPS = 1e-05
        Bs, Ts, Ds = x.shape
        xt = x.reshape(Bs * Ts, Ds)
        logits = xt @ Wg.T
        top1 = jnp.argmax(logits, axis=-1)
        mu = jnp.mean(xt, axis=-1, keepdims=True)
        var = jnp.mean(jnp.square(xt - mu), axis=-1, keepdims=True)
        xhat = (xt - mu) * jax.lax.rsqrt(var + LN_EPS)
        n_experts = Wg.shape[0]

        def body(y, p):
            s_e, b_e, w1, bb1, w2, bb2, eid = p
            h = jax.nn.gelu((xhat * s_e + b_e) @ w1 + bb1, approximate=False)
            out = h @ w2 + bb2
            mask = (top1 == eid)[:, None].astype(out.dtype)
            return (y + mask * out, None)
        y0 = jnp.zeros_like(xt)
        y, _ = jax.lax.scan(body, y0, (ln_scale, ln_bias, W1, b1, W2, b2, jnp.arange(n_experts)))
        return y.reshape(Bs, Ts, Ds)

    def _L1_attn_a_ref(x, Wq, bq, Wk, bk, Wv, bv, Wo, bo, rel_emb):
        import jax, jax.numpy as jnp
        import numpy as np
        import math
        NUM_HEADS = 16
        MAX_REL_POS = 128
        B, S, H = x.shape
        nh = NUM_HEADS
        hd = H // nh
        inv_sqrt_d = 1.0 / math.sqrt(hd)

        def proj(W, b):
            return (x @ W.T + b).reshape(B, S, nh, hd).transpose(0, 2, 1, 3)
        Q = proj(Wq, bq)
        K = proj(Wk, bk)
        V = proj(Wv, bv)
        pos = jnp.arange(S)
        rel_idx = jnp.clip(pos[None, :] - pos[:, None], -MAX_REL_POS, MAX_REL_POS) + MAX_REL_POS
        E = rel_emb[rel_idx]
        scores = (jnp.einsum('bnqd,bnkd->bnqk', Q, K) + jnp.einsum('bnqd,qkd->bnqk', Q, E)) * inv_sqrt_d
        attn = jax.nn.softmax(scores, axis=-1)
        out = jnp.einsum('bnqk,bnkd->bnqd', attn, V)
        out = out.transpose(0, 2, 1, 3).reshape(B, S, H)
        return out @ Wo.T + bo

    def _L1_attn_b_ref(x, w_qkv, w_out):
        import jax, jax.numpy as jnp
        import numpy as np
        D_MODEL, N_HEADS, D_HEAD = (128, 16, 64)
        B, T = (4, 256)
        Bx, Tx, Dx = x.shape
        scale = D_HEAD ** (-0.5)
        qkv = jnp.einsum('btd,ed->bte', x, w_qkv)
        q, k, v = jnp.split(qkv, 3, axis=-1)

        def heads(t):
            return t.reshape(Bx, Tx, N_HEADS, D_HEAD).transpose(0, 2, 1, 3)
        q, k, v = (heads(q), heads(k), heads(v))
        att = jnp.einsum('bhqd,bhkd->bhqk', q, k) * scale
        causal = jnp.tril(jnp.ones((Tx, Tx), dtype=bool))
        att = jnp.where(causal, att, -jnp.inf)
        att = jax.nn.softmax(att, axis=-1)
        y = jnp.einsum('bhqk,bhkd->bhqd', att, v)
        y = y.transpose(0, 2, 1, 3).reshape(Bx, Tx, N_HEADS * D_HEAD)
        return jnp.einsum('bte,de->btd', y, w_out)

    def _L1_ffn_ref(x, w_shared_in, w_shared_out, w1_shared, w2, w_gate, gate_bias):
        import jax, jax.numpy as jnp
        import numpy as np
        B, T, C, H, E, K = (4, 128, 128, 128, 8, 2)

        def _swiglu(x):
            a, b = jnp.split(x, 2, axis=-1)
            return jax.nn.silu(a) * b
        Bx, Tx, Cx = x.shape
        S = Bx * Tx
        fx = x.reshape(S, Cx)
        shared_out = _swiglu(fx @ w_shared_in) @ w_shared_out
        logits = fx @ w_gate + gate_bias
        probs = jax.nn.softmax(logits, axis=-1)
        top_val, top_idx = jax.lax.top_k(probs, K)
        wdense = jnp.zeros((S, E), probs.dtype).at[jnp.arange(S)[:, None], top_idx].add(top_val)
        hid = _swiglu(fx @ w1_shared)
        routed_out = jnp.zeros_like(shared_out)
        for e in range(E):
            routed_out = routed_out + wdense[:, e:e + 1] * (hid @ w2[e])
        return (shared_out + routed_out).reshape(Bx, Tx, Cx)
    x = L0_attn_a_x
    x = x + _L0_attn_a_ref(_layernorm(x, axis=-1), L0_attn_a_Wq, L0_attn_a_bq, L0_attn_a_Wk, L0_attn_a_bk, L0_attn_a_Wv, L0_attn_a_bv, L0_attn_a_rel_emb)
    x = x + _L0_ffn_ref(_layernorm(x, axis=-1), L0_ffn_Wg, L0_ffn_ln_scale, L0_ffn_ln_bias, L0_ffn_W1, L0_ffn_b1, L0_ffn_W2, L0_ffn_b2)
    x = x + _L0_attn_b_ref(_layernorm(x, axis=-1), L0_attn_b_qkv_w, L0_attn_b_qkv_b, L0_attn_b_out_w, L0_attn_b_out_b)
    x = x + _L0_ffn_ref(_layernorm(x, axis=-1), L0_ffn_Wg, L0_ffn_ln_scale, L0_ffn_ln_bias, L0_ffn_W1, L0_ffn_b1, L0_ffn_W2, L0_ffn_b2)
    x = x + _L1_attn_a_ref(_layernorm(x, axis=-1), L1_attn_a_Wq, L1_attn_a_bq, L1_attn_a_Wk, L1_attn_a_bk, L1_attn_a_Wv, L1_attn_a_bv, L1_attn_a_Wo, L1_attn_a_bo, L1_attn_a_rel_emb)
    x = x + _L1_ffn_ref(_layernorm(x, axis=-1), L1_ffn_w_shared_in, L1_ffn_w_shared_out, L1_ffn_w1_shared, L1_ffn_w2, L1_ffn_w_gate, L1_ffn_gate_bias)
    x = x + _L1_attn_b_ref(_layernorm(x, axis=-1), L1_attn_b_w_qkv, L1_attn_b_w_out)
    x = x + _L1_ffn_ref(_layernorm(x, axis=-1), L1_ffn_w_shared_in, L1_ffn_w_shared_out, L1_ffn_w1_shared, L1_ffn_w2, L1_ffn_w_gate, L1_ffn_gate_bias)
    return x

_drawn_inputs = setup_inputs


def setup_inputs(seed=0):
    import zlib

    import numpy as np

    out = dict(_drawn_inputs(seed))
    spreads = {'L0_attn_a_bq': (0.0, 0.8),
     'L0_attn_a_bk': (0.0, 0.8),
     'L0_attn_a_bv': (0.0, 0.1),
     'L0_ffn_ln_scale': (1.0, 0.6),
     'L0_ffn_ln_bias': (0.0, 0.8),
     'L0_ffn_b1': (0.0, 0.463),
     'L0_ffn_b2': (0.0, 0.1),
     'L1_attn_a_bq': (0.0, 0.65),
     'L1_attn_a_bk': (0.0, 0.8),
     'L1_attn_a_bv': (0.0, 0.1),
     'L1_attn_a_bo': (0.0, 0.1),
     'L1_ffn_gate_bias': (0.0, 0.8)}
    factors = {'L0_attn_a_Wq': 8.0,
     'L0_attn_a_Wk': 8.0,
     'L1_attn_a_rel_emb': 8.0,
     'L1_ffn_w_shared_in': 5.161,
     'L1_ffn_w_shared_out': 5.157,
     'L1_ffn_w1_shared': 8.0,
     'L1_ffn_w2': 8.0,
     'L1_ffn_w_gate': 8.0}
    for name, (base, spread) in spreads.items():
        noise = np.random.default_rng([zlib.crc32(name.encode()), seed]).standard_normal(out[name].shape)
        drawn = base * np.exp(spread * noise) if base else spread * noise
        out[name] = jnp.asarray(drawn.astype(out[name].dtype))
    for name, factor in factors.items():
        out[name] = (out[name] * factor).astype(out[name].dtype)
    return out
```

```python
import numpy as np
import concourse.bass as bass
from concourse import mybir
from contextlib import ExitStack

F32 = mybir.dt.float32
BF16 = mybir.dt.bfloat16
ALU = mybir.AluOpType
ACT = mybir.ActivationFunctionType
AX = mybir.AxisListType

P = 128
D = 128
SEQ = 256
TPB = SEQ // P
NH = 16
DH = D // NH
PAD = 4
VW = 32
GH = P // VW
NG = NH // GH
NTERM = 6
Q_PART = (0, 0, 0, 1, 1, 2)
K_PART = (0, 1, 2, 0, 1, 0)
LN_EPS = 1e-5
BIG = 3.0e38


def chain(engine, sem, base):
    done = [0]

    def step(instruction):
        done[0] += 1
        instruction.then_inc(sem, 1)

    def settle(but=0):
        engine.wait_ge(sem, base + (done[0] - but))

    return step, settle, lambda: done[0]


def core(nc, ctx, n_batches):
    tiles = TPB * n_batches
    sb = lambda name, shape: ctx.enter_context(nc.sbuf_tensor(name, shape, F32))
    return {
        "nc": nc, "batches": n_batches, "tiles": tiles,
        "x": sb("x_stream", [P, tiles + PAD, D]),
        "moments": sb("moments", [P, tiles + PAD, 2]),
        "rstd": sb("rstd", [P, tiles + PAD]),
        "rstd2": sb("rstd2", [P, tiles + PAD]),
        "tmp": sb("norm_tmp", [P, 2, tiles + PAD]),
        "ident": sb("ident", [P, P]),
        "psum": ctx.enter_context(nc.psum_tensor("banks", [P, 8, 512], F32)),
    }


def load_stage(c, x_dram, ident_dram):
    nc = c["nc"]
    chunk = max(1, c["tiles"] // 8)
    n_chunks = c["tiles"] // chunk
    with nc.cleanup_on_exit(), ExitStack() as ctx:
        sem = lambda n: nc.alloc_semaphore(n)
        x_loaded = [sem(f"x_loaded{k}") for k in range(n_chunks)]
        ident_loaded, zeroed, stats_done, moments_done = sem("ident_loaded"), sem("zeroed"), sem("l_stats"), sem("l_mom")
        stats = ctx.enter_context(nc.sbuf_tensor("l_stats_sb", [P, 8, 6], F32))
        block = ctx.enter_context(nc.Block())

        @block.sync
        def _(sp):
            src = x_dram.rearrange("b (t p) d -> p (b t) d", p=P)
            for k in range(n_chunks):
                sp.dma_start(c["x"][:, k * chunk:(k + 1) * chunk, :],
                             src[:, k * chunk:(k + 1) * chunk, :]).then_inc(x_loaded[k], 16)
            sp.dma_start(c["ident"][:, :], ident_dram).then_inc(ident_loaded, 16)
            sp.wait_ge(ident_loaded, 16)

        @block.vector
        def _(dve):
            nc.vector.memset(c["x"][:, c["tiles"]:, :], 0.0).then_inc(zeroed, 1)
            nc.vector.memset(c["moments"][:, c["tiles"]:, :], 0.0).then_inc(zeroed, 1)
            for k in range(n_chunks):
                dve.wait_ge(x_loaded[k], 16)
                for t in range(k * chunk, (k + 1) * chunk):
                    if t >= 8:
                        dve.wait_ge(moments_done, t - 7)
                    nc.vector.bn_stats(stats[:, t % 8, :], c["x"][:, t, :]).then_inc(stats_done, 1)
                    if t % 4 == 3:
                        for u in range(t - 3, t + 1):
                            dve.wait_ge(stats_done, u + 1)
                            nc.vector.bn_aggr(c["moments"][:, u, :], stats[:, u % 8, :]).then_inc(moments_done, 1)
            dve.wait_ge(zeroed, 2)


def rstd_stage(c, tag, double):
    nc = c["nc"]
    with nc.cleanup_on_exit(), ExitStack() as ctx:
        sem = lambda n: nc.alloc_semaphore(n + tag)
        chain_sem, root_in, root_out = sem("r_chain"), sem("r_in"), sem("r_out")
        block = ctx.enter_context(nc.Block())
        shifted, root = c["tmp"][:, 0, :], c["tmp"][:, 1, :]

        @block.scalar
        def _(act):
            for k in range(2 if double else 1):
                act.wait_ge(root_in, k + 1)
                nc.scalar.activation(root, shifted, ACT.Sqrt).then_inc(root_out, 1)

        @block.vector
        def _(dve):
            step, settle, steps = chain(dve, chain_sem, 0)

            def newton(out):
                step(nc.vector.reciprocal(out, root))
                settle()
                step(nc.vector.tensor_tensor(root, out, out, ALU.mult))
                settle()
                step(nc.vector.tensor_tensor(root, root, shifted, ALU.mult))
                settle()
                step(nc.vector.tensor_scalar(root, root, -0.5, 1.5, ALU.mult, ALU.add))
                settle()
                step(nc.vector.tensor_tensor(out, out, root, ALU.mult))
                settle()

            nc.vector.tensor_scalar(shifted, c["moments"][:, :, 1], LN_EPS, None, ALU.add).then_inc(root_in, 1)
            dve.wait_ge(root_out, 1)
            newton(c["rstd"][:, :])
            if double:
                step(nc.vector.tensor_tensor(shifted, c["rstd"][:, :], c["rstd"][:, :], ALU.mult))
                settle()
                step(nc.vector.tensor_tensor(shifted, shifted, c["moments"][:, :, 1], ALU.mult))
                settle()
                nc.vector.tensor_scalar(shifted, shifted, LN_EPS, None, ALU.add).then_inc(root_in, 1)
                dve.wait_ge(root_out, 2)
                newton(c["rstd2"][:, :])
                step(nc.vector.tensor_tensor(c["rstd2"][:, :], c["rstd2"][:, :], c["rstd"][:, :], ALU.mult))
                settle()


def store_stage(c, out_dram):
    nc = c["nc"]
    with nc.cleanup_on_exit(), ExitStack() as ctx:
        stored = nc.alloc_semaphore("stored")
        block = ctx.enter_context(nc.Block())

        @block.sync
        def _(sp):
            dst = out_dram.rearrange("b (t p) d -> p (b t) d", p=P)
            n, step = 0, max(1, c["tiles"] // 4)
            for t in range(0, c["tiles"], step):
                sp.dma_start(dst[:, t:t + step, :], c["x"][:, t:t + step, :]).then_inc(stored, 16)
                n += 16
            sp.wait_ge(stored, n)


def later(n):
    return not isinstance(n, int)


def normalise(nc, c, xh, n, scale, tiles=TPB):
    for t in range(tiles):
        tile = bass.ds(n * tiles + t, 1)
        ins = nc.vector.tensor_scalar(xh[:, t, :], c["x"][:, tile, :].rearrange("p a d -> p (a d)"),
                                      c["moments"][:, tile, 0], scale[:, tile], ALU.subtract, ALU.mult)
    return ins


MEASURE_STEPS = 2


def updater(c, ctx, tag, tiles=TPB):
    nc = c["nc"]
    sb = lambda name, shape: ctx.enter_context(nc.sbuf_tensor(tag + name, shape, F32))
    fresh, stats, fresh_moments = sb("fresh", [P, tiles, D]), sb("stats", [P, tiles, 6]), sb("fresh_moments", [P, tiles, 2])
    summed, added, measured = (nc.alloc_semaphore(tag + n) for n in ("summed", "added", "measured"))

    def add(n, delta):
        nc.vector.tensor_tensor(fresh[:, :, :], c["x"][:, bass.ds(n * tiles, tiles), :], delta, ALU.add).then_inc(summed, 1)

    def measure(dve, n, step, settle):
        for t in range(tiles):
            ins = nc.vector.bn_stats(stats[:, t, :], fresh[:, t, :])
        step(ins)
        settle()
        nc.vector.tensor_scalar(c["x"][:, bass.ds(n * tiles, tiles), :], fresh[:, :, :], 0.0, None, ALU.add).then_inc(added, 1)
        for t in range(tiles):
            ins = nc.vector.bn_aggr(fresh_moments[:, t, :], stats[:, t, :])
        step(ins)
        settle()
        nc.vector.tensor_scalar(c["moments"][:, bass.ds(n * tiles, tiles), :], fresh_moments[:, :, :], 0.0, None,
                                ALU.add).then_inc(measured, 1)
        dve.wait_ge(measured, n + 1)

    def close(dve, n, step, settle, delta):
        add(n, delta)
        dve.wait_ge(summed, n + 1)
        measure(dve, n, step, settle)

    return fresh, summed, add, measure, close


def attention_bias_stage(c, w):
    nc = c["nc"]
    scale = -1.0 / float(np.sqrt(DH))
    with nc.cleanup_on_exit(), ExitStack() as ctx:
        sb = lambda name, shape, dt=F32: ctx.enter_context(nc.sbuf_tensor("a_" + name, shape, dt))
        sem = lambda n: nc.alloc_semaphore("a_" + n)
        wq, wk, wv, bv = (sb(n, [P, D]) for n in ("wq", "wk", "wv", "bv"))
        bqk = sb("bqk", [P, 2])
        bias = sb("bias", [P, NH, TPB, SEQ])
        xh = sb("xh", [P, TPB, D])
        xt = sb("xt", [P, SEQ])
        qk = sb("qk", [P, 2, SEQ])
        rest = sb("rest", [P, 2, SEQ])
        parts = sb("parts", [P, 3, 2, SEQ], BF16)
        stack = sb("stack", [P, 2, 2, NH, SEQ], BF16)
        va = sb("va", [P, 2, TPB, NH, VW])
        sc = sb("sc", [P, 2, TPB, SEQ])
        nmax = sb("nmax", [P, 2, TPB])
        prob = sb("prob", [P, 2, TPB, SEQ])
        pt = sb("pt", [P, 2, GH, TPB, SEQ])
        ot = sb("ot", [P, NG, SEQ])
        rec = sb("rec", [P, TPB * NH])
        att = sb("att", [P, TPB, D])
        fresh, summed, add, measure, close = updater(c, ctx, "a_")
        ps_s, ps_t, ps_o = c["psum"][:, 0:2], c["psum"][:, 2:4], c["psum"][:, 4:6]
        ps_qk, ps_xt, ps_v = c["psum"][:, 6], c["psum"][:, 7, 0:SEQ], c["psum"][:, 7, SEQ:2 * SEQ]
        ps_f = c["psum"][:, 6:8]

        passed = sem("passed")
        weights, bias_in, preset, bias_neg, bq_ready = (sem(n) for n in ("weights", "bias_in", "preset", "bias_neg", "bq_ready"))
        xh_done, xt_ps, xt_sb, qk_ps, v_ps, qk_sb, v_sb, parts_done, stacked, pool_chain = (
            sem(n) for n in ("xh_done", "xt_ps", "xt_sb", "qk_ps", "v_ps", "qk_sb", "v_sb", "parts_done", "stacked", "pool_chain"))
        s_ready, m_done, e_done, t_done, ce_done, co_done, av_done, o_done, f_ps, f_done, dve_chain = (
            sem(n) for n in ("s_ready", "m_done", "e_done", "t_done", "ce_done", "co_done", "av_done", "o_done", "f_ps", "f_done", "dve_chain"))
        STACK = 16 * 2 * NTERM

        block = ctx.enter_context(nc.Block())

        @block.sync
        def _(sp):
            for dst, src in ((wq, w["wq"]), (wk, w["wk"]), (wv, w["wv"]), (bv, w["bv"]), (bqk, w["bqk"])):
                sp.dma_start(dst[:, :], src).then_inc(weights, 16)
            for g in range(NG):
                sp.dma_start(bias[:, g * GH:(g + 1) * GH], w["bias"][:, g * GH:(g + 1) * GH]).then_inc(bias_in, 16)

            def stack_up(n, u):
                sp.wait_ge(parts_done, n + 1)
                for t in range(NTERM):
                    for side, part in ((0, Q_PART[t]), (1, K_PART[t])):
                        sp.dma_start(stack[t * DH:(t + 1) * DH, u, side], parts[:, part, side, :]).then_inc(stacked, 16)

            sp.wait_ge(preset, 3)
            stack_up(0, 0)
            with sp.Fori(0, c["batches"] // 2) as pair:
                b = pair * 2
                for u in range(2):
                    stack_up(b + (u + 1), (u + 1) % 2)

        @block.gpsimd
        def _(pool):
            nc.gpsimd.memset(stack[:, 0], 0.0).then_inc(preset, 1)
            nc.gpsimd.memset(stack[:, 1], 0.0).then_inc(preset, 1)
            nc.gpsimd.memset(va[:, :, :, :, :], 0.0).then_inc(preset, 1)
            pool.wait_ge(preset, 3)
            nc.gpsimd.memset(va[:, :, :, :, DH:DH + 1], 1.0).then_inc(preset, 1)

            def split(n):
                pool.wait_ge(qk_sb, n + 1)
                if later(n):
                    pool.wait_ge(stacked, STACK * n)
                    pool.wait_ge(s_ready, NH * (n - 1))
                step, settle, steps = chain(pool, pool_chain, n * 1)
                hi, mid, lo = (parts[:, k] for k in range(3))
                nc.gpsimd.tensor_tensor(rest[:, :, :], qk[:, :, :], hi, ALU.subtract)
                step(nc.gpsimd.tensor_tensor(mid, qk[:, :, :], hi, ALU.subtract))
                settle()
                nc.gpsimd.tensor_tensor(lo, rest[:, :, :], mid, ALU.subtract).then_inc(parts_done, 1)

            split(0)
            with pool.Fori(0, c["batches"] // 2) as pair:
                b = pair * 2
                for u in range(2):
                    split(b + (u + 1))

        @block.scalar
        def _(act):
            act.wait_ge(weights, 16 * 5)
            nc.scalar.mul(bqk[:, 0:1], bqk[:, 0:1], scale).then_inc(bq_ready, 1)
            act.wait_ge(bias_in, 16 * NG)
            for g in range(NG):
                nc.scalar.mul(bias[:, g * GH:(g + 1) * GH], bias[:, g * GH:(g + 1) * GH], -1.0).then_inc(bias_neg, 1)
            act.wait_ge(bq_ready, 1)

            def copy_xt(n):
                act.wait_ge(xt_ps, n + 1)
                if later(n):
                    act.wait_ge(v_ps, n)
                nc.scalar.activation(xt[:, :], ps_xt, ACT.Copy).then_inc(xt_sb, 1)

            def copy_qk(n):
                act.wait_ge(qk_ps, n + 1)
                if later(n):
                    act.wait_ge(parts_done, n)
                    act.wait_ge(stacked, STACK * n)
                for dst in (qk, parts[:, 0]):
                    nc.scalar.activation(dst[:, 0, :], ps_qk[:, 0:SEQ], ACT.Identity, bias=bqk[:, 0:1], scale=scale)
                    ins = nc.scalar.activation(dst[:, 1, :], ps_qk[:, SEQ:2 * SEQ], ACT.Identity, bias=bqk[:, 1:2])
                ins.then_inc(qk_sb, 1)

            def exps(n, s, first=False):
                h = n * NH + s
                act.wait_ge(m_done, h + 1)
                if not first:
                    act.wait_ge(t_done, h - 1)
                for qt in range(TPB):
                    ins = nc.scalar.activation(prob[:, s % 2, qt, :], sc[:, s % 2, qt, :], ACT.Exp,
                                               bias=nmax[:, s % 2, qt:qt + 1], scale=-1.0)
                ins.then_inc(e_done, 1)

            def copy_pt(n, s):
                act.wait_ge(t_done, n * NH + s + 1)
                g, j = s // GH, s % GH
                if j == 1:
                    act.wait_ge(av_done, n * NG + g - 1 if g else n * NG)
                nc.scalar.activation(pt[:, g % 2, j], ps_t[:, s % 2].rearrange("p (k q) -> p k q", k=TPB),
                                     ACT.Copy).then_inc(co_done, 1)

            def copy_out(n, g):
                act.wait_ge(av_done, n * NG + g + 1)
                if g == 0:
                    act.wait_ge(f_ps, n)
                nc.scalar.activation(ot[:, g, :], ps_o[:, g % 2, (g // 2) * SEQ:(g // 2 + 1) * SEQ],
                                     ACT.Copy).then_inc(o_done, 1)

            copy_xt(0)
            copy_qk(0)
            exps(0, 0, first=True)
            with act.Fori(0, c["batches"] // 2) as pair:
                b = pair * 2
                for u in range(2):
                    n = b + u
                    for s in range(NH):
                        exps(n, s + 1) if s + 1 < NH else exps(n + 1, 0)
                        if s == 3:
                            copy_xt(n + 1)
                        if s == 5:
                            copy_qk(n + 1)
                        if s % 2:
                            copy_pt(n, s)
                        if s in (6, 10, 14):
                            copy_out(n, (s - 6) // 4)
                    copy_out(n, NG - 1)

        @block.vector
        def _(dve):
            def norm(n):
                if later(n):
                    dve.wait_ge(xt_ps, n)
                normalise(nc, c, xh, n, c["rstd"]).then_inc(xh_done, 1)

            def copy_v(n, u):
                dve.wait_ge(v_ps, n + 1)
                if later(n):
                    dve.wait_ge(av_done, NG * (n - 1))
                nc.vector.tensor_tensor(va[:, u, :, :, 0:DH],
                                        ps_v.rearrange("p (t h d) -> p t h d", t=TPB, h=NH),
                                        bvb, ALU.add).then_inc(v_sb, 1)

            bvb = bv[:, :].rearrange("p (o h d) -> p o h d", o=1, h=NH).broadcast_to([P, TPB, NH, DH])

            def maxima(n, s, first=False):
                h = n * NH + s
                dve.wait_ge(s_ready, h + 1)
                if not first:
                    dve.wait_ge(e_done, h - 1)
                dve.sem_inc(passed, 1)
                for qt in range(TPB):
                    ins = nc.vector.tensor_tensor_reduce(
                        out=sc[:, s % 2, qt, :], in0=ps_s[:, s % 2, qt * SEQ:(qt + 1) * SEQ], in1=bias[:, s, qt, :],
                        scale=1.0, scalar=BIG, op0=ALU.add, op1=ALU.min, accum_out=nmax[:, s % 2, qt:qt + 1])
                ins.then_inc(m_done, 1)

            def copy_pt(n, s):
                dve.wait_ge(t_done, n * NH + s + 1)
                g, j = s // GH, s % GH
                if j == 0:
                    dve.wait_ge(av_done, n * NG + g - 1 if g else n * NG)
                nc.vector.tensor_copy(pt[:, g % 2, j], ps_t[:, s % 2].rearrange("p (k q) -> p k q", k=TPB)
                                      ).then_inc(ce_done, 1)

            def finish(n):
                step, settle, steps = chain(dve, dve_chain, n * 3)
                outs = ps_f.rearrange("p t (h v) -> p (t h) v", v=VW)
                dve.wait_ge(f_ps, n + 1)
                step(nc.vector.reciprocal(rec[:, :], outs[:, :, DH]))
                settle()
                nc.vector.tensor_tensor(att[:, :, :].rearrange("p t (h d) -> p (t h) d", d=DH), outs[:, :, 0:DH],
                                                rec[:, :].rearrange("p (a o) -> p a o", o=1).broadcast_to([P, TPB * NH, DH]), ALU.mult).then_inc(f_done, 1)
                dve.wait_ge(f_done, n + 1)
                close(dve, n, step, settle, att[:, :, :])
                assert steps() == 3

            dve.wait_ge(weights, 16 * 5)
            norm(0)
            dve.wait_ge(preset, 4)
            copy_v(0, 0)
            dve.wait_ge(bias_neg, NG)
            maxima(0, 0, first=True)
            with dve.Fori(0, c["batches"] // 2) as pair:
                b = pair * 2
                for u in range(2):
                    n = b + u
                    for s in range(NH):
                        maxima(n, s + 1) if s + 1 < NH else maxima(n + 1, 0)
                        if s == 1:
                            norm(n + 1)
                        if s == 6:
                            copy_v(n + 1, (u + 1) % 2)
                        if s % 2 == 0:
                            copy_pt(n, s)
                    finish(n)

        @block.tensor
        def _(pe):
            def transpose_x(n):
                pe.wait_ge(xh_done, n + 1)
                if later(n):
                    pe.wait_ge(xt_sb, n)
                    pe.wait_ge(f_done, n - 1)
                for t in range(TPB):
                    ins = nc.tensor.transpose(ps_xt[:, t * P:(t + 1) * P], xh[:, t, :], c["ident"][:, :])
                ins.then_inc(xt_ps, 1)

            def project(n):
                pe.wait_ge(xt_sb, n + 1)
                if later(n):
                    pe.wait_ge(qk_sb, n)
                    pe.wait_ge(v_sb, n)
                nc.tensor.matmul(ps_qk[:, 0:SEQ], wq[:, :], xt[:, :], start=True, stop=True)
                nc.tensor.matmul(ps_qk[:, SEQ:2 * SEQ], wk[:, :], xt[:, :], start=True, stop=True).then_inc(qk_ps, 1)
                for t in range(TPB):
                    ins = nc.tensor.matmul(ps_v[:, t * P:(t + 1) * P], xt[:, t * P:(t + 1) * P], wv[:, :], start=True, stop=True)
                ins.then_inc(v_ps, 1)

            def scores(n, u, s, first=False):
                h = n * NH + s
                if s == 0:
                    pe.wait_ge(stacked, STACK * (n + 1))
                if not first:
                    pe.wait_ge(m_done, h - 1)
                for qt in range(TPB):
                    ins = nc.tensor.matmul(ps_s[:, s % 2, qt * SEQ:(qt + 1) * SEQ], stack[:, u, 0, s, qt * P:(qt + 1) * P],
                                           stack[:, u, 1, s, :], start=True, stop=True)
                ins.then_inc(s_ready, 1)

            def transpose_p(n, s):
                pe.wait_ge(e_done, n * NH + s + 1)
                if s >= 2:
                    pe.wait_ge(co_done if s % 2 else ce_done, n * (NH // 2) + s // 2)
                for qt in range(TPB):
                    for kt in range(TPB):
                        ins = nc.tensor.transpose(ps_t[:, s % 2, kt * SEQ + qt * P:kt * SEQ + (qt + 1) * P],
                                                  prob[:, s % 2, qt, kt * P:(kt + 1) * P], c["ident"][:, :])
                ins.then_inc(t_done, 1)

            def values(n, u, g):
                pe.wait_ge(ce_done, n * (NH // 2) + 2 * (g + 1))
                pe.wait_ge(co_done, n * (NH // 2) + 2 * (g + 1))
                if g == 0:
                    pe.wait_ge(v_sb, n + 1)
                if g >= 2:
                    pe.wait_ge(o_done, n * NG + g - 1)
                for kt in range(TPB):
                    for j in range(GH):
                        ins = nc.tensor.matmul(ps_o[j * VW:(j + 1) * VW, g % 2, (g // 2) * SEQ:(g // 2 + 1) * SEQ],
                                               va[:, u, kt, g * GH + j, :], pt[:, g % 2, j, kt, :],
                                               start=kt == 0, stop=kt == TPB - 1, tile_position=(0, j * VW))
                ins.then_inc(av_done, 1)

            def transpose_out(n):
                pe.wait_ge(o_done, NG * (n + 1))
                pe.wait_ge(xt_sb, n + 2)
                pe.wait_ge(qk_sb, n + 2)
                pe.wait_ge(v_sb, n + 2)
                for t in range(TPB):
                    for g in range(NG):
                        ins = nc.tensor.transpose(ps_f[:, t, g * P:(g + 1) * P], ot[:, g, t * P:(t + 1) * P], c["ident"][:, :])
                ins.then_inc(f_ps, 1)

            pe.wait_ge(weights, 16 * 5)
            transpose_x(0)
            project(0)
            pe.wait_ge(preset, 4)
            scores(0, 0, 0, first=True)
            scores(0, 0, 1, first=True)
            with pe.Fori(0, c["batches"] // 2) as pair:
                b = pair * 2
                for u in range(2):
                    n = b + u
                    for s in range(NH):
                        scores(n, u, s + 2) if s + 2 < NH else scores(n + 1, (u + 1) % 2, s + 2 - NH)
                        transpose_p(n, s)
                        if s == 2:
                            transpose_x(n + 1)
                        if s == 4:
                            project(n + 1)
                        if s in (5, 9, 13):
                            values(n, u, (s - 5) // 4)
                    values(n, u, NG - 1)
                    transpose_out(n)


CH = 64
NC = NH * CH // P
NPIECE = 12


def causal_attention_stage(c, w):
    nc = c["nc"]
    scale = -1.0 / float(np.sqrt(CH))
    with nc.cleanup_on_exit(), ExitStack() as ctx:
        sb = lambda name, shape, dt=F32: ctx.enter_context(nc.sbuf_tensor("c_" + name, shape, dt))
        sem = lambda n: nc.alloc_semaphore("c_" + n)
        wq, wk, wv = (sb(n, [P, NH * CH]) for n in ("wq", "wk", "wv"))
        wo = sb("wo", [P, NC, D])
        mask = sb("mask", [P, SEQ])
        xh, xt = sb("xh", [P, TPB, D]), sb("xt", [P, SEQ])
        q = sb("q", [P, 2, 2, NC, SEQ])
        k = sb("k", [P, 2, NC, SEQ])
        v = sb("v", [P, 2, TPB, NH * CH])
        sc, prob = sb("sc", [P, 2, P + SEQ]), sb("prob", [P, 2, P + SEQ])
        nmax, total, share = (sb(n, [P, 2, TPB]) for n in ("nmax", "total", "share"))
        pt = sb("pt", [P, 4, P + SEQ])
        ot = sb("ot", [P, NC, SEQ])
        fresh, summed, add, measure, close = updater(c, ctx, "c_")
        ps_s, ps_t, ps_o, ring = c["psum"][:, 0:2], c["psum"][:, 2:4], c["psum"][:, 4:6], c["psum"][:, 6:8]
        ps_xt, ps_y = ring[:, 0, 0:SEQ], ring[:, 1, 0:SEQ]
        piece_bank = lambda i: ring[:, (i + 1) % 2]
        SPAN = ((0, slice(0, P)), (1, slice(P, P + SEQ)))

        weights, preset, dve_chain = (sem(n) for n in ("weights", "preset", "dve_chain"))
        xh_done, xt_ps, xt_sb, piece_ps, act_pieces, dve_pieces = (
            sem(n) for n in ("xh_done", "xt_ps", "xt_sb", "piece_ps", "act_pieces", "dve_pieces"))
        passed, s_ready, m_done, e_done, inverted, n_done, t_done, ce_done, co_done, av_done, o_done, y_ps = (
            sem(n) for n in ("passed", "s_ready", "m_done", "e_done", "inverted", "n_done", "t_done", "ce_done", "co_done",
                             "av_done", "o_done", "y_ps"))
        n_weights = 16 * 5
        HALF = NPIECE // 2
        block = ctx.enter_context(nc.Block())

        @block.sync
        def _(sp):
            for dst, src in ((wq, "wq"), (wk, "wk"), (wv, "wv"), (mask, "mask")):
                sp.dma_start(dst[:, :], w[src]).then_inc(weights, 16)
            sp.dma_start(wo[:, :, :], w["wo"]).then_inc(weights, 16)

        @block.gpsimd
        def _(pool):
            nc.gpsimd.memset(q[:, :, :, :, :], 0.0).then_inc(preset, 1)

        def copy_piece(copy, n, u, i):
            bank = piece_bank(i)
            if i < 8:
                two = slice(i // 2 * 2, i // 2 * 2 + 2)
                if i % 2:
                    return copy(k[:, u, two, :].rearrange("p c t -> p (c t)"), bank)
                for j in range(2):
                    rows = slice(j * CH, (j + 1) * CH)
                    ins = nc.scalar.mul(q[rows, u, j, two, :].rearrange("p c t -> p (c t)"), bank[rows], scale)
                return ins
            t, half = divmod(i - 8, 2)
            return copy(v[:, u, t, half * 512:(half + 1) * 512], bank)

        @block.scalar
        def _(act):
            def copy_xt(n):
                act.wait_ge(xt_ps, n + 1)
                if later(n):
                    act.wait_ge(piece_ps, NPIECE * n)
                nc.scalar.activation(xt[:, :], ps_xt, ACT.Copy).then_inc(xt_sb, 1)

            def piece(n, u, i):
                act.wait_ge(piece_ps, NPIECE * n + i + 1)
                if i == 0 and later(n):
                    act.wait_ge(y_ps, n - 1)
                copy_piece(lambda out, in_: nc.scalar.activation(out, in_, ACT.Copy), n, u, i).then_inc(act_pieces, 1)

            def exps(n, s, first=False):
                h = n * NH + s
                act.wait_ge(m_done, h + 1)
                if not first:
                    act.wait_ge(t_done, h - 1)
                for t, span in SPAN:
                    ins = nc.scalar.activation(prob[:, s % 2, span], sc[:, s % 2, span], ACT.Exp, bias=nmax[:, s % 2, t:t + 1],
                                               scale=-1.0, accum_out=total[:, s % 2, t:t + 1])
                ins.then_inc(e_done, 1)

            def copy_pt(n, s):
                act.wait_ge(t_done, n * NH + s + 1)
                ch = s // 2
                act.wait_ge(av_done, n * NC + ch - 1 if ch else n * NC)
                nc.scalar.activation(pt[:, s % 4, :], ps_t[:, s % 2, 0:P + SEQ], ACT.Copy).then_inc(co_done, 1)

            def copy_out(n, ch):
                act.wait_ge(av_done, n * NC + ch + 1)
                if ch == 0:
                    act.wait_ge(y_ps, n)
                nc.scalar.activation(ot[:, ch, :], ps_o[:, ch % 2, 0:SEQ], ACT.Copy).then_inc(o_done, 1)

            act.wait_ge(preset, 1)
            copy_xt(0)
            for i in range(0, NPIECE, 2):
                piece(0, 0, i)
            exps(0, 0, first=True)
            with act.Fori(0, c["batches"] // 2) as pair:
                for u in range(2):
                    n = pair * 2 + u
                    for s in range(NH):
                        exps(n, s + 1) if s + 1 < NH else exps(n + 1, 0)
                        if s == 1:
                            copy_xt(n + 1)
                        if s >= 2 and s % 2 == 0 and s - 2 < NPIECE:
                            piece(n + 1, (u + 1) % 2, s - 2)
                        if s % 2 == 0 and s:
                            copy_pt(n, s - 1)
                        if s % 2 == 0 and s >= 4:
                            copy_out(n, s // 2 - 2)
                    copy_pt(n, NH - 1)
                    copy_out(n, NC - 2)
                    copy_out(n, NC - 1)

        @block.vector
        def _(dve):
            def norm(n):
                if later(n):
                    dve.wait_ge(xt_ps, n)
                normalise(nc, c, xh, n, c["rstd"]).then_inc(xh_done, 1)

            def piece(n, u, i):
                dve.wait_ge(piece_ps, NPIECE * n + i + 1)
                if i == 1 and later(n):
                    dve.wait_ge(y_ps, n - 1)
                copy_piece(nc.vector.tensor_copy, n, u, i).then_inc(dve_pieces, 1)

            def maxima(n, s, first=False):
                h = n * NH + s
                dve.wait_ge(s_ready, h + 1)
                if not first:
                    dve.wait_ge(e_done, h - 1)
                dve.sem_inc(passed, 1)
                for t, span in SPAN:
                    in1 = mask[:, P:SEQ] if t == 0 else mask[:, :]
                    ins = nc.vector.tensor_tensor_reduce(
                        out=sc[:, s % 2, span], in0=ps_s[:, s % 2, span], in1=in1, scale=1.0, scalar=BIG, op0=ALU.add,
                        op1=ALU.min, accum_out=nmax[:, s % 2, t:t + 1])
                ins.then_inc(m_done, 1)

            def divide(n, s):
                h = n * NH + s
                dve.wait_ge(e_done, h + 1)
                nc.vector.reciprocal(share[:, s % 2, :], total[:, s % 2, :]).then_inc(inverted, 1)
                dve.wait_ge(inverted, h + 1)
                for t, span in SPAN:
                    ins = nc.vector.tensor_scalar(prob[:, s % 2, span], prob[:, s % 2, span], share[:, s % 2, t:t + 1], None, ALU.mult)
                ins.then_inc(n_done, 1)

            def copy_pt(n, s):
                dve.wait_ge(t_done, n * NH + s + 1)
                ch = s // 2
                dve.wait_ge(av_done, n * NC + ch - 1 if ch else n * NC)
                nc.vector.tensor_copy(pt[:, s % 4, :], ps_t[:, s % 2, 0:P + SEQ]).then_inc(ce_done, 1)

            def finish(n):
                step, settle, steps = chain(dve, dve_chain, n * 2)
                dve.wait_ge(y_ps, n + 1)
                close(dve, n, step, settle, ps_y.rearrange("p (t d) -> p t d", t=TPB))
                assert steps() == 2

            norm(0)
            for i in range(1, NPIECE, 2):
                piece(0, 0, i)
            dve.wait_ge(weights, n_weights)
            maxima(0, 0, first=True)
            with dve.Fori(0, c["batches"] // 2) as pair:
                for u in range(2):
                    n = pair * 2 + u
                    for s in range(NH):
                        maxima(n, s + 1) if s + 1 < NH else maxima(n + 1, 0)
                        divide(n, s)
                        if s == 0:
                            norm(n + 1)
                        if s >= 3 and s % 2 and s - 2 < NPIECE:
                            piece(n + 1, (u + 1) % 2, s - 2)
                        if s % 2:
                            copy_pt(n, s - 1)
                    finish(n)

        @block.tensor
        def _(pe):
            def transpose_x(n):
                pe.wait_ge(xh_done, n + 1)
                if later(n):
                    pe.wait_ge(dve_pieces, HALF * n)
                for t in range(TPB):
                    ins = nc.tensor.transpose(ps_xt[:, t * P:(t + 1) * P], xh[:, t, :], c["ident"][:, :])
                ins.then_inc(xt_ps, 1)

            def piece(n, i):
                if i == 0:
                    pe.wait_ge(xt_sb, n + 1)
                    if later(n):
                        pe.wait_ge(summed, n - 1)
                elif i >= 2:
                    pe.wait_ge(dve_pieces if i % 2 else act_pieces, HALF * n + i // 2)
                bank = piece_bank(i)
                if i < 8:
                    for j in range(2):
                        at = (i // 2 * 2 + j) * P
                        ins = nc.tensor.matmul(bank[:, j * SEQ:(j + 1) * SEQ], (wk if i % 2 else wq)[:, at:at + P], xt[:, :],
                                               start=True, stop=True)
                else:
                    t, half = divmod(i - 8, 2)
                    ins = nc.tensor.matmul(bank, xt[:, t * P:(t + 1) * P], wv[:, half * 512:(half + 1) * 512], start=True, stop=True)
                ins.then_inc(piece_ps, 1)

            def scores(n, u, s, first=False):
                h = n * NH + s
                if s == 0:
                    pe.wait_ge(act_pieces, HALF * (n + 1))
                    pe.wait_ge(dve_pieces, HALF * (n + 1))
                if not first:
                    pe.wait_ge(m_done, h - 1)
                for t, span in SPAN:
                    ins = nc.tensor.matmul(ps_s[:, s % 2, span], q[:, u, s % 2, s // 2, t * P:(t + 1) * P],
                                           k[:, u, s // 2, 0:(t + 1) * P], start=True, stop=True)
                ins.then_inc(s_ready, 1)

            def transpose_p(n, s):
                pe.wait_ge(n_done, n * NH + s + 1)
                if s >= 2:
                    pe.wait_ge(co_done if s % 2 else ce_done, n * (NH // 2) + s // 2)
                for i in range(3):
                    ins = nc.tensor.transpose(ps_t[:, s % 2, i * P:(i + 1) * P], prob[:, s % 2, i * P:(i + 1) * P], c["ident"][:, :])
                ins.then_inc(t_done, 1)

            def values(n, u, ch):
                pe.wait_ge(ce_done, n * (NH // 2) + ch + 1)
                pe.wait_ge(co_done, n * (NH // 2) + ch + 1)
                if ch >= 2:
                    pe.wait_ge(o_done, n * NC + ch - 1)
                for t in range(TPB):
                    for j in range(2):
                        head = 2 * ch + j
                        queries = slice(0, SEQ) if t == 0 else slice(P, SEQ)
                        weights_t = pt[:, head % 4, 0:SEQ] if t == 0 else pt[:, head % 4, SEQ:SEQ + P]
                        ins = nc.tensor.matmul(ps_o[j * CH:(j + 1) * CH, ch % 2, queries], v[:, u, t, head * CH:(head + 1) * CH],
                                               weights_t, start=t == 0, stop=t == TPB - 1, tile_position=(0, j * CH))
                ins.then_inc(av_done, 1)

            def project_out(n):
                pe.wait_ge(o_done, NC * (n + 1))
                pe.wait_ge(act_pieces, HALF * (n + 2))
                for t in range(TPB):
                    for ch in range(NC):
                        ins = nc.tensor.matmul(ps_y[:, t * P:(t + 1) * P], ot[:, ch, t * P:(t + 1) * P], wo[:, ch, :],
                                               start=ch == 0, stop=ch == NC - 1)
                ins.then_inc(y_ps, 1)

            pe.wait_ge(weights, n_weights)
            transpose_x(0)
            for i in range(NPIECE):
                piece(0, i)
            scores(0, 0, 0, first=True)
            scores(0, 0, 1, first=True)
            with pe.Fori(0, c["batches"] // 2) as pair:
                for u in range(2):
                    n = pair * 2 + u
                    for s in range(NH):
                        scores(n, u, s + 2) if s + 2 < NH else scores(n + 1, (u + 1) % 2, s + 2 - NH)
                        transpose_p(n, s)
                        if s == 0:
                            transpose_x(n + 1)
                        if s >= 1 and s - 1 < NPIECE:
                            piece(n + 1, s - 1)
                        if s >= 3 and s % 2:
                            values(n, u, (s - 3) // 2)
                    values(n, u, NC - 1)
                    project_out(n)


def gated_expert_stage(c, w, tag):
    nc = c["nc"]
    blocks = c["tiles"] // BT
    H = w["shared_out"].shape[0]
    HALF = NE // 2
    with nc.cleanup_on_exit(), ExitStack() as ctx:
        sb = lambda name, shape, dt=F32: ctx.enter_context(nc.sbuf_tensor(tag + name, shape, dt))
        sem = lambda n: nc.alloc_semaphore(tag + n)
        w_in = sb("w_in", [P, 2, 2, H])
        w_so, w2, wg = sb("w_so", [P, D]), sb("w2", [P, NE, D]), sb("wg", [P, NE])
        gbias, order = sb("gbias", [P, BT, NE]), sb("order", [P, BT, NE])
        xh, xt = sb("xh", [P, BT, D]), sb("xt", [P, BTOK])
        gate = sb("gate", [P, 2, BTOK])
        hid = sb("hid", [P, 2, 2, BTOK])
        logit, prob, left, cand, pick1, pick2 = (sb(n, [P, BT, NE]) for n in ("logit", "prob", "left", "cand", "pick1", "pick2"))
        weight = sb("weight", [P, 2, BT, NE])
        peak, total = sb("peak", [P, BT]), sb("total", [P, BT])
        fresh, summed, add, measure, close = updater(c, ctx, tag, BT)
        ps_xt, ps_ab, ps_r, ps_so = c["psum"][:, 0], c["psum"][:, 1:3], c["psum"][:, 3:7], c["psum"][:, 7]
        ps_logit = ps_xt[:, 0:BT * NE].rearrange("p (t e) -> p t e", e=NE)

        weights, dve_chain, gate_chain = (sem(n) for n in ("weights", "dve_chain", "gate_chain"))
        xh_done, xt_ps, xt_sb, logit_ps, logit_sb, exp_in, exp_out, ab_ps, gate_sb, hid_done, so_ps, r_ps, r_used, weighed = (
            sem(n) for n in ("xh_done", "xt_ps", "xt_sb", "logit_ps", "logit_sb", "exp_in", "exp_out", "ab_ps", "gate_sb",
                             "hid_done", "so_ps", "r_ps", "r_used", "weighed"))
        n_weights = 16 * 6
        GATE = 16
        block = ctx.enter_context(nc.Block())

        @block.sync
        def _(sp):
            for dst, src in ((w_in, "in"), (w_so, "shared_out"), (w2, "w2"), (wg, "gate"), (gbias, "gbias"), (order, "order")):
                sp.dma_start(dst[tuple(slice(None) for _ in dst.shape)], w[src]).then_inc(weights, 16)

        @block.tensor
        def _(pe):
            def transpose_x(n):
                pe.wait_ge(xh_done, n + 1)
                if later(n):
                    pe.wait_ge(logit_sb, n)
                for t in range(BT):
                    ins = nc.tensor.transpose(ps_xt[:, t * P:(t + 1) * P], xh[:, t, :], c["ident"][:, :])
                ins.then_inc(xt_ps, 1)

            def logits(n):
                pe.wait_ge(xt_sb, n + 1)
                for t in range(BT):
                    ins = nc.tensor.matmul(ps_logit[:, t, :], xt[:, t * P:(t + 1) * P], wg[:, :], start=True, stop=True)
                ins.then_inc(logit_ps, 1)

            def hidden(n, k):
                if k or later(n):
                    pe.wait_ge(hid_done, n * 2 + k)
                for ab in range(2):
                    ins = nc.tensor.matmul(ps_ab[:, ab], w_in[:, k, ab, :], xt[:, :], start=True, stop=True)
                ins.then_inc(ab_ps, 1)

            def shared(n, u):
                pe.wait_ge(hid_done, n * 2 + 1)
                pe.wait_ge(summed, n)
                for t in range(BT):
                    ins = nc.tensor.matmul(ps_so[:, t * P:(t + 1) * P], hid[:, u, 0, t * P:(t + 1) * P], w_so[:, :], start=True, stop=True)
                ins.then_inc(so_ps, 1)

            def routed(n, u, k):
                if k == 0:
                    pe.wait_ge(hid_done, n * 2 + 2)
                if k >= 2:
                    pe.wait_ge(r_used, n * 4 + k - 1)
                else:
                    pe.wait_ge(r_used, n * 4)
                for t in range(2):
                    tile, half = (k // 2) * 2 + t, k % 2
                    ins = nc.tensor.matmul(ps_r[:, (k % 2) * 2 + t], hid[:, u, 1, tile * P:(tile + 1) * P],
                                           w2[:, half * HALF:(half + 1) * HALF, :].rearrange("p e d -> p (e d)"), start=True, stop=True)
                ins.then_inc(r_ps, 1)

            pe.wait_ge(weights, n_weights)
            transpose_x(0)
            logits(0)
            hidden(0, 0)
            hidden(0, 1)
            with pe.Fori(0, blocks // 2) as pair:
                for u in range(2):
                    n = pair * 2 + u
                    shared(n, u)
                    routed(n, u, 0)
                    transpose_x(n + 1)
                    routed(n, u, 1)
                    logits(n + 1)
                    hidden(n + 1, 0)
                    routed(n, u, 2)
                    hidden(n + 1, 1)
                    routed(n, u, 3)

        @block.scalar
        def _(act):
            def copy_xt(n):
                act.wait_ge(xt_ps, n + 1)
                if later(n):
                    act.wait_ge(ab_ps, n * 2)
                nc.scalar.activation(xt[:, :], ps_xt, ACT.Copy).then_inc(xt_sb, 1)

            def silu(n, k):
                act.wait_ge(ab_ps, n * 2 + k + 1)
                if later(n):
                    act.wait_ge(hid_done, n * 2 + k - 1)
                nc.scalar.activation(gate[:, k, :], ps_ab[:, 0], ACT.Silu).then_inc(gate_sb, 1)

            def exp(n):
                act.wait_ge(exp_in, n + 1)
                nc.scalar.activation(prob[:, :, :], logit[:, :, :], ACT.Exp).then_inc(exp_out, 1)

            copy_xt(0)
            silu(0, 0)
            silu(0, 1)
            exp(0)
            with act.Fori(0, blocks // 2) as pair:
                for u in range(2):
                    n = pair * 2 + u
                    copy_xt(n + 1)
                    silu(n + 1, 0)
                    silu(n + 1, 1)
                    exp(n + 1)

        @block.vector
        def _(dve):
            wide = lambda t: t.rearrange("p (a o) -> p a o", o=1).broadcast_to([P, BT, NE])

            def norm(n):
                if later(n):
                    dve.wait_ge(xt_ps, n)
                normalise(nc, c, xh, n, c["rstd"], BT).then_inc(xh_done, 1)

            def multiply(n, u, k):
                dve.wait_ge(gate_sb, n * 2 + k + 1)
                if later(n):
                    dve.wait_ge(r_ps if k else so_ps, n * 4 - 4 if k else n - 1)
                nc.vector.tensor_tensor(hid[:, u, k, :], gate[:, k, :], ps_ab[:, 1], ALU.mult).then_inc(hid_done, 1)

            def gate_front(n, g_step, g_settle):
                dve.wait_ge(logit_ps, n + 1)
                nc.vector.tensor_tensor(logit[:, :, :], ps_logit, gbias[:, :, :], ALU.add).then_inc(logit_sb, 1)
                dve.wait_ge(logit_sb, n + 1)
                g_step(nc.vector.tensor_reduce(peak[:, :], logit[:, :, :], AX.X, ALU.max))
                g_settle()
                nc.vector.tensor_tensor(logit[:, :, :], logit[:, :, :], wide(peak[:, :]), ALU.subtract).then_inc(exp_in, 1)

            def gate_back(n, u, g_step, g_settle, g_steps):
                dve.wait_ge(exp_out, n + 1)
                g_step(nc.vector.tensor_reduce(total[:, :], prob[:, :, :], AX.X, ALU.add))
                g_settle()
                g_step(nc.vector.reciprocal(total[:, :], total[:, :]))
                g_settle()
                g_step(nc.vector.tensor_tensor(prob[:, :, :], prob[:, :, :], wide(total[:, :]), ALU.mult))
                g_settle()
                g_step(pick_first_max(nc, g_step, g_settle, pick1[:, :, :], prob[:, :, :], order[:, :, :], peak[:, :], cand[:, :, :]))
                g_settle()
                g_step(nc.vector.scalar_tensor_tensor(left[:, :, :], pick1[:, :, :], -2.0, prob[:, :, :], ALU.mult, ALU.add))
                g_settle()
                g_step(pick_first_max(nc, g_step, g_settle, pick2[:, :, :], left[:, :, :], order[:, :, :], peak[:, :], cand[:, :, :]))
                g_settle()
                g_step(nc.vector.tensor_tensor(pick1[:, :, :], pick1[:, :, :], pick2[:, :, :], ALU.add))
                g_settle()
                nc.vector.tensor_tensor(weight[:, u, :, :], prob[:, :, :], pick1[:, :, :], ALU.mult).then_inc(weighed, 1)
                assert g_steps() == GATE

            def add_shared(n):
                dve.wait_ge(so_ps, n + 1)
                add(n, ps_so.rearrange("p (t d) -> p t d", t=BT))
                dve.wait_ge(summed, n + 1)
                dve.wait_ge(weighed, n + 1)

            def add_routed(n, u, k, step, settle):
                dve.wait_ge(r_ps, n * 4 + k + 1)
                for e in range(HALF):
                    for t in range(2):
                        tile, expert = (k // 2) * 2 + t, (k % 2) * HALF + e
                        acc = fresh[:, tile, :]
                        ins = nc.vector.scalar_tensor_tensor(acc, ps_r[:, (k % 2) * 2 + t, e * D:(e + 1) * D],
                                                             weight[:, u, tile, expert:expert + 1], acc, ALU.mult, ALU.add)
                        if e == HALF - 1 and t == 1:
                            ins.then_inc(r_used, 1)
                        else:
                            step(ins)
                            settle(but=1)
                dve.wait_ge(r_used, n * 4 + k + 1)

            dve.wait_ge(weights, n_weights)
            g_step, g_settle, g_steps = chain(dve, gate_chain, 0)
            norm(0)
            gate_front(0, g_step, g_settle)
            multiply(0, 0, 0)
            multiply(0, 0, 1)
            gate_back(0, 0, g_step, g_settle, g_steps)
            with dve.Fori(0, blocks // 2) as pair:
                for u in range(2):
                    n = pair * 2 + u
                    step, settle, steps = chain(dve, dve_chain, n * (4 * 7 + MEASURE_STEPS))
                    g_step, g_settle, g_steps = chain(dve, gate_chain, (n + 1) * GATE)
                    norm(n + 1)
                    add_shared(n)
                    add_routed(n, u, 0, step, settle)
                    add_routed(n, u, 1, step, settle)
                    gate_front(n + 1, g_step, g_settle)
                    multiply(n + 1, (u + 1) % 2, 0)
                    add_routed(n, u, 2, step, settle)
                    multiply(n + 1, (u + 1) % 2, 1)
                    add_routed(n, u, 3, step, settle)
                    measure(dve, n, step, settle)
                    gate_back(n + 1, (u + 1) % 2, g_step, g_settle, g_steps)
                    assert steps() == 4 * 7 + MEASURE_STEPS


BT = 4
BTOK = BT * P
NE = 8
EH = 32
NHALF = NE * EH // P


def pick_first_max(nc, step, settle, picked, values, order, peak, cand):
    wide = lambda t: t.rearrange("p (a o) -> p a o", o=1).broadcast_to([P, BT, NE])
    step(nc.vector.tensor_reduce(peak, values, AX.X, ALU.max))
    settle()
    step(nc.vector.tensor_tensor(cand, values, wide(peak), ALU.is_equal))
    settle()
    step(nc.vector.tensor_tensor(cand, cand, order, ALU.mult))
    settle()
    step(nc.vector.tensor_reduce(peak, cand, AX.X, ALU.max))
    settle()
    return nc.vector.tensor_tensor(picked, cand, wide(peak), ALU.is_equal)


def expert_stage(c, w, tag):
    nc = c["nc"]
    blocks = c["tiles"] // BT
    with nc.cleanup_on_exit(), ExitStack() as ctx:
        sb = lambda name, shape, dt=F32: ctx.enter_context(nc.sbuf_tensor(tag + name, shape, dt))
        sem = lambda n: nc.alloc_semaphore(tag + n)
        w1, w1s, b1 = sb("w1", [P, NE, EH]), sb("w1s", [P, NE, EH]), sb("b1", [P, NHALF])
        lns, lnb, wg = (sb(n, [P, NE]) for n in ("lns", "lnb", "wg"))
        own = sb("own", [P, NHALF, NE])
        foldsum = sb("foldsum", [P, NHALF])
        folded = sb("folded", [P, NHALF, NE])
        w2, b2 = sb("w2", [P, NHALF, D]), sb("b2", [NE, D])
        spread32, spread = sb("spread32", [NE, NHALF, P]), sb("spread", [NE, NHALF, P], BF16)
        order = sb("order", [P, BT, NE])
        xh, xt = sb("xh", [P, BT, D]), sb("xt", [P, BTOK])
        hid, masked = sb("hid", [P, 2, NHALF, BTOK]), sb("masked", [P, NHALF, BTOK])
        peak, cand, picked = sb("peak", [P, BT]), sb("cand", [P, BT, NE]), sb("picked", [P, BT, NE])
        pick32, pick16 = sb("pick32", [NE, 2, BTOK]), sb("pick16", [NE, 2, BTOK], BF16)
        fresh, summed, add, measure, close = updater(c, ctx, tag, BT)
        ps_xt, ps_h, ps_small, ps_pick, ps_mask, ps_y = (
            c["psum"][:, 0], c["psum"][:, 1:3], c["psum"][:, 3], c["psum"][:, 4], c["psum"][:, 5:7], c["psum"][:, 7])
        ps_logit = ps_small[:, 0:BT * NE].rearrange("p (t e) -> p t e", e=NE)
        ps_fold = ps_small[:, 64:64 + NHALF * NE].rearrange("p (t e) -> p t e", e=NE)

        weights, fold_ps, ready, w_chain, dve_chain = (sem(n) for n in ("weights", "fold_ps", "ready", "w_chain", "dve_chain"))
        xh_done, xt_ps, xt_sb, h_ps, logit_ps, h_sb, picked_done, pick_ps, pick_sb, mask_ps, masked_done, y_ps = (
            sem(n) for n in ("xh_done", "xt_ps", "xt_sb", "h_ps", "logit_ps", "h_sb", "picked_done", "pick_ps", "pick_sb",
                             "mask_ps", "masked_done", "y_ps"))
        n_weights = 16 * 10
        block = ctx.enter_context(nc.Block())

        @block.sync
        def _(sp):
            for dst, src in ((w1, "w1"), (b1, "b1"), (lns, "lns"), (lnb, "lnb"), (wg, "wg"), (own, "own"), (w2, "w2"),
                             (b2, "b2"), (spread32, "spread"), (order, "order")):
                sp.dma_start(dst[tuple(slice(None) for _ in dst.shape)], w[src]).then_inc(weights, 16)

        @block.tensor
        def _(pe):
            pe.wait_ge(weights, n_weights)
            for k in range(NHALF):
                ins = nc.tensor.matmul(ps_fold[:, k, :], w1[:, k * NE // NHALF:(k + 1) * NE // NHALF, :].rearrange("p e h -> p (e h)"),
                                       lnb[:, :], start=True, stop=True)
            ins.then_inc(fold_ps, 1)
            pe.wait_ge(ready, 1)

            def front(n):
                pe.wait_ge(xh_done, n + 1)
                if later(n):
                    pe.wait_ge(xt_sb, n)
                for t in range(BT):
                    ins = nc.tensor.transpose(ps_xt[:, t * P:(t + 1) * P], xh[:, t, :], c["ident"][:, :])
                ins.then_inc(xt_ps, 1)
                pe.wait_ge(xt_sb, n + 1)
                if later(n):
                    pe.wait_ge(h_sb, n)
                    pe.wait_ge(picked_done, n)
                for t in range(BT):
                    ins = nc.tensor.matmul(ps_logit[:, t, :], xt[:, t * P:(t + 1) * P], wg[:, :], start=True, stop=True)
                ins.then_inc(logit_ps, 1)
                for k in range(NHALF):
                    ins = nc.tensor.matmul(ps_h[:, k], w1s[:, k * NE // NHALF:(k + 1) * NE // NHALF, :].rearrange("p e h -> p (e h)"),
                                           xt[:, :], start=True, stop=True)
                ins.then_inc(h_ps, 1)

            def pick(n):
                pe.wait_ge(picked_done, n + 1)
                if later(n):
                    pe.wait_ge(pick_sb, n)
                for t in range(BT):
                    ins = nc.tensor.transpose(ps_pick[0:NE, t * P:(t + 1) * P], picked[:, t, :], c["ident"][:, :])
                ins.then_inc(pick_ps, 1)

            def back(n, u):
                pe.wait_ge(masked_done, n + 1)
                pe.wait_ge(summed, n)
                for t in range(BT):
                    out = ps_y[:, t * P:(t + 1) * P]
                    for k in range(NHALF):
                        nc.tensor.matmul(out, masked[:, k, t * P:(t + 1) * P], w2[:, k, :], start=k == 0, stop=False)
                    ins = nc.tensor.matmul(out, pick32[:, u, t * P:(t + 1) * P], b2[:, :], start=False, stop=True)
                ins.then_inc(y_ps, 1)

            front(0)
            pick(0)
            with pe.Fori(0, blocks // 2) as pair:
                for u in range(2):
                    n = pair * 2 + u
                    pe.wait_ge(pick_sb, n + 1)
                    pe.wait_ge(masked_done, n)
                    for k in range(NHALF):
                        ins = nc.tensor.matmul(ps_mask[:, k], spread[:, k, :], pick16[:, u, :], start=True, stop=True)
                    ins.then_inc(mask_ps, 1)
                    front(n + 1)
                    back(n, u)
                    pick(n + 1)

        @block.scalar
        def _(act):
            def front(n, u):
                act.wait_ge(xt_ps, n + 1)
                if later(n):
                    act.wait_ge(h_ps, n)
                nc.scalar.activation(xt[:, :], ps_xt, ACT.Copy).then_inc(xt_sb, 1)
                act.wait_ge(h_ps, n + 1)
                if later(n):
                    act.wait_ge(masked_done, n - 1)
                for k in range(NHALF):
                    ins = nc.scalar.activation(hid[:, u, k, :], ps_h[:, k], ACT.Gelu, bias=b1[:, k:k + 1])
                ins.then_inc(h_sb, 1)
                act.wait_ge(pick_ps, n + 1)
                if later(n):
                    act.wait_ge(y_ps, n - 1)
                nc.scalar.activation(pick16[:, u, :], ps_pick[0:NE, :], ACT.Copy)
                nc.scalar.activation(pick32[:, u, :], ps_pick[0:NE, :], ACT.Copy).then_inc(pick_sb, 1)

            act.wait_ge(ready, 1)
            front(0, 0)
            with act.Fori(0, blocks // 2) as pair:
                for u in range(2):
                    front(pair * 2 + (u + 1), (u + 1) % 2)

        @block.vector
        def _(dve):
            w_step, w_settle, _ = chain(dve, w_chain, 0)
            dve.wait_ge(weights, n_weights)
            w_step(nc.vector.tensor_tensor(w1s[:, :, :], w1[:, :, :], lns[:, :].rearrange("p (e o) -> p e o", o=1)
                                            .broadcast_to([P, NE, EH]), ALU.mult))
            w_step(nc.vector.tensor_copy(spread[:, :, :], spread32[:, :, :]))
            dve.wait_ge(fold_ps, 1)
            w_step(nc.vector.tensor_tensor(folded[:, :, :], ps_fold, own[:, :, :], ALU.mult))
            w_settle()
            w_step(nc.vector.tensor_reduce(foldsum[:, :], folded[:, :, :], AX.X, ALU.add))
            w_settle()
            nc.vector.tensor_tensor(b1[:, :], b1[:, :], foldsum[:, :], ALU.add).then_inc(ready, 1)

            def norm(n):
                if later(n):
                    dve.wait_ge(xt_ps, n)
                normalise(nc, c, xh, n, c["rstd2"], BT).then_inc(xh_done, 1)

            def choose(n, step, settle):
                dve.wait_ge(logit_ps, n + 1)
                if later(n):
                    dve.wait_ge(pick_ps, n)
                pick_first_max(nc, step, settle, picked[:, :, :], ps_logit, order[:, :, :], peak[:, :], cand[:, :, :]).then_inc(picked_done, 1)

            norm(0)
            choose(0, w_step, w_settle)
            with dve.Fori(0, blocks // 2) as pair:
                for u in range(2):
                    n = pair * 2 + u
                    step, settle, steps = chain(dve, dve_chain, n * 6)
                    norm(n + 1)
                    dve.wait_ge(mask_ps, n + 1)
                    dve.wait_ge(h_sb, n + 1)
                    dve.wait_ge(y_ps, n)
                    for k in range(NHALF):
                        ins = nc.vector.tensor_tensor(masked[:, k, :], hid[:, u, k, :], ps_mask[:, k], ALU.mult)
                    ins.then_inc(masked_done, 1)
                    choose(n + 1, step, settle)
                    dve.wait_ge(y_ps, n + 1)
                    close(dve, n, step, settle, ps_y.rearrange("p (t d) -> p t d", t=BT))
                    assert steps() == 6


FEATURE_EPS = 1e-6
DEN_EPS = 1e-6


def linear_attention_stage(c, w):
    nc = c["nc"]
    with nc.cleanup_on_exit(), ExitStack() as ctx:
        sb = lambda name, shape, dt=F32: ctx.enter_context(nc.sbuf_tensor("b_" + name, shape, dt))
        sem = lambda n: nc.alloc_semaphore("b_" + n)
        wq, wk, wv, wo, bv, bk_row, bo = (sb(n, [P, D]) for n in ("wq", "wk", "wv", "wo", "bv", "bk_row", "bo"))
        bqk = sb("bqk", [P, 2])
        own, causal = sb("own", [P, NH * VW]), sb("causal", [P, P])
        xh, xt = sb("xh", [P, TPB, D]), sb("xt", [P, SEQ])
        raw = sb("raw", [P, 2, SEQ])
        qk = sb("qk", [P, 2, 2, SEQ])
        rest, parts = sb("rest", [P, 2, SEQ]), sb("parts", [P, 3, 2, SEQ], BF16)
        stack = sb("stack", [P, 2, 2, NH, SEQ], BF16)
        kn = sb("kn", [P, D])
        kv = sb("kv", [P, 2, NH * VW])
        va = sb("va", [P, 2, TPB, NH, VW])
        am = sb("am", [P, 4, 2, TPB, P])
        ot = sb("ot", [P, NG, SEQ])
        rec, att, att_t, delta = sb("rec", [P, TPB * NH]), sb("att", [P, TPB, D]), sb("att_t", [P, SEQ]), sb("delta", [P, TPB, D])
        fresh, summed, add, measure, close = updater(c, ctx, "b_")
        ps_s, ps_kv, ps_kn, ps_at, ps_o = c["psum"][:, 0:2], c["psum"][:, 2], c["psum"][:, 3, 0:P], c["psum"][:, 3, P:P + SEQ], c["psum"][:, 4:6]
        ps_qk, ps_xt, ps_v = c["psum"][:, 6], c["psum"][:, 7, 0:SEQ], c["psum"][:, 7, SEQ:2 * SEQ]
        ps_f, ps_y = c["psum"][:, 6:8], c["psum"][:, 6, 0:SEQ]

        weights, preset, dve_chain, pool_chain = (sem(n) for n in ("weights", "preset", "dve_chain", "pool_chain"))
        xh_done, xt_ps, xt_sb, qk_ps, v_ps, raw_done, qk_sb, v_sb, kn_sum, kn_done, kv_ps, kv_done, parts_done, stacked = (
            sem(n) for n in ("xh_done", "xt_ps", "xt_sb", "qk_ps", "v_ps", "raw_done", "qk_sb", "v_sb", "kn_sum", "kn_done",
                             "kv_ps", "kv_done", "parts_done", "stacked"))
        s_ready, m_done, av_done, o_done, f_ps, f_done, at_ps, at_sb, y_ps, y_used = (
            sem(n) for n in ("s_ready", "m_done", "av_done", "o_done", "f_ps", "f_done", "at_ps", "at_sb", "y_ps", "y_used"))
        n_weights = 16 * 10
        STACK = 16 * 2 * NTERM
        STEPS = NH // 2
        block = ctx.enter_context(nc.Block())

        @block.sync
        def _(sp):
            for dst, src in ((wq, "wq"), (wk, "wk"), (wv, "wv"), (wo, "wo"), (bv, "bv"), (bk_row, "bk_row"), (bo, "bo"),
                             (bqk, "bqk"), (own, "own"), (causal, "causal")):
                sp.dma_start(dst[:, :], w[src]).then_inc(weights, 16)

            def stack_up(n, u):
                sp.wait_ge(parts_done, n + 1)
                for t in range(NTERM):
                    for side, part in ((0, Q_PART[t]), (1, K_PART[t])):
                        sp.dma_start(stack[t * DH:(t + 1) * DH, u, side], parts[:, part, side, :]).then_inc(stacked, 16)

            sp.wait_ge(preset, 3)
            stack_up(0, 0)
            with sp.Fori(0, c["batches"] // 2) as pair:
                b = pair * 2
                for u in range(2):
                    stack_up(b + (u + 1), (u + 1) % 2)

        @block.gpsimd
        def _(pool):
            nc.gpsimd.memset(stack[:, 0], 0.0).then_inc(preset, 1)
            nc.gpsimd.memset(stack[:, 1], 0.0).then_inc(preset, 1)
            nc.gpsimd.memset(va[:, :, :, :, :], 0.0).then_inc(preset, 1)
            pool.wait_ge(preset, 3)
            nc.gpsimd.memset(va[:, :, :, :, DH:DH + 1], 1.0).then_inc(preset, 1)

            def split(n, u):
                pool.wait_ge(qk_sb, n + 1)
                if later(n):
                    pool.wait_ge(stacked, STACK * n)
                    pool.wait_ge(s_ready, STEPS * (n - 1))
                step, settle, steps = chain(pool, pool_chain, n * 1)
                hi, mid, lo = (parts[:, k] for k in range(3))
                nc.gpsimd.tensor_tensor(rest[:, :, :], qk[:, u], hi, ALU.subtract)
                step(nc.gpsimd.tensor_tensor(mid, qk[:, u], hi, ALU.subtract))
                settle()
                nc.gpsimd.tensor_tensor(lo, rest[:, :, :], mid, ALU.subtract).then_inc(parts_done, 1)

            split(0, 0)
            with pool.Fori(0, c["batches"] // 2) as pair:
                b = pair * 2
                for u in range(2):
                    split(b + (u + 1), (u + 1) % 2)

        @block.scalar
        def _(act):
            def copy_xt(n):
                act.wait_ge(xt_ps, n + 1)
                if later(n):
                    act.wait_ge(v_ps, n)
                nc.scalar.activation(xt[:, :], ps_xt, ACT.Copy).then_inc(xt_sb, 1)

            def relu_qk(n):
                act.wait_ge(qk_ps, n + 1)
                if later(n):
                    act.wait_ge(qk_sb, n)
                nc.scalar.activation(raw[:, 0, :], ps_qk[:, 0:SEQ], ACT.Relu, bias=bqk[:, 0:1])
                nc.scalar.activation(raw[:, 1, :], ps_qk[:, SEQ:2 * SEQ], ACT.Relu, bias=bqk[:, 1:2]).then_inc(raw_done, 1)

            def copy_out(n, g):
                act.wait_ge(av_done, n * NG + g + 1)
                if g == 0:
                    act.wait_ge(f_ps, n)
                nc.scalar.activation(ot[:, g, :], ps_o[:, g % 2, (g // 2) * SEQ:(g // 2 + 1) * SEQ],
                                     ACT.Copy).then_inc(o_done, 1)

            def copy_att(n):
                act.wait_ge(at_ps, n + 1)
                act.wait_ge(y_ps, n)
                nc.scalar.activation(att_t[:, :], ps_at, ACT.Copy).then_inc(at_sb, 1)

            act.wait_ge(weights, n_weights)
            copy_xt(0)
            relu_qk(0)
            with act.Fori(0, c["batches"] // 2) as pair:
                b = pair * 2
                for u in range(2):
                    n = b + u
                    copy_xt(n + 1)
                    relu_qk(n + 1)
                    for g in range(NG):
                        copy_out(n, g)
                    copy_att(n)

        @block.vector
        def _(dve):
            by_head = lambda t: t.rearrange("p (o h d) -> p o h d", o=1, h=NH).broadcast_to([P, TPB, NH, DH])
            every_block = causal[:, :].rearrange("p (o q) -> p o q", o=1).broadcast_to([P, 2 * TPB, P])

            def norm(n):
                if later(n):
                    dve.wait_ge(xt_ps, n)
                normalise(nc, c, xh, n, c["rstd"]).then_inc(xh_done, 1)

            def features(n, u):
                dve.wait_ge(raw_done, n + 1)
                if later(n):
                    dve.wait_ge(parts_done, n - 1)
                    dve.wait_ge(av_done, NG * (n - 1))
                    dve.wait_ge(stacked, STACK * n)
                nc.vector.tensor_scalar(qk[:, u], raw[:, :, :], FEATURE_EPS, None, ALU.add)
                nc.vector.tensor_scalar(parts[:, 0], raw[:, :, :], FEATURE_EPS, None, ALU.add).then_inc(qk_sb, 1)

            def natural(n, u):
                dve.wait_ge(v_ps, n + 1)
                nc.vector.tensor_tensor(va[:, u, :, :, 0:DH], ps_v.rearrange("p (t h d) -> p t h d", t=TPB, h=NH),
                                        by_head(bv[:, :]), ALU.add).then_inc(v_sb, 1)
                if later(n):
                    dve.wait_ge(kv_ps, n)
                nc.vector.tensor_tensor(kn[:, :], ps_kn, bk_row[:, :], ALU.add).then_inc(kn_sum, 1)
                dve.wait_ge(kn_sum, n + 1)
                nc.vector.tensor_scalar(kn[:, :], kn[:, :], 0.0, FEATURE_EPS, ALU.max, ALU.add).then_inc(kn_done, 1)

            def state(n, u):
                dve.wait_ge(kv_ps, n + 1)
                nc.vector.tensor_tensor(kv[:, u, :], ps_kv, own[:, :], ALU.mult).then_inc(kv_done, 1)

            def mask(n, s):
                dve.wait_ge(s_ready, n * STEPS + s + 1)
                if s >= 4:
                    dve.wait_ge(av_done, n * NG + s // 2 - 1)
                elif s % 2 == 0:
                    dve.wait_ge(av_done, n * NG)
                nc.vector.tensor_tensor(am[:, s % 4].rearrange("p h t q -> p (h t) q"),
                                        ps_s[:, s % 2].rearrange("p (b q) -> p b q", q=P), every_block, ALU.mult).then_inc(m_done, 1)

            def finish(n):
                step, settle, steps = chain(dve, dve_chain, n * 4)
                outs = ps_f.rearrange("p t (h v) -> p (t h) v", v=VW)
                dve.wait_ge(f_ps, n + 1)
                step(nc.vector.tensor_scalar(rec[:, :], outs[:, :, DH], DEN_EPS, None, ALU.max))
                settle()
                step(nc.vector.reciprocal(rec[:, :], rec[:, :]))
                settle()
                nc.vector.tensor_tensor(att[:, :, :].rearrange("p t (h d) -> p (t h) d", d=DH), outs[:, :, 0:DH],
                                        rec[:, :].rearrange("p (a o) -> p a o", o=1).broadcast_to([P, TPB * NH, DH]),
                                        ALU.mult).then_inc(f_done, 1)
                dve.wait_ge(y_ps, n + 1)
                nc.vector.tensor_tensor(delta[:, :, :], ps_y.rearrange("p (t d) -> p t d", t=TPB),
                                        bo[:, :].rearrange("p (o d) -> p o d", o=1).broadcast_to([P, TPB, D]), ALU.add).then_inc(y_used, 1)
                dve.wait_ge(y_used, n + 1)
                close(dve, n, step, settle, delta[:, :, :])
                assert steps() == 4

            dve.wait_ge(weights, n_weights)
            norm(0)
            features(0, 0)
            dve.wait_ge(preset, 4)
            natural(0, 0)
            state(0, 0)
            with dve.Fori(0, c["batches"] // 2) as pair:
                b = pair * 2
                for u in range(2):
                    n, v = b + u, (u + 1) % 2
                    norm(n + 1)
                    for s in range(STEPS):
                        mask(n, s)
                        if s == 2:
                            features(n + 1, v)
                        if s == 3:
                            natural(n + 1, v)
                        if s == 4:
                            state(n + 1, v)
                    finish(n)

        @block.tensor
        def _(pe):
            def transpose_x(n):
                pe.wait_ge(xh_done, n + 1)
                if later(n):
                    pe.wait_ge(xt_sb, n)
                    pe.wait_ge(y_used, n - 1)
                for t in range(TPB):
                    ins = nc.tensor.transpose(ps_xt[:, t * P:(t + 1) * P], xh[:, t, :], c["ident"][:, :])
                ins.then_inc(xt_ps, 1)

            def project(n):
                pe.wait_ge(xt_sb, n + 1)
                if later(n):
                    pe.wait_ge(raw_done, n)
                    pe.wait_ge(v_sb, n)
                    pe.wait_ge(kn_sum, n)
                nc.tensor.matmul(ps_qk[:, 0:SEQ], wq[:, :], xt[:, :], start=True, stop=True)
                nc.tensor.matmul(ps_qk[:, SEQ:2 * SEQ], wk[:, :], xt[:, :], start=True, stop=True).then_inc(qk_ps, 1)
                for t in range(TPB):
                    nc.tensor.matmul(ps_v[:, t * P:(t + 1) * P], xt[:, t * P:(t + 1) * P], wv[:, :], start=True, stop=True)
                nc.tensor.matmul(ps_kn, xt[:, 0:P], wk[:, :], start=True, stop=True).then_inc(v_ps, 1)

            def state(n, u):
                pe.wait_ge(kn_done, n + 1)
                pe.wait_ge(v_sb, n + 1)
                if later(n):
                    pe.wait_ge(kv_done, n)
                nc.tensor.matmul(ps_kv, kn[:, :], va[:, u, 0].rearrange("p h v -> p (h v)"), start=True, stop=True).then_inc(kv_ps, 1)

            def scores(n, u, s):
                if s == 0:
                    pe.wait_ge(stacked, STACK * (n + 1))
                if s >= 2 or later(n):
                    pe.wait_ge(m_done, n * STEPS + s - 1)
                for j in range(2):
                    for t in range(TPB):
                        here = slice(t * P, (t + 1) * P)
                        at = (j * TPB + t) * P
                        ins = nc.tensor.matmul(ps_s[:, s % 2, at:at + P], stack[:, u, 1, 2 * s + j, here],
                                               stack[:, u, 0, 2 * s + j, here], start=True, stop=True)
                ins.then_inc(s_ready, 1)

            def values(n, u, g):
                pe.wait_ge(m_done, n * STEPS + 2 * (g + 1))
                if g == 0:
                    pe.wait_ge(kv_done, n + 1)
                if g >= 2:
                    pe.wait_ge(o_done, n * NG + g - 1)
                bank, off = ps_o[:, g % 2], (g // 2) * SEQ

                def within(t, start):
                    for j in range(GH):
                        ins = nc.tensor.matmul(bank[j * VW:(j + 1) * VW, off + t * P:off + (t + 1) * P], va[:, u, t, g * GH + j, :],
                                               am[:, (2 * g + j // 2) % 4, j % 2, t, :], start=start, stop=True, tile_position=(0, j * VW))
                    return ins

                within(0, True)
                nc.tensor.matmul(bank[:, off + P:off + SEQ], kv[:, u, g * P:(g + 1) * P], qk[:, u, 0, P:SEQ], start=True, stop=False)
                within(1, False).then_inc(av_done, 1)

            def transpose_out(n):
                pe.wait_ge(o_done, NG * (n + 1))
                pe.wait_ge(xt_sb, n + 2)
                pe.wait_ge(raw_done, n + 2)
                pe.wait_ge(v_sb, n + 2)
                for t in range(TPB):
                    for g in range(NG):
                        ins = nc.tensor.transpose(ps_f[:, t, g * P:(g + 1) * P], ot[:, g, t * P:(t + 1) * P], c["ident"][:, :])
                ins.then_inc(f_ps, 1)

            def project_out(n):
                pe.wait_ge(f_done, n + 1)
                pe.wait_ge(kn_sum, n + 2)
                for t in range(TPB):
                    ins = nc.tensor.transpose(ps_at[:, t * P:(t + 1) * P], att[:, t, :], c["ident"][:, :])
                ins.then_inc(at_ps, 1)
                pe.wait_ge(at_sb, n + 1)
                for t in range(TPB):
                    ins = nc.tensor.matmul(ps_y[:, t * P:(t + 1) * P], att_t[:, t * P:(t + 1) * P], wo[:, :], start=True, stop=True)
                ins.then_inc(y_ps, 1)

            pe.wait_ge(weights, n_weights)
            transpose_x(0)
            project(0)
            state(0, 0)
            pe.wait_ge(preset, 4)
            scores(0, 0, 0)
            scores(0, 0, 1)
            with pe.Fori(0, c["batches"] // 2) as pair:
                b = pair * 2
                for u in range(2):
                    n, v = b + u, (u + 1) % 2
                    for s in range(STEPS):
                        if s == 0:
                            transpose_x(n + 1)
                        if s == 2:
                            project(n + 1)
                        if s == 4:
                            state(n + 1, v)
                        if s in (2, 4, 6):
                            values(n, u, s // 2 - 1)
                        scores(n, u, s + 2) if s + 2 < STEPS else scores(n + 1, v, s + 2 - STEPS)
                    values(n, u, NG - 1)
                    transpose_out(n)
                    project_out(n)


REL_CLIP = 128
UQ = P // NH // 2
NUNIT = P // UQ
REL_W = SEQ + P - 1


def attention_relative_stage(c, w):
    nc = c["nc"]
    scale = -1.0 / float(np.sqrt(DH))
    with nc.cleanup_on_exit(), ExitStack() as ctx:
        sb = lambda name, shape, dt=F32: ctx.enter_context(nc.sbuf_tensor("r_" + name, shape, dt))
        sem = lambda n: nc.alloc_semaphore("r_" + n)
        wq, wk, wv, wo, bv, bo = (sb(n, [P, D]) for n in ("wq", "wk", "wv", "wo", "bv", "bo"))
        bqk, own, part_of = sb("bqk", [P, 2]), sb("own", [P, NH]), sb("part_of", [P, 3])
        table = sb("table", [P, REL_W], BF16)
        xh, xt = sb("xh", [P, TPB, D]), sb("xt", [P, SEQ])
        qt, kt = sb("qt", [P, SEQ]), sb("kt", [P, 2, SEQ])
        split_q = sb("split_q", [P, 2, SEQ])
        rest, parts = sb("rest", [P, 2, SEQ]), sb("parts", [P, 3, 2, SEQ], BF16)
        stack = sb("stack", [P, 2, NH, SEQ], BF16)
        spread = sb("spread", [P, 2, P, NH, TPB])
        va = sb("va", [P, 2, TPB, NH, VW])
        nmax = sb("nmax", [P, 2, 2])
        prob = sb("prob", [P, 2, 2, SEQ])
        pt = sb("pt", [P, TPB, NH * TPB, P])
        ot = sb("ot", [P, NG, SEQ])
        rec, att, att_t, delta = sb("rec", [P, TPB * NH]), sb("att", [P, TPB, D]), sb("att_t", [P, SEQ]), sb("delta", [P, TPB, D])
        fresh, summed, add, measure, close = updater(c, ctx, "r_")
        ps_s, ps_t, ps_o = c["psum"][:, 0:2], c["psum"][:, 2:4], c["psum"][:, 4:6]
        ps_qk, ps_xt, ps_v = c["psum"][:, 6], c["psum"][:, 7, 0:SEQ], c["psum"][:, 7, SEQ:2 * SEQ]
        ps_f, ps_at, ps_y = c["psum"][:, 6:8], c["psum"][:, 4, 0:SEQ], c["psum"][:, 4, SEQ:2 * SEQ]

        weights, preset, bq_ready, table_chain, table_done, pool_chain, dve_chain = (
            sem(n) for n in ("weights", "preset", "bq_ready", "table_chain", "table_done", "pool_chain", "dve_chain"))
        xh_done, xt_ps, xt_sb, qk_ps, v_ps, qk_sb, v_sb, parts_done, stacked, spread_done = (
            sem(n) for n in ("xh_done", "xt_ps", "xt_sb", "qk_ps", "v_ps", "qk_sb", "v_sb", "parts_done", "stacked", "spread_done"))
        s_ready, m_done, e_done, t_done, ce_done, co_done, av_done, o_done, f_ps, f_done, at_ps, at_sb, y_ps, y_used = (
            sem(n) for n in ("s_ready", "m_done", "e_done", "t_done", "ce_done", "co_done", "av_done", "o_done", "f_ps", "f_done",
                             "at_ps", "at_sb", "y_ps", "y_used"))
        n_weights = 16 * 10
        STACK = 16 * 2 * NTERM
        STEPS = NUNIT // 2
        table32, table_rest = (prob[:, k].rearrange("p i k -> p (i k)")[:, 0:REL_W] for k in range(2))
        table_parts = [stack[:, 1, 2 * k:2 * k + 2].rearrange("p h q -> p (h q)")[:, 0:REL_W] for k in range(3)]
        def to_pt(s):
            return pt[:, :, :, s * 2 * UQ:(s + 1) * 2 * UQ].rearrange("p k m q -> p k q m")

        def from_ps(s):
            return ps_t[:, s % 2].rearrange("p (k q m) -> p k q m", k=TPB, m=NH * TPB)

        block = ctx.enter_context(nc.Block())

        @block.sync
        def _(sp):
            for dst, src in ((wq, "wq"), (wk, "wk"), (wv, "wv"), (wo, "wo"), (bv, "bv"), (bo, "bo"), (bqk, "bqk"), (own, "own"),
                             (part_of, "part_of")):
                sp.dma_start(dst[:, :], w[src]).then_inc(weights, 16)
            sp.dma_start(table32, w["table"]).then_inc(weights, 16)

            def stack_up(n, u):
                sp.wait_ge(parts_done, n + 1)
                for t in range(NTERM):
                    for side in range(2):
                        row = side * P // 2 + t * DH
                        sp.dma_start(stack[row:row + DH, u], parts[:, Q_PART[t], side, :]).then_inc(stacked, 16)

            sp.wait_ge(preset, 5)
            stack_up(0, 0)
            with sp.Fori(0, c["batches"] // 2) as pair:
                for u in range(2):
                    stack_up(pair * 2 + (u + 1), (u + 1) % 2)

        @block.gpsimd
        def _(pool):
            nc.gpsimd.memset(stack[:, 0], 0.0).then_inc(preset, 1)
            nc.gpsimd.memset(split_q[:, :, :], 0.0).then_inc(preset, 1)
            nc.gpsimd.memset(parts[:, 0], 0.0).then_inc(preset, 1)
            nc.gpsimd.memset(va[:, :, :, :, :], 0.0).then_inc(preset, 1)
            pool.wait_ge(table_done, 1)
            nc.gpsimd.memset(stack[:, 1], 0.0).then_inc(preset, 1)
            pool.wait_ge(preset, 5)
            nc.gpsimd.memset(va[:, :, :, :, DH:DH + 1], 1.0).then_inc(preset, 1)

            def split(n, u):
                pool.wait_ge(qk_sb, n + 1)
                if later(n):
                    pool.wait_ge(stacked, STACK * n)
                    pool.wait_ge(s_ready, STEPS * (n - 1))
                step, settle, steps = chain(pool, pool_chain, n * 1)
                hi, mid, lo = (parts[:, k] for k in range(3))
                nc.gpsimd.tensor_tensor(rest[:, :, :], split_q[:, :, :], hi, ALU.subtract)
                step(nc.gpsimd.tensor_tensor(mid, split_q[:, :, :], hi, ALU.subtract))
                settle()
                nc.gpsimd.tensor_tensor(lo, rest[:, :, :], mid, ALU.subtract).then_inc(parts_done, 1)
                nc.gpsimd.tensor_tensor(spread[:, u], qt[:, :].rearrange("p (t q o) -> p q o t", t=TPB, o=1).broadcast_to([P, P, NH, TPB]),
                                        own[:, :].rearrange("p (o h t) -> p o h t", o=1, t=1).broadcast_to([P, P, NH, TPB]),
                                        ALU.mult).then_inc(spread_done, 1)

            split(0, 0)
            with pool.Fori(0, c["batches"] // 2) as pair:
                for u in range(2):
                    split(pair * 2 + (u + 1), (u + 1) % 2)

        @block.scalar
        def _(act):
            act.wait_ge(weights, n_weights)
            nc.scalar.mul(bqk[:, 0:1], bqk[:, 0:1], scale).then_inc(bq_ready, 1)
            act.wait_ge(bq_ready, 1)
            act.wait_ge(preset, 5)

            def copy_xt(n):
                act.wait_ge(xt_ps, n + 1)
                if later(n):
                    act.wait_ge(v_ps, n)
                nc.scalar.activation(xt[:, :], ps_xt, ACT.Copy).then_inc(xt_sb, 1)

            def copy_qk(n, u):
                act.wait_ge(qk_ps, n + 1)
                if later(n):
                    act.wait_ge(spread_done, n)
                    act.wait_ge(stacked, STACK * n)
                    act.wait_ge(s_ready, STEPS * (n - 1))
                nc.scalar.activation(kt[:, u, :], ps_qk[:, SEQ:2 * SEQ], ACT.Identity, bias=bqk[:, 1:2])
                nc.scalar.activation(qt[:, :], ps_qk[:, 0:SEQ], ACT.Identity, bias=bqk[:, 0:1], scale=scale)
                for dst in (split_q, parts[:, 0]):
                    for side in range(2):
                        own_tile = slice(side * P, (side + 1) * P)
                        ins = nc.scalar.activation(dst[:, side, own_tile], ps_qk[:, own_tile], ACT.Identity,
                                                   bias=bqk[:, 0:1], scale=scale)
                ins.then_inc(qk_sb, 1)

            def exps(n, s, first=False):
                h = n * STEPS + s
                act.wait_ge(m_done, h + 1)
                if not first:
                    act.wait_ge(t_done, h - 1)
                for i in range(2):
                    ins = nc.scalar.activation(prob[:, s % 2, i, :], ps_s[:, s % 2, i * SEQ:(i + 1) * SEQ], ACT.Exp,
                                               bias=nmax[:, s % 2, i:i + 1], scale=-1.0)
                ins.then_inc(e_done, 1)

            def copy_pt(n, s):
                act.wait_ge(t_done, n * STEPS + s + 1)
                if s == 1:
                    act.wait_ge(av_done, n * NG)
                nc.scalar.activation(to_pt(s), from_ps(s), ACT.Copy).then_inc(co_done, 1)

            def copy_out(n, g):
                act.wait_ge(av_done, n * NG + g + 1)
                if g == 0:
                    act.wait_ge(f_ps, n)
                nc.scalar.activation(ot[:, g, :], ps_o[:, g % 2, (g // 2) * SEQ:(g // 2 + 1) * SEQ],
                                     ACT.Copy).then_inc(o_done, 1)

            def copy_att(n):
                act.wait_ge(at_ps, n + 1)
                act.wait_ge(y_ps, n)
                nc.scalar.activation(att_t[:, :], ps_at, ACT.Copy).then_inc(at_sb, 1)

            copy_xt(0)
            copy_qk(0, 0)
            exps(0, 0, first=True)
            with act.Fori(0, c["batches"] // 2) as pair:
                for u in range(2):
                    n = pair * 2 + u
                    for s in range(STEPS):
                        exps(n, s + 1) if s + 1 < STEPS else exps(n + 1, 0)
                        if s == 3:
                            copy_xt(n + 1)
                        if s == 5:
                            copy_qk(n + 1, (u + 1) % 2)
                        if s % 2:
                            copy_pt(n, s)
                    for g in range(NG):
                        copy_out(n, g)
                    copy_att(n)

        @block.vector
        def _(dve):
            bvb = bv[:, :].rearrange("p (o h d) -> p o h d", o=1, h=NH).broadcast_to([P, TPB, NH, DH])
            step, settle, steps = chain(dve, table_chain, 0)
            dve.wait_ge(weights, n_weights)
            hi, mid, lo = table_parts
            step(nc.vector.tensor_copy(hi, table32))
            settle()
            step(nc.vector.tensor_tensor(table_rest, table32, hi, ALU.subtract))
            settle()
            step(nc.vector.tensor_copy(mid, table_rest))
            settle()
            step(nc.vector.tensor_tensor(lo, table_rest, mid, ALU.subtract))
            step(nc.vector.tensor_scalar(table[:, :], hi, part_of[:, 0:1], None, ALU.mult))
            settle()
            step(nc.vector.scalar_tensor_tensor(table[:, :], mid, part_of[:, 1:2], table[:, :], ALU.mult, ALU.add))
            settle()
            nc.vector.scalar_tensor_tensor(table[:, :], lo, part_of[:, 2:3], table[:, :], ALU.mult, ALU.add).then_inc(table_done, 1)

            def norm(n):
                if later(n):
                    dve.wait_ge(xt_ps, n)
                normalise(nc, c, xh, n, c["rstd"]).then_inc(xh_done, 1)

            def copy_v(n, u):
                dve.wait_ge(v_ps, n + 1)
                if later(n):
                    dve.wait_ge(av_done, NG * (n - 1))
                nc.vector.tensor_tensor(va[:, u, :, :, 0:DH], ps_v.rearrange("p (t h d) -> p t h d", t=TPB, h=NH), bvb,
                                        ALU.add).then_inc(v_sb, 1)

            def maxima(n, s, first=False):
                h = n * STEPS + s
                dve.wait_ge(s_ready, h + 1)
                if not first:
                    dve.wait_ge(e_done, h - 1)
                nc.vector.tensor_reduce(nmax[:, s % 2, :], ps_s[:, s % 2].rearrange("p (i k) -> p i k", i=2), AX.X,
                                        ALU.min).then_inc(m_done, 1)

            def copy_pt(n, s):
                dve.wait_ge(t_done, n * STEPS + s + 1)
                if s == 0:
                    dve.wait_ge(av_done, n * NG)
                nc.vector.tensor_copy(to_pt(s), from_ps(s)).then_inc(ce_done, 1)

            def finish(n):
                step, settle, steps = chain(dve, dve_chain, n * 3)
                outs = ps_f.rearrange("p t (h v) -> p (t h) v", v=VW)
                dve.wait_ge(f_ps, n + 1)
                step(nc.vector.reciprocal(rec[:, :], outs[:, :, DH]))
                settle()
                nc.vector.tensor_tensor(att[:, :, :].rearrange("p t (h d) -> p (t h) d", d=DH), outs[:, :, 0:DH],
                                        rec[:, :].rearrange("p (a o) -> p a o", o=1).broadcast_to([P, TPB * NH, DH]),
                                        ALU.mult).then_inc(f_done, 1)
                dve.wait_ge(y_ps, n + 1)
                nc.vector.tensor_tensor(delta[:, :, :], ps_y.rearrange("p (t d) -> p t d", t=TPB),
                                        bo[:, :].rearrange("p (o d) -> p o d", o=1).broadcast_to([P, TPB, D]), ALU.add).then_inc(y_used, 1)
                dve.wait_ge(y_used, n + 1)
                close(dve, n, step, settle, delta[:, :, :])
                assert steps() == 3

            norm(0)
            dve.wait_ge(preset, 6)
            copy_v(0, 0)
            maxima(0, 0, first=True)
            with dve.Fori(0, c["batches"] // 2) as pair:
                for u in range(2):
                    n = pair * 2 + u
                    for s in range(STEPS):
                        maxima(n, s + 1) if s + 1 < STEPS else maxima(n + 1, 0)
                        if s == 1:
                            norm(n + 1)
                        if s == 6:
                            copy_v(n + 1, (u + 1) % 2)
                        if s % 2 == 0:
                            copy_pt(n, s)
                    finish(n)

        @block.tensor
        def _(pe):
            def transpose_x(n):
                pe.wait_ge(xh_done, n + 1)
                if later(n):
                    pe.wait_ge(xt_sb, n)
                    pe.wait_ge(f_done, n - 1)
                for t in range(TPB):
                    ins = nc.tensor.transpose(ps_xt[:, t * P:(t + 1) * P], xh[:, t, :], c["ident"][:, :])
                ins.then_inc(xt_ps, 1)

            def project(n):
                pe.wait_ge(xt_sb, n + 1)
                if later(n):
                    pe.wait_ge(qk_sb, n)
                    pe.wait_ge(v_sb, n)
                nc.tensor.matmul(ps_qk[:, 0:SEQ], wq[:, :], xt[:, :], start=True, stop=True)
                nc.tensor.matmul(ps_qk[:, SEQ:2 * SEQ], wk[:, :], xt[:, :], start=True, stop=True).then_inc(qk_ps, 1)
                for t in range(TPB):
                    ins = nc.tensor.matmul(ps_v[:, t * P:(t + 1) * P], xt[:, t * P:(t + 1) * P], wv[:, :], start=True, stop=True)
                ins.then_inc(v_ps, 1)

            def pair_stack(u, q):
                return stack[:, u].rearrange("p h (t q) -> p (h t) q", t=TPB)[:, :, q]

            def scores(n, u, s, first=False):
                h = n * STEPS + s
                if s == 0:
                    pe.wait_ge(stacked, STACK * (n + 1))
                    pe.wait_ge(spread_done, n + 1)
                if not first:
                    pe.wait_ge(e_done, h - 1)
                for i in range(2):
                    q0 = (2 * s + i) * UQ
                    nc.tensor.matmul(ps_s[:, s % 2, i * SEQ:(i + 1) * SEQ], spread[:, u, q0:q0 + UQ].rearrange("p q h t -> p (q h t)"),
                                     kt[:, u, :], start=True, stop=False)
                    for j in range(UQ):
                        both, at = pair_stack(u, q0 + j), P - 1 - (q0 + j)
                        row, width = j * NH * TPB, NH * TPB
                        ins = nc.tensor.matmul(ps_s[row:row + width, s % 2, i * SEQ:(i + 1) * SEQ], both, table[:, at:at + SEQ],
                                               start=False, stop=True, tile_position=(0, row))
                ins.then_inc(s_ready, 1)

            def transpose_p(n, s):
                pe.wait_ge(e_done, n * STEPS + s + 1)
                if s >= 2:
                    pe.wait_ge(co_done if s % 2 else ce_done, n * (STEPS // 2) + s // 2)
                for i in range(2):
                    for k in range(TPB):
                        ins = nc.tensor.transpose(ps_t[:, s % 2, k * SEQ + i * P:k * SEQ + (i + 1) * P],
                                                  prob[:, s % 2, i, k * P:(k + 1) * P], c["ident"][:, :])
                ins.then_inc(t_done, 1)

            def values(n, u, g):
                if g == 0:
                    pe.wait_ge(ce_done, (n + 1) * (STEPS // 2))
                    pe.wait_ge(co_done, (n + 1) * (STEPS // 2))
                    pe.wait_ge(v_sb, n + 1)
                    pe.wait_ge(y_used, n)
                if g >= 2:
                    pe.wait_ge(o_done, n * NG + g - 1)
                for k in range(TPB):
                    for j in range(GH):
                        ins = nc.tensor.matmul(ps_o[j * VW:(j + 1) * VW, g % 2, (g // 2) * SEQ:(g // 2 + 1) * SEQ],
                                               va[:, u, k, g * GH + j, :], pt[:, k, (g * GH + j) * TPB:(g * GH + j + 1) * TPB, :].rearrange("p t q -> p (t q)"),
                                               start=k == 0, stop=k == TPB - 1, tile_position=(0, j * VW))
                ins.then_inc(av_done, 1)

            def transpose_out(n):
                pe.wait_ge(o_done, NG * (n + 1))
                pe.wait_ge(xt_sb, n + 2)
                pe.wait_ge(qk_sb, n + 2)
                pe.wait_ge(v_sb, n + 2)
                for t in range(TPB):
                    for g in range(NG):
                        ins = nc.tensor.transpose(ps_f[:, t, g * P:(g + 1) * P], ot[:, g, t * P:(t + 1) * P], c["ident"][:, :])
                ins.then_inc(f_ps, 1)

            def project_out(n):
                pe.wait_ge(f_done, n + 1)
                for t in range(TPB):
                    ins = nc.tensor.transpose(ps_at[:, t * P:(t + 1) * P], att[:, t, :], c["ident"][:, :])
                ins.then_inc(at_ps, 1)
                pe.wait_ge(at_sb, n + 1)
                for t in range(TPB):
                    ins = nc.tensor.matmul(ps_y[:, t * P:(t + 1) * P], att_t[:, t * P:(t + 1) * P], wo[:, :], start=True, stop=True)
                ins.then_inc(y_ps, 1)

            pe.wait_ge(weights, n_weights)
            transpose_x(0)
            project(0)
            pe.wait_ge(table_done, 1)
            scores(0, 0, 0, first=True)
            scores(0, 0, 1, first=True)
            with pe.Fori(0, c["batches"] // 2) as pair:
                for u in range(2):
                    n = pair * 2 + u
                    for s in range(STEPS):
                        scores(n, u, s + 2) if s + 2 < STEPS else scores(n + 1, (u + 1) % 2, s + 2 - STEPS)
                        transpose_p(n, s)
                        if s == 2:
                            transpose_x(n + 1)
                        if s == 4:
                            project(n + 1)
                    for g in range(NG):
                        values(n, u, g)
                    transpose_out(n)
                    project_out(n)


def lay_out(inputs):
    a = {k: np.asarray(v) for k, v in inputs.items()}
    rows = lambda v: np.broadcast_to(v.reshape(1, -1), (P, v.size))
    by_width = lambda m: m.reshape(m.shape[0], NH, DH).transpose(0, 2, 1).reshape(m.shape[0], D)
    q, k = np.arange(SEQ)[:, None], np.arange(SEQ)[None, :]
    toeplitz = a["L0_attn_a_rel_emb"][:, q - k + SEQ - 1]
    of_expert = np.arange(NHALF * P).reshape(NHALF, P) // EH
    one_of = (of_expert[:, :, None] == np.arange(NE)).astype(np.float32)
    out = {
        "x": a["L0_attn_a_x"],
        "ident": np.eye(P, dtype=np.float32),
        "a_wq": by_width(a["L0_attn_a_Wq"]), "a_wk": by_width(a["L0_attn_a_Wk"]), "a_wv": a["L0_attn_a_Wv"],
        "a_bv": rows(a["L0_attn_a_bv"]),
        "a_bqk": np.stack([by_width(a["L0_attn_a_bq"][None])[0], by_width(a["L0_attn_a_bk"][None])[0]], 1),
        "a_bias": toeplitz.reshape(NH, TPB, P, SEQ).transpose(2, 0, 1, 3),
        "f_w1": a["L0_ffn_W1"].transpose(1, 0, 2), "f_b1": a["L0_ffn_b1"].reshape(NHALF, P).T,
        "f_lns": a["L0_ffn_ln_scale"].T, "f_lnb": a["L0_ffn_ln_bias"].T, "f_wg": a["L0_ffn_Wg"].T,
        "f_own": one_of.transpose(1, 0, 2), "f_spread": one_of.transpose(2, 0, 1),
        "f_w2": a["L0_ffn_W2"].reshape(NHALF, P, D).transpose(1, 0, 2), "f_b2": a["L0_ffn_b2"],
        "f_order": np.broadcast_to(np.arange(NE, 0, -1, dtype=np.float32), (P, BT, NE)),
    }
    qkv_w, qkv_b = a["L0_attn_b_qkv_w"].reshape(3, D, D), a["L0_attn_b_qkv_b"].reshape(3, D)
    head_of = np.arange(P) % NH
    out |= {
        "b_wq": by_width(qkv_w[0].T), "b_wk": by_width(qkv_w[1].T), "b_wv": qkv_w[2].T, "b_wo": a["L0_attn_b_out_w"].T,
        "b_bv": rows(qkv_b[2]), "b_bk_row": rows(by_width(qkv_b[1:2])[0]), "b_bo": rows(a["L0_attn_b_out_b"]),
        "b_bqk": np.stack([by_width(qkv_b[0:1])[0], by_width(qkv_b[1:2])[0]], 1),
        "b_own": (head_of[:, None] == np.arange(NH * VW) // VW).astype(np.float32),
        "b_causal": np.triu(np.ones((P, P), np.float32)),
    }
    rel = a["L1_attn_a_rel_emb"]
    table, part_of = np.zeros((P, REL_W), np.float32), np.zeros((P, 3), np.float32)
    for j in range(2):
        distance = np.clip(np.arange(REL_W) - (P - 1) - j * P, -REL_CLIP, REL_CLIP) + REL_CLIP
        for t in range(NTERM):
            at = j * P // 2 + t * DH
            table[at:at + DH] = rel[distance].T
            part_of[at:at + DH, K_PART[t]] = 1.0
    out |= {
        "r_wq": by_width(a["L1_attn_a_Wq"].T), "r_wk": by_width(a["L1_attn_a_Wk"].T), "r_wv": a["L1_attn_a_Wv"].T,
        "r_wo": a["L1_attn_a_Wo"].T, "r_bv": rows(a["L1_attn_a_bv"]), "r_bo": rows(a["L1_attn_a_bo"]),
        "r_bqk": np.stack([by_width(a["L1_attn_a_bq"][None])[0], by_width(a["L1_attn_a_bk"][None])[0]], 1),
        "r_own": (head_of[:, None] == np.arange(NH)).astype(np.float32), "r_table": table, "r_part_of": part_of,
    }
    w_qkv = a["L1_attn_b_w_qkv"].reshape(3, NH * CH, D)
    out |= {
        "c_wq": w_qkv[0].T, "c_wk": w_qkv[1].T, "c_wv": w_qkv[2].T,
        "c_wo": a["L1_attn_b_w_out"].T.reshape(NC, P, D).transpose(1, 0, 2),
        "c_mask": np.concatenate([np.zeros((P, P)), np.triu(np.full((P, P), BIG), 1)], 1).astype(np.float32),
    }
    shared, routed = a["L1_ffn_w_shared_in"], a["L1_ffn_w1_shared"]
    hidden = a["L1_ffn_w_shared_out"].shape[0]
    out |= {
        "g_in": np.stack([m.reshape(D, 2, hidden) for m in (shared, routed)], 1),
        "g_shared_out": a["L1_ffn_w_shared_out"], "g_w2": a["L1_ffn_w2"].transpose(1, 0, 2), "g_gate": a["L1_ffn_w_gate"],
        "g_gbias": np.broadcast_to(a["L1_ffn_gate_bias"], (P, BT, NE)), "g_order": out["f_order"],
    }
    return {k: np.ascontiguousarray(v) for k, v in out.items()}


def build(nc, w, out, stages=None):
    with ExitStack() as ctx:
        c = core(nc, ctx, w["x"].shape[0])
        sub = lambda p: {k[len(p):]: v for k, v in w.items() if k.startswith(p)}
        run = lambda k: stages is None or k in stages
        load_stage(c, w["x"], w["ident"])
        if run(1):
            rstd_stage(c, "0", False)
            attention_bias_stage(c, sub("a_"))
        if run(2):
            rstd_stage(c, "1", True)
            expert_stage(c, sub("f_"), "f0_")
        if run(3):
            rstd_stage(c, "2", False)
            linear_attention_stage(c, sub("b_"))
        if run(4):
            rstd_stage(c, "3", True)
            expert_stage(c, sub("f_"), "f1_")
        if run(5):
            rstd_stage(c, "4", False)
            attention_relative_stage(c, sub("r_"))
        if run(6):
            rstd_stage(c, "5", False)
            gated_expert_stage(c, sub("g_"), "g0_")
        if run(7):
            rstd_stage(c, "6", False)
            causal_attention_stage(c, sub("c_"))
        if run(8):
            rstd_stage(c, "7", False)
            gated_expert_stage(c, sub("g_"), "g1_")
        store_stage(c, out)


def kernel(**inputs):
    import concourse.bacc as bacc
    from concourse.bass_utils import run_bass_kernel_spmd

    nc = bacc.Bacc("TRN2", target_bir_lowering=False, num_devices=1)
    arrays = lay_out(inputs)
    w = {k: nc.dram_tensor("in_" + k, v.shape, mybir.dt.from_np(v.dtype), kind="ExternalInput").ap() for k, v in arrays.items()}
    out = nc.dram_tensor("out", arrays["x"].shape, F32, kind="ExternalOutput").ap()
    build(nc, w, out)
    result = run_bass_kernel_spmd(nc, [{"in_" + k: v for k, v in arrays.items()}], core_ids=[0])
    return result.results[0]["out"]
```

```python
import numpy as np
import concourse.bass as bass
from concourse import mybir
from contextlib import ExitStack

F32 = mybir.dt.float32
BF16 = mybir.dt.bfloat16
ALU = mybir.AluOpType
ACT = mybir.ActivationFunctionType
AX = mybir.AxisListType

P = 128
D = 128
SEQ = 256
TPB = SEQ // P
NH = 16
DH = D // NH
PAD = 8
VW = 32
GH = P // VW
NG = NH // GH
NTERM = 6
Q_PART = (0, 0, 0, 1, 1, 2)
K_PART = (0, 1, 2, 0, 1, 0)
LN_EPS = 1e-5
BIG = 3.0e38


def later(n, by=1):
    return not isinstance(n, int) or n >= by


def chain(engine, sem, base):
    done = [0]

    def step(instruction):
        done[0] += 1
        instruction.then_inc(sem, 1)

    def settle(but=0):
        count = base + (done[0] - but)
        if later(count):
            engine.wait_ge(sem, count)

    return step, settle, lambda: done[0]


def core(nc, ctx, n_batches):
    tiles = TPB * n_batches
    sb = lambda name, shape: ctx.enter_context(nc.sbuf_tensor(name, shape, F32))
    return {
        "nc": nc, "batches": n_batches, "tiles": tiles,
        "x": sb("x_stream", [P, tiles + PAD, D]),
        "moments": sb("moments", [P, tiles + PAD, 2]),
        "rstd": sb("rstd", [P, tiles + PAD]),
        "rstd2": sb("rstd2", [P, tiles + PAD]),
        "tmp": sb("norm_tmp", [P, 2, tiles + PAD]),
        "ident": sb("ident", [P, P]),
        "psum": ctx.enter_context(nc.psum_tensor("banks", [P, 8, 512], F32)),
    }


def load_steps(c, ctx, x_dram, ident_dram):
    nc = c["nc"]
    chunk = max(1, c["tiles"] // 8)
    n_chunks = c["tiles"] // chunk
    sem = nc.alloc_semaphore
    x_loaded = [sem(f"x_loaded{k}") for k in range(n_chunks)]
    ident_loaded, zeroed, stats_done, moments_done = sem("ident_loaded"), sem("zeroed"), sem("l_stats"), sem("l_mom")
    stats = ctx.enter_context(nc.sbuf_tensor("l_stats_sb", [P, 8, 6], F32))

    def issue(sp):
        src = x_dram.rearrange("b (t p) d -> p (b t) d", p=P)
        for k in range(n_chunks):
            sp.dma_start(c["x"][:, k * chunk:(k + 1) * chunk, :], src[:, k * chunk:(k + 1) * chunk, :]).then_inc(x_loaded[k], 16)
        sp.dma_start(c["ident"][:, :], ident_dram).then_inc(ident_loaded, 16)

    def take_moments(dve):
        nc.vector.memset(c["x"][:, c["tiles"]:, :], 0.0).then_inc(zeroed, 1)
        nc.vector.memset(c["moments"][:, c["tiles"]:, :], 0.0).then_inc(zeroed, 1)
        for k in range(n_chunks):
            dve.wait_ge(x_loaded[k], 16)
            for t in range(k * chunk, (k + 1) * chunk):
                if t >= 8:
                    dve.wait_ge(moments_done, t - 7)
                nc.vector.bn_stats(stats[:, t % 8, :], c["x"][:, t, :]).then_inc(stats_done, 1)
                if t % 4 == 3:
                    for u in range(t - 3, t + 1):
                        dve.wait_ge(stats_done, u + 1)
                        nc.vector.bn_aggr(c["moments"][:, u, :], stats[:, u % 8, :]).then_inc(moments_done, 1)
        dve.wait_ge(zeroed, 2)
        dve.wait_ge(moments_done, c["tiles"])

    return issue, take_moments, ident_loaded


def load_stage(c, x_dram, ident_dram):
    nc = c["nc"]
    with nc.cleanup_on_exit(), ExitStack() as ctx:
        issue, take_moments, ident_loaded = load_steps(c, ctx, x_dram, ident_dram)
        block = ctx.enter_context(nc.Block())

        @block.sync
        def _(sp):
            issue(sp)
            sp.wait_ge(ident_loaded, 16)

        @block.vector
        def _(dve):
            take_moments(dve)


def rstd_steps(c, tag, double):
    nc = c["nc"]
    chain_sem, root_in, root_out = (nc.alloc_semaphore(tag + n) for n in ("r_chain", "r_in", "r_out"))
    shifted, root = c["tmp"][:, 0, :], c["tmp"][:, 1, :]

    def take_roots(act):
        for k in range(2 if double else 1):
            act.wait_ge(root_in, k + 1)
            nc.scalar.activation(root, shifted, ACT.Sqrt).then_inc(root_out, 1)

    def take_rstd(dve):
        step, settle, steps = chain(dve, chain_sem, 0)

        def newton(out):
            step(nc.vector.reciprocal(out, root))
            settle()
            step(nc.vector.tensor_tensor(root, out, out, ALU.mult))
            settle()
            step(nc.vector.tensor_tensor(root, root, shifted, ALU.mult))
            settle()
            step(nc.vector.tensor_scalar(root, root, -0.5, 1.5, ALU.mult, ALU.add))
            settle()
            step(nc.vector.tensor_tensor(out, out, root, ALU.mult))
            settle()

        nc.vector.tensor_scalar(shifted, c["moments"][:, :, 1], LN_EPS, None, ALU.add).then_inc(root_in, 1)
        dve.wait_ge(root_out, 1)
        newton(c["rstd"][:, :])
        if double:
            step(nc.vector.tensor_tensor(shifted, c["rstd"][:, :], c["rstd"][:, :], ALU.mult))
            settle()
            step(nc.vector.tensor_tensor(shifted, shifted, c["moments"][:, :, 1], ALU.mult))
            settle()
            nc.vector.tensor_scalar(shifted, shifted, LN_EPS, None, ALU.add).then_inc(root_in, 1)
            dve.wait_ge(root_out, 2)
            newton(c["rstd2"][:, :])
            step(nc.vector.tensor_tensor(c["rstd2"][:, :], c["rstd2"][:, :], c["rstd"][:, :], ALU.mult))
            settle()

    return take_roots, take_rstd


def store_stage(c, out_dram):
    nc = c["nc"]
    with nc.cleanup_on_exit(), ExitStack() as ctx:
        stored = nc.alloc_semaphore("stored")
        block = ctx.enter_context(nc.Block())

        @block.sync
        def _(sp):
            dst = out_dram.rearrange("b (t p) d -> p (b t) d", p=P)
            n, step = 0, max(1, c["tiles"] // 4)
            for t in range(0, c["tiles"], step):
                sp.dma_start(dst[:, t:t + step, :], c["x"][:, t:t + step, :]).then_inc(stored, 16)
                n += 16
            sp.wait_ge(stored, n)


def each_pair(engine, count, unit):
    for u in range(2):
        unit(u, u)
    with engine.Fori(1, count // 2) as pair:
        for u in range(2):
            unit(pair * 2 + u, u)


def normalise(engine, c, xh, n, scale, tiles=TPB):
    for t in range(tiles):
        tile = bass.ds(n * tiles + t, 1)
        ins = engine.tensor_scalar(xh[:, t, :], c["x"][:, tile, :].rearrange("p a d -> p (a d)"),
                                      c["moments"][:, tile, 0], scale[:, tile], ALU.subtract, ALU.mult)
    return ins


def normalise_by_pool(pool, nc, c, xh, n, scale, centred, tiles=TPB):
    here = bass.ds(n * tiles, tiles)
    wide = lambda t: t.rearrange("p (t o) -> p t o", o=1).broadcast_to([P, tiles, D])
    nc.gpsimd.tensor_tensor(xh[:, :, :], c["x"][:, here, :], wide(c["moments"][:, here, 0]), ALU.subtract).then_inc(centred, 1)
    pool.wait_ge(centred, n + 1)
    return nc.gpsimd.tensor_tensor(xh[:, :, :], xh[:, :, :], wide(scale[:, here]), ALU.mult)


MEASURE_STEPS = 2


def updater(c, ctx, tag, tiles=TPB):
    nc = c["nc"]
    sb = lambda name, shape: ctx.enter_context(nc.sbuf_tensor(tag + name, shape, F32))
    fresh, stats, fresh_moments = sb("fresh", [P, tiles, D]), sb("stats", [P, tiles, 6]), sb("fresh_moments", [P, tiles, 2])
    summed, added, measured = (nc.alloc_semaphore(tag + n) for n in ("summed", "added", "measured"))

    def add(n, delta):
        nc.vector.tensor_tensor(fresh[:, :, :], c["x"][:, bass.ds(n * tiles, tiles), :], delta, ALU.add).then_inc(summed, 1)

    def measure(dve, n, step, settle, part):
        if part == 0:
            for t in range(tiles):
                ins = nc.vector.bn_stats(stats[:, t, :], fresh[:, t, :])
            step(ins)
        elif part == 1:
            settle()
            nc.vector.tensor_scalar(c["x"][:, bass.ds(n * tiles, tiles), :], fresh[:, :, :], 0.0, None, ALU.add).then_inc(added, 1)
            for t in range(tiles):
                ins = nc.vector.bn_aggr(fresh_moments[:, t, :], stats[:, t, :])
            step(ins)
        else:
            settle()
            nc.vector.tensor_scalar(c["moments"][:, bass.ds(n * tiles, tiles), :], fresh_moments[:, :, :], 0.0, None,
                                    ALU.add).then_inc(measured, 1)
            dve.wait_ge(measured, n + 1)

    def close(dve, n, step, settle, delta):
        add(n, delta)
        dve.wait_ge(summed, n + 1)
        for part in range(3):
            measure(dve, n, step, settle, part)

    return fresh, summed, added, add, measure, close


def attention_bias_stage(c, w, x_dram, ident_dram):
    nc = c["nc"]
    scale = -1.0 / float(np.sqrt(DH))
    DEPTH = 4
    with nc.cleanup_on_exit(), ExitStack() as ctx:
        sb = lambda name, shape, dt=F32: ctx.enter_context(nc.sbuf_tensor("a_" + name, shape, dt))
        sem = lambda n: nc.alloc_semaphore("a_" + n)
        wq, wk, wv, bv = (sb(n, [P, D]) for n in ("wq", "wk", "wv", "bv"))
        bqk, zero = sb("bqk", [P, 2]), sb("zero", [P, 2])
        bias = sb("bias", [P, NH, TPB, SEQ])
        xh = sb("xh", [P, TPB, D])
        xt = sb("xt", [P, 2, SEQ])
        qk = sb("qk", [P, 2, SEQ])
        rest = sb("rest", [P, 2, SEQ])
        parts = sb("parts", [P, 3, 2, SEQ], BF16)
        stack = sb("stack", [P, 2, 2, NH, SEQ], BF16)
        va = sb("va", [P, 2, TPB, NH, VW])
        sc = sb("sc", [P, DEPTH, TPB, SEQ])
        nmax = sb("nmax", [P, DEPTH, TPB])
        prob = sb("prob", [P, DEPTH, TPB, SEQ])
        pt = sb("pt", [P, 2, GH, TPB, SEQ])
        ot = sb("ot", [P, NG, SEQ])
        rec = sb("rec", [P, TPB * NH])
        att = sb("att", [P, TPB, D])
        fresh, summed, added, add, measure, close = updater(c, ctx, "a_")
        ps_s, ps_t, ps_o = c["psum"][:, 0:2], c["psum"][:, 2:4], c["psum"][:, 4:6]
        ps_qk, ps_xt, ps_v = c["psum"][:, 6], c["psum"][:, 7, 0:SEQ], c["psum"][:, 7, SEQ:2 * SEQ]
        ps_f = c["psum"][:, 6:8]

        passed = sem("passed")
        weights, bias_in, preset, cleared, bias_neg, bq_ready = (
            sem(n) for n in ("weights", "bias_in", "preset", "cleared", "bias_neg", "bq_ready"))
        xh_done, xt_ps, xt_sb, qk_ps, v_ps, qk_sb, v_sb, parts_done, stacked, pool_chain = (
            sem(n) for n in ("xh_done", "xt_ps", "xt_sb", "qk_ps", "v_ps", "qk_sb", "v_sb", "parts_done", "stacked", "pool_chain"))
        s_ready, m_done, e_done, t_done, ce_done, co_done, av_done, o_done, f_ps, f_done, dve_chain = (
            sem(n) for n in ("s_ready", "m_done", "e_done", "t_done", "ce_done", "co_done", "av_done", "o_done", "f_ps", "f_done", "dve_chain"))
        STACK = 16 * 2 * NTERM

        issue_loads, take_moments, ident_loaded = load_steps(c, ctx, x_dram, ident_dram)
        take_roots, take_rstd = rstd_steps(c, "a_", double=False)
        block = ctx.enter_context(nc.Block())

        @block.sync
        def _(sp):
            issue_loads(sp)
            for dst, src in ((wq, w["wq"]), (wk, w["wk"]), (wv, w["wv"]), (bv, w["bv"]), (bqk, w["bqk"])):
                sp.dma_start(dst[:, :], src).then_inc(weights, 16)
            for g in range(NG):
                sp.dma_start(bias[:, g * GH:(g + 1) * GH], w["bias"][:, g * GH:(g + 1) * GH]).then_inc(bias_in, 16)

            def stack_up(n, u):
                sp.wait_ge(parts_done, n + 1)
                for t in range(NTERM):
                    for side, part in ((0, Q_PART[t]), (1, K_PART[t])):
                        sp.dma_start(stack[t * DH:(t + 1) * DH, u, side], parts[:, part, side, :]).then_inc(stacked, 16)

            sp.wait_ge(cleared, 1)
            stack_up(0, 0)
            sp.wait_ge(preset, 4)
            stack_up(1, 1)
            each_pair(sp, c["batches"], lambda n, u: stack_up(n + 2, u))
            sp.wait_ge(stacked, STACK * (c["batches"] + 2))

        @block.gpsimd
        def _(pool):
            nc.gpsimd.memset(va[:, :, :, :, :], 0.0).then_inc(preset, 1)
            nc.gpsimd.memset(zero[:, :], 0.0).then_inc(preset, 1)
            nc.gpsimd.memset(stack[:, 1], 0.0).then_inc(preset, 1)
            pool.wait_ge(preset, 3)
            nc.gpsimd.memset(va[:, :, :, :, DH:DH + 1], 1.0).then_inc(preset, 1)

            def split(n):
                pool.wait_ge(qk_sb, n + 1)
                if later(n):
                    pool.wait_ge(stacked, STACK * n)
                step, settle, steps = chain(pool, pool_chain, n * 2)
                hi, mid, lo = (parts[:, k] for k in range(3))
                step(nc.gpsimd.tensor_tensor(hi, qk[:, :, :], zero[:, :].rearrange("p (a o) -> p a o", o=1).broadcast_to([P, 2, SEQ]), ALU.add))
                settle()
                nc.gpsimd.tensor_tensor(rest[:, :, :], qk[:, :, :], hi, ALU.subtract)
                step(nc.gpsimd.tensor_tensor(mid, qk[:, :, :], hi, ALU.subtract))
                settle()
                if later(n, 2):
                    pool.wait_ge(s_ready, NH * (n - 1))
                nc.gpsimd.tensor_tensor(lo, rest[:, :, :], mid, ALU.subtract).then_inc(parts_done, 1)

            split(0)
            split(1)
            each_pair(pool, c["batches"], lambda n, u: split(n + 2))

        @block.scalar
        def _(act):
            take_roots(act)
            act.wait_ge(weights, 16 * 5)
            nc.scalar.mul(bqk[:, 0:1], bqk[:, 0:1], scale).then_inc(bq_ready, 1)

            def copy_xt(n, u):
                act.wait_ge(xt_ps, n + 1)
                if later(n, 2):
                    act.wait_ge(v_ps, n - 1)
                nc.scalar.activation(xt[:, u], ps_xt, ACT.Copy).then_inc(xt_sb, 1)

            def copy_qk(n):
                act.wait_ge(qk_ps, n + 1)
                if later(n):
                    act.wait_ge(parts_done, n)
                nc.scalar.activation(qk[:, 0, :], ps_qk[:, 0:SEQ], ACT.Identity, bias=bqk[:, 0:1], scale=scale)
                nc.scalar.activation(qk[:, 1, :], ps_qk[:, SEQ:2 * SEQ], ACT.Identity, bias=bqk[:, 1:2]).then_inc(qk_sb, 1)

            def exps(n, s):
                h, at = n * NH + s, s % DEPTH
                act.wait_ge(m_done, h + 1)
                if s >= DEPTH or later(n):
                    act.wait_ge(t_done, h + 1 - DEPTH)
                for qt in range(TPB):
                    ins = nc.scalar.activation(prob[:, at, qt, :], sc[:, at, qt, :], ACT.Exp,
                                               bias=nmax[:, at, qt:qt + 1], scale=-1.0)
                ins.then_inc(e_done, 1)

            def copy_pt(n, s):
                act.wait_ge(t_done, n * NH + s + 1)
                g, j = s // GH, s % GH
                if j == 1 and (g > 1 or later(n)):
                    act.wait_ge(av_done, n * NG + g - 1)
                nc.scalar.activation(pt[:, g % 2, j], ps_t[:, s % 2].rearrange("p (k q) -> p k q", k=TPB),
                                     ACT.Copy).then_inc(co_done, 1)

            def copy_out(n, g):
                act.wait_ge(av_done, n * NG + g + 1)
                if g == 0 and later(n):
                    act.wait_ge(f_ps, n)
                nc.scalar.activation(ot[:, g, :], ps_o[:, g % 2, (g // 2) * SEQ:(g // 2 + 1) * SEQ],
                                     ACT.Copy).then_inc(o_done, 1)

            def batch(n, u):
                for s in range(NH):
                    exps(n, s + 1) if s + 1 < NH else exps(n + 1, 0)
                    if s == 0 and later(n):
                        copy_pt(n - 1, NH - 1)
                    if s == 0 and not later(n):
                        copy_qk(1)
                    if s == 2 and later(n):
                        copy_out(n - 1, NG - 1)
                    if s == 6:
                        copy_xt(n + 2, u)
                    if s == 9:
                        copy_qk(n + 2)
                    if s % 2 == 0 and s:
                        copy_pt(n, s - 1)
                    if s in (6, 10, 14):
                        copy_out(n, (s - 6) // 4)

            copy_xt(0, 0)
            act.wait_ge(bq_ready, 1)
            copy_qk(0)
            copy_xt(1, 1)
            exps(0, 0)
            each_pair(act, c["batches"], batch)
            copy_pt(c["batches"] - 1, NH - 1)
            copy_out(c["batches"] - 1, NG - 1)

        @block.vector
        def _(dve):
            take_moments(dve)
            take_rstd(dve)
            def norm(n):
                if later(n):
                    dve.wait_ge(xt_ps, n)
                normalise(nc.vector, c, xh, n, c["rstd"]).then_inc(xh_done, 1)

            def copy_v(n, u):
                dve.wait_ge(v_ps, n + 1)
                if later(n, 2):
                    dve.wait_ge(av_done, NG * (n - 1))
                nc.vector.tensor_tensor(va[:, u, :, :, 0:DH],
                                        ps_v.rearrange("p (t h d) -> p t h d", t=TPB, h=NH),
                                        bvb, ALU.add).then_inc(v_sb, 1)

            bvb = bv[:, :].rearrange("p (o h d) -> p o h d", o=1, h=NH).broadcast_to([P, TPB, NH, DH])

            def maxima(n, s):
                h, at = n * NH + s, s % DEPTH
                dve.wait_ge(s_ready, h + 1)
                if s >= DEPTH or later(n):
                    dve.wait_ge(e_done, h + 1 - DEPTH)
                dve.sem_inc(passed, 1)
                for qt in range(TPB):
                    ins = nc.vector.tensor_tensor_reduce(
                        out=sc[:, at, qt, :], in0=ps_s[:, s % 2, qt * SEQ:(qt + 1) * SEQ], in1=bias[:, s, qt, :],
                        scale=1.0, scalar=BIG, op0=ALU.add, op1=ALU.min, accum_out=nmax[:, at, qt:qt + 1])
                ins.then_inc(m_done, 1)

            def copy_pt(n, s):
                dve.wait_ge(t_done, n * NH + s + 1)
                g, j = s // GH, s % GH
                if j == 0 and (g > 1 or later(n)):
                    dve.wait_ge(av_done, n * NG + g - 1)
                nc.vector.tensor_copy(pt[:, g % 2, j], ps_t[:, s % 2].rearrange("p (k q) -> p k q", k=TPB)
                                      ).then_inc(ce_done, 1)

            def divide(n, step, settle):
                outs = ps_f.rearrange("p t (h v) -> p (t h) v", v=VW)
                dve.wait_ge(f_ps, n + 1)
                step(nc.vector.reciprocal(rec[:, :], outs[:, :, DH]))
                settle()
                nc.vector.tensor_tensor(att[:, :, :].rearrange("p t (h d) -> p (t h) d", d=DH), outs[:, :, 0:DH],
                                                rec[:, :].rearrange("p (a o) -> p a o", o=1).broadcast_to([P, TPB * NH, DH]), ALU.mult).then_inc(f_done, 1)

            def finish(n, step, settle):
                dve.wait_ge(f_done, n + 1)
                close(dve, n, step, settle, att[:, :, :])

            def batch(n, u):
                step, settle, steps = chain(dve, dve_chain, (n - 1) * 3)
                for s in range(NH):
                    maxima(n, s + 2) if s + 2 < NH else maxima(n + 1, s + 2 - NH)
                    if s % 2:
                        copy_pt(n, s - 1)
                    if s == 2:
                        norm(n + 2)
                    if s == 4 and later(n):
                        divide(n - 1, step, settle)
                    if s == 5 and later(n):
                        dve.wait_ge(f_done, n)
                        add(n - 1, att[:, :, :])
                    if s in (6, 7, 8) and later(n):
                        dve.wait_ge(summed, n)
                        measure(dve, n - 1, step, settle, s - 6)
                    if s == 12:
                        copy_v(n + 1, 1 - u)

            norm(0)
            nc.vector.memset(stack[:, 0], 0.0).then_inc(cleared, 1)
            norm(1)
            dve.wait_ge(weights, 16 * 5)
            dve.wait_ge(preset, 4)
            copy_v(0, 0)
            dve.wait_ge(bias_in, 16 * NG)
            for g in range(NG):
                group = bias[:, g * GH:(g + 1) * GH]
                nc.vector.tensor_scalar(group, group, -1.0, None, ALU.mult).then_inc(bias_neg, 1)
            dve.wait_ge(bias_neg, NG)
            maxima(0, 0)
            maxima(0, 1)
            each_pair(dve, c["batches"], batch)
            last = c["batches"] - 1
            step, settle, steps = chain(dve, dve_chain, last * 3)
            divide(last, step, settle)
            finish(last, step, settle)

        @block.tensor
        def _(pe):
            def transpose_x(n):
                pe.wait_ge(xh_done, n + 1)
                if later(n):
                    pe.wait_ge(xt_sb, n)
                    pe.wait_ge(v_sb, n - 1 if later(n, 2) else n)
                if later(n, 3):
                    pe.wait_ge(f_done, n - 2)
                for t in range(TPB):
                    ins = nc.tensor.transpose(ps_xt[:, t * P:(t + 1) * P], xh[:, t, :], c["ident"][:, :])
                ins.then_inc(xt_ps, 1)

            def project_qk(n, u):
                pe.wait_ge(xt_sb, n + 1)
                if later(n):
                    pe.wait_ge(qk_sb, n)
                nc.tensor.matmul(ps_qk[:, 0:SEQ], wq[:, :], xt[:, u], start=True, stop=True)
                nc.tensor.matmul(ps_qk[:, SEQ:2 * SEQ], wk[:, :], xt[:, u], start=True, stop=True).then_inc(qk_ps, 1)

            def project_v(n, u):
                if later(n):
                    pe.wait_ge(v_sb, n)
                    pe.wait_ge(xt_sb, n + 2)
                if later(n, 2):
                    pe.wait_ge(f_done, n - 1)
                for t in range(TPB):
                    ins = nc.tensor.matmul(ps_v[:, t * P:(t + 1) * P], xt[:, u, t * P:(t + 1) * P], wv[:, :], start=True, stop=True)
                ins.then_inc(v_ps, 1)

            def scores(n, u, s):
                h = n * NH + s
                if s == 0:
                    pe.wait_ge(stacked, STACK * (n + 1))
                if s >= 2 or later(n):
                    pe.wait_ge(m_done, h - 1)
                for qt in range(TPB):
                    ins = nc.tensor.matmul(ps_s[:, s % 2, qt * SEQ:(qt + 1) * SEQ], stack[:, u, 0, s, qt * P:(qt + 1) * P],
                                           stack[:, u, 1, s, :], start=True, stop=True)
                ins.then_inc(s_ready, 1)

            def transpose_p(n, s):
                pe.wait_ge(e_done, n * NH + s + 1)
                if s >= 2 or later(n):
                    pe.wait_ge(co_done if s % 2 else ce_done, n * (NH // 2) + s // 2)
                for qt in range(TPB):
                    for kt in range(TPB):
                        ins = nc.tensor.transpose(ps_t[:, s % 2, kt * SEQ + qt * P:kt * SEQ + (qt + 1) * P],
                                                  prob[:, s % DEPTH, qt, kt * P:(kt + 1) * P], c["ident"][:, :])
                ins.then_inc(t_done, 1)

            def values(n, u, g):
                pe.wait_ge(ce_done, n * (NH // 2) + 2 * (g + 1))
                pe.wait_ge(co_done, n * (NH // 2) + 2 * (g + 1))
                if g == 0:
                    pe.wait_ge(v_sb, n + 1)
                if g >= 2:
                    pe.wait_ge(o_done, n * NG + g - 1)
                for kt in range(TPB):
                    for j in range(GH):
                        ins = nc.tensor.matmul(ps_o[j * VW:(j + 1) * VW, g % 2, (g // 2) * SEQ:(g // 2 + 1) * SEQ],
                                               va[:, u, kt, g * GH + j, :], pt[:, g % 2, j, kt, :],
                                               start=kt == 0, stop=kt == TPB - 1, tile_position=(0, j * VW))
                ins.then_inc(av_done, 1)

            def transpose_out(n):
                pe.wait_ge(o_done, NG * (n + 1))
                pe.wait_ge(xt_sb, n + 3)
                pe.wait_ge(qk_sb, n + 3)
                pe.wait_ge(v_sb, n + 2)
                for t in range(TPB):
                    for g in range(NG):
                        ins = nc.tensor.transpose(ps_f[:, t, g * P:(g + 1) * P], ot[:, g, t * P:(t + 1) * P], c["ident"][:, :])
                ins.then_inc(f_ps, 1)

            def batch(n, u):
                for s in range(NH):
                    scores(n, u, s + 3) if s + 3 < NH else scores(n + 1, 1 - u, s + 3 - NH)
                    transpose_p(n, s)
                    if s == 1 and later(n):
                        values(n - 1, 1 - u, NG - 1)
                    if s == 3 and later(n):
                        transpose_out(n - 1)
                    if s == 5:
                        transpose_x(n + 2)
                    if s == 7:
                        project_qk(n + 2, u)
                    if s == 11:
                        project_v(n + 1, 1 - u)
                    if s in (5, 9, 13):
                        values(n, u, (s - 5) // 4)

            pe.wait_ge(ident_loaded, 16)
            transpose_x(0)
            pe.wait_ge(weights, 16 * 5)
            project_qk(0, 0)
            project_v(0, 0)
            transpose_x(1)
            project_qk(1, 1)
            pe.wait_ge(preset, 4)
            for s in range(3):
                scores(0, 0, s)
            each_pair(pe, c["batches"], batch)
            last = c["batches"] - 1
            values(last, last % 2, NG - 1)
            transpose_out(last)


CH = 64
NC = NH * CH // P
NPIECE = 12


def causal_attention_stage(c, w):
    nc = c["nc"]
    scale = -1.0 / float(np.sqrt(CH))
    DEPTH = 4
    with nc.cleanup_on_exit(), ExitStack() as ctx:
        sb = lambda name, shape, dt=F32: ctx.enter_context(nc.sbuf_tensor("c_" + name, shape, dt))
        sem = lambda n: nc.alloc_semaphore("c_" + n)
        wq, wk, wv = (sb(n, [P, NH * CH]) for n in ("wq", "wk", "wv"))
        wo = sb("wo", [P, NC, D])
        mask = sb("mask", [P, SEQ])
        xh, xt = sb("xh", [P, TPB, D]), sb("xt", [P, SEQ])
        q = sb("q", [P, 2, 2, NC, SEQ])
        k = sb("k", [P, 2, NC, SEQ])
        v = sb("v", [P, 2, TPB, NH * CH])
        sc, prob = sb("sc", [P, DEPTH, P + SEQ]), sb("prob", [P, DEPTH, P + SEQ])
        nmax, total, share = (sb(n, [P, DEPTH, TPB]) for n in ("nmax", "total", "share"))
        pt = sb("pt", [P, 4, P + SEQ])
        ot = sb("ot", [P, NC, SEQ])
        fresh, summed, added, add, measure, close = updater(c, ctx, "c_")
        ps_s, ps_t, ps_o, ring = c["psum"][:, 0:2], c["psum"][:, 2:4], c["psum"][:, 4:6], c["psum"][:, 6:8]
        ps_xt, ps_y = ring[:, 0, 0:SEQ], ps_o[:, 1, SEQ:2 * SEQ]
        piece_bank = lambda i: ring[:, (i + 1) % 2]
        SPAN = ((0, slice(0, P)), (1, slice(P, P + SEQ)))

        weights, preset, dve_chain = (sem(n) for n in ("weights", "preset", "dve_chain"))
        xh_done, xt_ps, xt_sb, piece_ps, act_pieces, dve_pieces = (
            sem(n) for n in ("xh_done", "xt_ps", "xt_sb", "piece_ps", "act_pieces", "dve_pieces"))
        passed, s_ready, m_done, e_done, inverted, n_done, t_done, ce_done, co_done, av_done, o_done, y_ps = (
            sem(n) for n in ("passed", "s_ready", "m_done", "e_done", "inverted", "n_done", "t_done", "ce_done", "co_done",
                             "av_done", "o_done", "y_ps"))
        n_weights = 16 * 5
        HALF = NPIECE // 2
        take_roots, take_rstd = rstd_steps(c, "c_", double=False)
        block = ctx.enter_context(nc.Block())

        @block.sync
        def _(sp):
            for dst, src in ((wq, "wq"), (wk, "wk"), (wv, "wv"), (mask, "mask")):
                sp.dma_start(dst[:, :], w[src]).then_inc(weights, 16)
            sp.dma_start(wo[:, :, :], w["wo"]).then_inc(weights, 16)

        @block.gpsimd
        def _(pool):
            nc.gpsimd.memset(q[:, :, :, :, :], 0.0).then_inc(preset, 1)

        def copy_piece(copy, n, u, i):
            bank = piece_bank(i)
            if i < 8:
                two = slice(i // 2 * 2, i // 2 * 2 + 2)
                if i % 2:
                    return copy(k[:, u, two, :].rearrange("p c t -> p (c t)"), bank)
                for j in range(2):
                    rows = slice(j * CH, (j + 1) * CH)
                    ins = nc.scalar.mul(q[rows, u, j, two, :].rearrange("p c t -> p (c t)"), bank[rows], scale)
                return ins
            t, half = divmod(i - 8, 2)
            return copy(v[:, u, t, half * 512:(half + 1) * 512], bank)

        @block.scalar
        def _(act):
            take_roots(act)
            def copy_xt(n):
                act.wait_ge(xt_ps, n + 1)
                if later(n):
                    act.wait_ge(piece_ps, NPIECE * n)
                nc.scalar.activation(xt[:, :], ps_xt, ACT.Copy).then_inc(xt_sb, 1)

            def piece(n, u, i):
                act.wait_ge(piece_ps, NPIECE * n + i + 1)
                if i == 0 and later(n, 2):
                    act.wait_ge(s_ready, NH * (n - 1))
                if i == 8 and later(n, 2):
                    act.wait_ge(av_done, NC * (n - 1))
                copy_piece(lambda out, in_: nc.scalar.activation(out, in_, ACT.Copy), n, u, i).then_inc(act_pieces, 1)

            def exps(n, s):
                h, at = n * NH + s, s % DEPTH
                act.wait_ge(m_done, h + 1)
                if s >= DEPTH or later(n):
                    act.wait_ge(t_done, h + 1 - DEPTH)
                for t, span in SPAN:
                    ins = nc.scalar.activation(prob[:, at, span], sc[:, at, span], ACT.Exp, bias=nmax[:, at, t:t + 1],
                                               scale=-1.0, accum_out=total[:, at, t:t + 1])
                ins.then_inc(e_done, 1)

            def copy_pt(n, s):
                act.wait_ge(t_done, n * NH + s + 1)
                ch = s // 2
                if ch >= 2 or later(n):
                    act.wait_ge(av_done, n * NC + ch - 1)
                nc.scalar.activation(pt[:, s % 4, :], ps_t[:, s % 2, 0:P + SEQ], ACT.Copy).then_inc(co_done, 1)

            def copy_out(n, ch):
                act.wait_ge(av_done, n * NC + ch + 1)
                if ch == 0 and later(n):
                    act.wait_ge(y_ps, n)
                nc.scalar.activation(ot[:, ch, :], ps_o[:, ch % 2, 0:SEQ], ACT.Copy).then_inc(o_done, 1)

            act.wait_ge(preset, 1)
            copy_xt(0)
            for i in range(0, NPIECE, 2):
                piece(0, 0, i)
            exps(0, 0)

            def batch(n, u):
                for s in range(NH):
                    exps(n, s + 1) if s + 1 < NH else exps(n + 1, 0)
                    if s == 1:
                        copy_xt(n + 1)
                    if s >= 2 and s % 2 == 0 and s - 2 < NPIECE:
                        piece(n + 1, 1 - u, s - 2)
                    if s == 0 and later(n):
                        copy_pt(n - 1, NH - 1)
                        copy_out(n - 1, NC - 2)
                    if s == 2 and later(n):
                        copy_out(n - 1, NC - 1)
                    if s % 2 == 0 and s:
                        copy_pt(n, s - 1)
                    if s % 2 == 0 and s >= 4:
                        copy_out(n, s // 2 - 2)

            each_pair(act, c["batches"], batch)
            last = c["batches"] - 1
            copy_pt(last, NH - 1)
            copy_out(last, NC - 2)
            copy_out(last, NC - 1)

        @block.vector
        def _(dve):
            take_rstd(dve)
            def norm(n):
                if later(n):
                    dve.wait_ge(xt_ps, n)
                normalise(nc.vector, c, xh, n, c["rstd"]).then_inc(xh_done, 1)

            def piece(n, u, i):
                dve.wait_ge(piece_ps, NPIECE * n + i + 1)
                if i == 1 and later(n, 2):
                    dve.wait_ge(s_ready, NH * (n - 1))
                if i == 9 and later(n, 2):
                    dve.wait_ge(av_done, NC * (n - 1))
                copy_piece(nc.vector.tensor_copy, n, u, i).then_inc(dve_pieces, 1)

            def maxima(n, s):
                h, at = n * NH + s, s % DEPTH
                dve.wait_ge(s_ready, h + 1)
                if s >= DEPTH or later(n):
                    dve.wait_ge(e_done, h + 1 - DEPTH)
                dve.sem_inc(passed, 1)
                for t, span in SPAN:
                    in1 = mask[:, P:SEQ] if t == 0 else mask[:, :]
                    ins = nc.vector.tensor_tensor_reduce(
                        out=sc[:, at, span], in0=ps_s[:, s % 2, span], in1=in1, scale=1.0, scalar=BIG, op0=ALU.add,
                        op1=ALU.min, accum_out=nmax[:, at, t:t + 1])
                ins.then_inc(m_done, 1)

            def invert(n, s):
                at = s % DEPTH
                dve.wait_ge(e_done, n * NH + s + 1)
                nc.vector.reciprocal(share[:, at, :], total[:, at, :]).then_inc(inverted, 1)

            def divide(n, s):
                at = s % DEPTH
                dve.wait_ge(inverted, n * NH + s + 1)
                for t, span in SPAN:
                    ins = nc.vector.tensor_scalar(prob[:, at, span], prob[:, at, span], share[:, at, t:t + 1], None, ALU.mult)
                ins.then_inc(n_done, 1)

            def copy_pt(n, s):
                dve.wait_ge(t_done, n * NH + s + 1)
                ch = s // 2
                if ch >= 2 or later(n):
                    dve.wait_ge(av_done, n * NC + ch - 1)
                nc.vector.tensor_copy(pt[:, s % 4, :], ps_t[:, s % 2, 0:P + SEQ]).then_inc(ce_done, 1)

            def add_result(n):
                dve.wait_ge(y_ps, n + 1)
                add(n, ps_y.rearrange("p (t d) -> p t d", t=TPB))

            norm(0)
            for i in range(1, NPIECE, 2):
                piece(0, 0, i)
            dve.wait_ge(weights, n_weights)
            maxima(0, 0)
            maxima(0, 1)

            def batch(n, u):
                step, settle, steps = chain(dve, dve_chain, (n - 1) * 2)
                for s in range(NH):
                    invert(n, s)
                    maxima(n, s + 2) if s + 2 < NH else maxima(n + 1, s + 2 - NH)
                    divide(n, s)
                    if s == 0:
                        norm(n + 1)
                    if s >= 3 and s % 2 and s - 2 < NPIECE:
                        piece(n + 1, 1 - u, s - 2)
                    if s % 2:
                        copy_pt(n, s - 1)
                    if s == 4 and later(n):
                        add_result(n - 1)
                    if s in (6, 8, 10) and later(n):
                        dve.wait_ge(summed, n)
                        measure(dve, n - 1, step, settle, s // 2 - 3)

            each_pair(dve, c["batches"], batch)
            last = c["batches"] - 1
            step, settle, steps = chain(dve, dve_chain, last * 2)
            add_result(last)
            dve.wait_ge(summed, last + 1)
            for part in range(3):
                measure(dve, last, step, settle, part)

        @block.tensor
        def _(pe):
            def transpose_x(n):
                pe.wait_ge(xh_done, n + 1)
                if later(n):
                    pe.wait_ge(dve_pieces, HALF * n)
                for t in range(TPB):
                    ins = nc.tensor.transpose(ps_xt[:, t * P:(t + 1) * P], xh[:, t, :], c["ident"][:, :])
                ins.then_inc(xt_ps, 1)

            def piece(n, i):
                if i == 0:
                    pe.wait_ge(xt_sb, n + 1)
                elif i >= 2:
                    pe.wait_ge(dve_pieces if i % 2 else act_pieces, HALF * n + i // 2)
                bank = piece_bank(i)
                if i < 8:
                    for j in range(2):
                        at = (i // 2 * 2 + j) * P
                        ins = nc.tensor.matmul(bank[:, j * SEQ:(j + 1) * SEQ], (wk if i % 2 else wq)[:, at:at + P], xt[:, :],
                                               start=True, stop=True)
                else:
                    t, half = divmod(i - 8, 2)
                    ins = nc.tensor.matmul(bank, xt[:, t * P:(t + 1) * P], wv[:, half * 512:(half + 1) * 512], start=True, stop=True)
                ins.then_inc(piece_ps, 1)

            def scores(n, u, s):
                h = n * NH + s
                if s == 0:
                    pe.wait_ge(act_pieces, HALF * n + 4)
                    pe.wait_ge(dve_pieces, HALF * n + 4)
                if s >= 2 or later(n):
                    pe.wait_ge(m_done, h - 1)
                for t, span in SPAN:
                    ins = nc.tensor.matmul(ps_s[:, s % 2, span], q[:, u, s % 2, s // 2, t * P:(t + 1) * P],
                                           k[:, u, s // 2, 0:(t + 1) * P], start=True, stop=True)
                ins.then_inc(s_ready, 1)

            def transpose_p(n, s):
                pe.wait_ge(n_done, n * NH + s + 1)
                if s >= 2 or later(n):
                    pe.wait_ge(co_done if s % 2 else ce_done, n * (NH // 2) + s // 2)
                for i in range(3):
                    ins = nc.tensor.transpose(ps_t[:, s % 2, i * P:(i + 1) * P], prob[:, s % DEPTH, i * P:(i + 1) * P], c["ident"][:, :])
                ins.then_inc(t_done, 1)

            def values(n, u, ch):
                pe.wait_ge(ce_done, n * (NH // 2) + ch + 1)
                pe.wait_ge(co_done, n * (NH // 2) + ch + 1)
                if ch == 0:
                    pe.wait_ge(act_pieces, HALF * (n + 1))
                    pe.wait_ge(dve_pieces, HALF * (n + 1))
                if ch >= 2 or later(n):
                    pe.wait_ge(o_done, n * NC + ch - 1)
                if ch == 1 and later(n):
                    pe.wait_ge(summed, n)
                for t in range(TPB):
                    for j in range(2):
                        head = 2 * ch + j
                        queries = slice(0, SEQ) if t == 0 else slice(P, SEQ)
                        weights_t = pt[:, head % 4, 0:SEQ] if t == 0 else pt[:, head % 4, SEQ:SEQ + P]
                        ins = nc.tensor.matmul(ps_o[j * CH:(j + 1) * CH, ch % 2, queries], v[:, u, t, head * CH:(head + 1) * CH],
                                               weights_t, start=t == 0, stop=t == TPB - 1, tile_position=(0, j * CH))
                ins.then_inc(av_done, 1)

            def project_out(n):
                pe.wait_ge(o_done, NC * (n + 1))
                for t in range(TPB):
                    for ch in range(NC):
                        ins = nc.tensor.matmul(ps_y[:, t * P:(t + 1) * P], ot[:, ch, t * P:(t + 1) * P], wo[:, ch, :],
                                               start=ch == 0, stop=ch == NC - 1)
                ins.then_inc(y_ps, 1)

            pe.wait_ge(weights, n_weights)
            transpose_x(0)
            for i in range(NPIECE):
                piece(0, i)
            for s in range(3):
                scores(0, 0, s)

            def batch(n, u):
                for s in range(NH):
                    scores(n, u, s + 3) if s + 3 < NH else scores(n + 1, 1 - u, s + 3 - NH)
                    transpose_p(n, s)
                    if s == 0:
                        transpose_x(n + 1)
                    if s == 1 and later(n):
                        values(n - 1, 1 - u, NC - 1)
                    if s >= 1 and s - 1 < NPIECE:
                        piece(n + 1, s - 1)
                    if s == 3 and later(n):
                        project_out(n - 1)
                    if s >= 3 and s % 2:
                        values(n, u, (s - 3) // 2)

            each_pair(pe, c["batches"], batch)
            last = c["batches"] - 1
            values(last, last % 2, NC - 1)
            project_out(last)


def gated_expert_stage(c, w, tag, out_dram=None):
    nc = c["nc"]
    blocks = c["tiles"] // BT
    H = w["shared_out"].shape[0]
    HALF = NE // 2
    with nc.cleanup_on_exit(), ExitStack() as ctx:
        sb = lambda name, shape, dt=F32: ctx.enter_context(nc.sbuf_tensor(tag + name, shape, dt))
        sem = lambda n: nc.alloc_semaphore(tag + n)
        w_in = sb("w_in", [P, 2, 2, H])
        w_so, w2, wg = sb("w_so", [P, D]), sb("w2", [P, NE, D]), sb("wg", [P, NE])
        gbias, order = sb("gbias", [P, BT, NE]), sb("order", [P, BT, NE])
        xh, xt = sb("xh", [P, BT, D]), sb("xt", [P, 2, BTOK])
        gate = sb("gate", [P, 2, BTOK])
        hid = sb("hid", [P, 2, 2, BTOK])
        logit, prob, left, cand, pick1, pick2 = (sb(n, [P, BT, NE]) for n in ("logit", "prob", "left", "cand", "pick1", "pick2"))
        weight = sb("weight", [P, 2, BT, NE])
        peak, total = sb("peak", [P, BT]), sb("total", [P, BT])
        fresh, summed, added, add, measure, close = updater(c, ctx, tag, BT)
        ps_xt, ps_ab, ps_r, ps_so = c["psum"][:, 0], c["psum"][:, 1:3], c["psum"][:, 3:7], c["psum"][:, 7]
        ps_logit = ps_xt[:, 0:BT * NE].rearrange("p (t e) -> p t e", e=NE)

        weights, stored, rstd_done, centred, dve_chain, gate_chain = (
            sem(n) for n in ("weights", "stored", "rstd_done", "centred", "dve_chain", "gate_chain"))
        xh_done, xt_ps, xt_sb, logit_ps, logit_sb, exp_in, exp_out, ab_ps, gate_sb, hid_done, so_ps, r_ps, r_used, weighed = (
            sem(n) for n in ("xh_done", "xt_ps", "xt_sb", "logit_ps", "logit_sb", "exp_in", "exp_out", "ab_ps", "gate_sb",
                             "hid_done", "so_ps", "r_ps", "r_used", "weighed"))
        n_weights = 16 * 6
        GATE = 16
        take_roots, take_rstd = rstd_steps(c, tag, double=False)
        block = ctx.enter_context(nc.Block())

        @block.sync
        def _(sp):
            for dst, src in ((w_in, "in"), (w_so, "shared_out"), (w2, "w2"), (wg, "gate"), (gbias, "gbias"), (order, "order")):
                sp.dma_start(dst[tuple(slice(None) for _ in dst.shape)], w[src]).then_inc(weights, 16)
            if out_dram is not None:
                dst = out_dram.rearrange("b (t p) d -> p (b t) d", p=P)

                def store(n, u):
                    here = bass.ds(n * BT, BT)
                    sp.wait_ge(added, n + 1)
                    sp.dma_start(dst[:, here, :], c["x"][:, here, :]).then_inc(stored, 16)

                each_pair(sp, blocks, store)
                sp.wait_ge(stored, 16 * blocks)

        @block.tensor
        def _(pe):
            def transpose_x(n):
                pe.wait_ge(xh_done, n + 1)
                if later(n):
                    pe.wait_ge(logit_sb, n)
                for t in range(BT):
                    ins = nc.tensor.transpose(ps_xt[:, t * P:(t + 1) * P], xh[:, t, :], c["ident"][:, :])
                ins.then_inc(xt_ps, 1)

            def logits(n, u):
                pe.wait_ge(xt_sb, n + 1)
                for t in range(BT):
                    ins = nc.tensor.matmul(ps_logit[:, t, :], xt[:, u, t * P:(t + 1) * P], wg[:, :], start=True, stop=True)
                ins.then_inc(logit_ps, 1)

            def hidden(n, u, k):
                if k or later(n):
                    pe.wait_ge(hid_done, n * 2 + k)
                for ab in range(2):
                    ins = nc.tensor.matmul(ps_ab[:, ab], w_in[:, k, ab, :], xt[:, u], start=True, stop=True)
                ins.then_inc(ab_ps, 1)

            def shared(n, u):
                pe.wait_ge(hid_done, n * 2 + 1)
                if later(n):
                    pe.wait_ge(summed, n)
                for t in range(BT):
                    ins = nc.tensor.matmul(ps_so[:, t * P:(t + 1) * P], hid[:, u, 0, t * P:(t + 1) * P], w_so[:, :], start=True, stop=True)
                ins.then_inc(so_ps, 1)

            def routed(n, u, k):
                if k == 0:
                    pe.wait_ge(hid_done, n * 2 + 2)
                if k >= 2:
                    pe.wait_ge(r_used, n * 4 + k - 1)
                elif later(n):
                    pe.wait_ge(r_used, n * 4 + k - 1)
                for t in range(2):
                    tile, half = (k // 2) * 2 + t, k % 2
                    ins = nc.tensor.matmul(ps_r[:, (k % 2) * 2 + t], hid[:, u, 1, tile * P:(tile + 1) * P],
                                           w2[:, half * HALF:(half + 1) * HALF, :].rearrange("p e d -> p (e d)"), start=True, stop=True)
                ins.then_inc(r_ps, 1)

            pe.wait_ge(weights, n_weights)
            transpose_x(0)
            logits(0, 0)
            hidden(0, 0, 0)
            transpose_x(1)
            hidden(0, 0, 1)

            def unit(n, u):
                shared(n, u)
                routed(n, u, 0)
                logits(n + 1, 1 - u)
                routed(n, u, 1)
                hidden(n + 1, 1 - u, 0)
                routed(n, u, 2)
                transpose_x(n + 2)
                hidden(n + 1, 1 - u, 1)
                routed(n, u, 3)

            each_pair(pe, blocks, unit)

        @block.gpsimd
        def _(pool):
            def norm(n):
                if later(n):
                    pool.wait_ge(xt_ps, n)
                normalise_by_pool(pool, nc, c, xh, n, c["rstd"], centred, BT).then_inc(xh_done, 1)

            pool.wait_ge(rstd_done, 1)
            norm(0)
            norm(1)
            each_pair(pool, blocks, lambda n, u: norm(n + 2))

        @block.scalar
        def _(act):
            take_roots(act)
            def copy_xt(n, u):
                act.wait_ge(xt_ps, n + 1)
                if later(n, 2):
                    act.wait_ge(ab_ps, (n - 1) * 2)
                nc.scalar.activation(xt[:, u], ps_xt, ACT.Copy).then_inc(xt_sb, 1)

            def silu(n, k):
                act.wait_ge(ab_ps, n * 2 + k + 1)
                if later(n):
                    act.wait_ge(hid_done, n * 2 + k - 1)
                nc.scalar.activation(gate[:, k, :], ps_ab[:, 0], ACT.Silu).then_inc(gate_sb, 1)

            def exp(n):
                act.wait_ge(exp_in, n + 1)
                nc.scalar.activation(prob[:, :, :], logit[:, :, :], ACT.Exp).then_inc(exp_out, 1)

            def ahead(n, u):
                exp(n)
                silu(n, 0)
                copy_xt(n + 1, 1 - u)
                silu(n, 1)

            copy_xt(0, 0)
            ahead(0, 0)
            each_pair(act, blocks, lambda n, u: ahead(n + 1, 1 - u))

        @block.vector
        def _(dve):
            take_rstd(dve)
            dve.sem_inc(rstd_done, 1)
            wide = lambda t: t.rearrange("p (a o) -> p a o", o=1).broadcast_to([P, BT, NE])

            def multiply(n, u, k):
                dve.wait_ge(gate_sb, n * 2 + k + 1)
                if later(n, 2):
                    dve.wait_ge(r_ps if k else so_ps, n * 4 - 4 if k else n - 1)
                nc.vector.tensor_tensor(hid[:, u, k, :], gate[:, k, :], ps_ab[:, 1], ALU.mult).then_inc(hid_done, 1)

            def gate_front(n, g_step, g_settle):
                dve.wait_ge(logit_ps, n + 1)
                nc.vector.tensor_tensor(logit[:, :, :], ps_logit, gbias[:, :, :], ALU.add).then_inc(logit_sb, 1)
                dve.wait_ge(logit_sb, n + 1)
                g_step(nc.vector.tensor_reduce(peak[:, :], logit[:, :, :], AX.X, ALU.max))
                g_settle()
                nc.vector.tensor_tensor(logit[:, :, :], logit[:, :, :], wide(peak[:, :]), ALU.subtract).then_inc(exp_in, 1)

            def gate_back(n, u, i, g_step, g_settle):
                if i == 0:
                    dve.wait_ge(exp_out, n + 1)
                    g_step(nc.vector.tensor_reduce(total[:, :], prob[:, :, :], AX.X, ALU.add))
                    return
                g_settle()
                if i == 1:
                    g_step(nc.vector.reciprocal(total[:, :], total[:, :]))
                elif i == 2:
                    g_step(nc.vector.tensor_tensor(prob[:, :, :], prob[:, :, :], wide(total[:, :]), ALU.mult))
                elif i < 8:
                    g_step(pick_step(nc, i - 3, pick1[:, :, :], prob[:, :, :], order[:, :, :], peak[:, :], cand[:, :, :]))
                elif i == 8:
                    g_step(nc.vector.scalar_tensor_tensor(left[:, :, :], pick1[:, :, :], -2.0, prob[:, :, :], ALU.mult, ALU.add))
                elif i < 14:
                    g_step(pick_step(nc, i - 9, pick2[:, :, :], left[:, :, :], order[:, :, :], peak[:, :], cand[:, :, :]))
                elif i == 14:
                    g_step(nc.vector.tensor_tensor(pick1[:, :, :], pick1[:, :, :], pick2[:, :, :], ALU.add))
                else:
                    nc.vector.tensor_tensor(weight[:, u, :, :], prob[:, :, :], pick1[:, :, :], ALU.mult).then_inc(weighed, 1)

            def add_shared(n):
                dve.wait_ge(so_ps, n + 1)
                add(n, ps_so.rearrange("p (t d) -> p t d", t=BT))
                dve.wait_ge(summed, n + 1)
                dve.wait_ge(weighed, n + 1)

            def add_routed(n, u, k, step, settle, between=None):
                dve.wait_ge(r_ps, n * 4 + k + 1)
                for e in range(HALF):
                    for t in range(2):
                        tile, expert = (k // 2) * 2 + t, (k % 2) * HALF + e
                        acc = fresh[:, tile, :]
                        ins = nc.vector.scalar_tensor_tensor(acc, ps_r[:, (k % 2) * 2 + t, e * D:(e + 1) * D],
                                                             weight[:, u, tile, expert:expert + 1], acc, ALU.mult, ALU.add)
                        last = e == HALF - 1 and t == 1
                        if last:
                            ins.then_inc(r_used, 1)
                        else:
                            step(ins)
                        if between:
                            between(e * 2 + t)
                        if not last:
                            settle(but=1)
                dve.wait_ge(r_used, n * 4 + k + 1)

            dve.wait_ge(weights, n_weights)
            g_step, g_settle, g_steps = chain(dve, gate_chain, 0)
            gate_front(0, g_step, g_settle)
            multiply(0, 0, 0)
            multiply(0, 0, 1)
            for i in range(GATE):
                gate_back(0, 0, i, g_step, g_settle)

            def unit(n, u):
                step, settle, steps = chain(dve, dve_chain, n * (4 * 7 + MEASURE_STEPS))
                g_step, g_settle, g_steps = chain(dve, gate_chain, (n + 1) * GATE)
                add_shared(n)
                add_routed(n, u, 0, step, settle)
                gate_front(n + 1, g_step, g_settle)
                add_routed(n, u, 1, step, settle)
                multiply(n + 1, 1 - u, 0)
                add_routed(n, u, 2, step, settle, lambda i: gate_back(n + 1, 1 - u, i, g_step, g_settle))
                multiply(n + 1, 1 - u, 1)
                add_routed(n, u, 3, step, settle, lambda i: gate_back(n + 1, 1 - u, 8 + i, g_step, g_settle))
                for part in range(3):
                    measure(dve, n, step, settle, part)
                assert steps() == 4 * 7 + MEASURE_STEPS and g_steps() == GATE

            each_pair(dve, blocks, unit)


BT = 4
BTOK = BT * P
NE = 8
EH = 32
NHALF = NE * EH // P


def pick_step(nc, i, picked, values, order, peak, cand):
    wide = lambda t: t.rearrange("p (a o) -> p a o", o=1).broadcast_to([P, BT, NE])
    if i == 0:
        return nc.vector.tensor_reduce(peak, values, AX.X, ALU.max)
    if i == 1:
        return nc.vector.tensor_tensor(cand, values, wide(peak), ALU.is_equal)
    if i == 2:
        return nc.vector.tensor_tensor(cand, cand, order, ALU.mult)
    if i == 3:
        return nc.vector.tensor_reduce(peak, cand, AX.X, ALU.max)
    return nc.vector.tensor_tensor(picked, cand, wide(peak), ALU.is_equal)


def expert_stage(c, w, tag):
    nc = c["nc"]
    blocks = c["tiles"] // BT
    with nc.cleanup_on_exit(), ExitStack() as ctx:
        sb = lambda name, shape, dt=F32: ctx.enter_context(nc.sbuf_tensor(tag + name, shape, dt))
        sem = lambda n: nc.alloc_semaphore(tag + n)
        w1, w1s, b1 = sb("w1", [P, NE, EH]), sb("w1s", [P, NE, EH]), sb("b1", [P, NHALF])
        lns, lnb, wg = (sb(n, [P, NE]) for n in ("lns", "lnb", "wg"))
        own = sb("own", [P, NHALF, NE])
        foldsum = sb("foldsum", [P, NHALF])
        folded = sb("folded", [P, NHALF, NE])
        w2, b2 = sb("w2", [P, NHALF, D]), sb("b2", [NE, D])
        spread32, spread = sb("spread32", [NE, NHALF, P]), sb("spread", [NE, NHALF, P], BF16)
        order = sb("order", [P, BT, NE])
        xh, xt = sb("xh", [P, BT, D]), sb("xt", [P, 2, BTOK])
        hid, masked = (sb(n, [P, 2, NHALF, BTOK]) for n in ("hid", "masked"))
        peak, cand, picked = sb("peak", [P, BT]), sb("cand", [P, BT, NE]), sb("picked", [P, BT, NE])
        pick32, pick16 = sb("pick32", [NE, 2, BTOK]), sb("pick16", [NE, 2, BTOK], BF16)
        fresh, summed, added, add, measure, close = updater(c, ctx, tag, BT)
        ps_xt, ps_h, ps_small, ps_pick, ps_mask, ps_y = (
            c["psum"][:, 0], c["psum"][:, 1:3], c["psum"][:, 3], c["psum"][:, 4], c["psum"][:, 5:7], c["psum"][:, 7])
        ps_logit = ps_small[:, 0:BT * NE].rearrange("p (t e) -> p t e", e=NE)
        ps_fold = ps_small[:, 64:64 + NHALF * NE].rearrange("p (t e) -> p t e", e=NE)

        weights, rstd_done, centred, fold_ps, ready, w_chain, dve_chain = (
            sem(n) for n in ("weights", "rstd_done", "centred", "fold_ps", "ready", "w_chain", "dve_chain"))
        xh_done, xt_ps, xt_sb, h_ps, logit_ps, h_sb, picked_done, pick_ps, pick_sb, mask_ps, masked_done, y_ps = (
            sem(n) for n in ("xh_done", "xt_ps", "xt_sb", "h_ps", "logit_ps", "h_sb", "picked_done", "pick_ps", "pick_sb",
                             "mask_ps", "masked_done", "y_ps"))
        n_weights = 16 * 10
        take_roots, take_rstd = rstd_steps(c, tag, double=True)
        block = ctx.enter_context(nc.Block())

        @block.sync
        def _(sp):
            for dst, src in ((w1, "w1"), (b1, "b1"), (lns, "lns"), (lnb, "lnb"), (wg, "wg"), (own, "own"), (w2, "w2"),
                             (b2, "b2"), (spread32, "spread"), (order, "order")):
                sp.dma_start(dst[tuple(slice(None) for _ in dst.shape)], w[src]).then_inc(weights, 16)

        @block.tensor
        def _(pe):
            pe.wait_ge(weights, n_weights)
            for k in range(NHALF):
                ins = nc.tensor.matmul(ps_fold[:, k, :], w1[:, k * NE // NHALF:(k + 1) * NE // NHALF, :].rearrange("p e h -> p (e h)"),
                                       lnb[:, :], start=True, stop=True)
            ins.then_inc(fold_ps, 1)
            pe.wait_ge(ready, 1)

            def transpose_x(n):
                pe.wait_ge(xh_done, n + 1)
                if later(n):
                    pe.wait_ge(xt_sb, n)
                for t in range(BT):
                    ins = nc.tensor.transpose(ps_xt[:, t * P:(t + 1) * P], xh[:, t, :], c["ident"][:, :])
                ins.then_inc(xt_ps, 1)

            def products(n, u):
                pe.wait_ge(xt_sb, n + 1)
                if later(n):
                    pe.wait_ge(h_sb, n)
                    pe.wait_ge(picked_done, n)
                for t in range(BT):
                    ins = nc.tensor.matmul(ps_logit[:, t, :], xt[:, u, t * P:(t + 1) * P], wg[:, :], start=True, stop=True)
                ins.then_inc(logit_ps, 1)
                for k in range(NHALF):
                    ins = nc.tensor.matmul(ps_h[:, k], w1s[:, k * NE // NHALF:(k + 1) * NE // NHALF, :].rearrange("p e h -> p (e h)"),
                                           xt[:, u], start=True, stop=True)
                ins.then_inc(h_ps, 1)

            def pick(n):
                pe.wait_ge(picked_done, n + 1)
                if later(n):
                    pe.wait_ge(pick_sb, n)
                for t in range(BT):
                    ins = nc.tensor.transpose(ps_pick[0:NE, t * P:(t + 1) * P], picked[:, t, :], c["ident"][:, :])
                ins.then_inc(pick_ps, 1)

            def spread_picks(n, u):
                pe.wait_ge(pick_sb, n + 1)
                if later(n):
                    pe.wait_ge(masked_done, n)
                for k in range(NHALF):
                    ins = nc.tensor.matmul(ps_mask[:, k], spread[:, k, :], pick16[:, u, :], start=True, stop=True)
                ins.then_inc(mask_ps, 1)

            def back(n, u):
                pe.wait_ge(masked_done, n + 1)
                if later(n):
                    pe.wait_ge(summed, n)
                for t in range(BT):
                    out = ps_y[:, t * P:(t + 1) * P]
                    for k in range(NHALF):
                        nc.tensor.matmul(out, masked[:, u, k, t * P:(t + 1) * P], w2[:, k, :], start=k == 0, stop=False)
                    ins = nc.tensor.matmul(out, pick32[:, u, t * P:(t + 1) * P], b2[:, :], start=False, stop=True)
                ins.then_inc(y_ps, 1)

            def unit(n, u):
                products(n + 1, 1 - u)
                spread_picks(n, u)
                if later(n):
                    back(n - 1, 1 - u)
                transpose_x(n + 2)
                pick(n + 1)

            transpose_x(0)
            products(0, 0)
            transpose_x(1)
            pick(0)
            each_pair(pe, blocks, unit)
            back(blocks - 1, (blocks - 1) % 2)

        @block.gpsimd
        def _(pool):
            def norm(n):
                if later(n):
                    pool.wait_ge(xt_ps, n)
                normalise_by_pool(pool, nc, c, xh, n, c["rstd2"], centred, BT).then_inc(xh_done, 1)

            pool.wait_ge(rstd_done, 1)
            norm(0)
            norm(1)
            each_pair(pool, blocks, lambda n, u: norm(n + 2))

        @block.scalar
        def _(act):
            take_roots(act)
            def copy_xt(n, u):
                act.wait_ge(xt_ps, n + 1)
                if later(n, 2):
                    act.wait_ge(h_ps, n - 1)
                nc.scalar.activation(xt[:, u], ps_xt, ACT.Copy).then_inc(xt_sb, 1)

            def ahead(n, u):
                act.wait_ge(h_ps, n + 1)
                if later(n, 2):
                    act.wait_ge(masked_done, n - 1)
                for k in range(NHALF):
                    ins = nc.scalar.activation(hid[:, u, k, :], ps_h[:, k], ACT.Gelu, bias=b1[:, k:k + 1])
                ins.then_inc(h_sb, 1)
                copy_xt(n + 1, 1 - u)
                act.wait_ge(pick_ps, n + 1)
                if later(n, 2):
                    act.wait_ge(y_ps, n - 1)
                nc.scalar.activation(pick16[:, u, :], ps_pick[0:NE, :], ACT.Copy)
                nc.scalar.activation(pick32[:, u, :], ps_pick[0:NE, :], ACT.Copy).then_inc(pick_sb, 1)

            act.wait_ge(ready, 1)
            copy_xt(0, 0)
            ahead(0, 0)
            each_pair(act, blocks, lambda n, u: ahead(n + 1, 1 - u))

        @block.vector
        def _(dve):
            take_rstd(dve)
            dve.sem_inc(rstd_done, 1)
            w_step, w_settle, _ = chain(dve, w_chain, 0)
            dve.wait_ge(weights, n_weights)
            w_step(nc.vector.tensor_tensor(w1s[:, :, :], w1[:, :, :], lns[:, :].rearrange("p (e o) -> p e o", o=1)
                                            .broadcast_to([P, NE, EH]), ALU.mult))
            w_step(nc.vector.tensor_copy(spread[:, :, :], spread32[:, :, :]))
            dve.wait_ge(fold_ps, 1)
            w_step(nc.vector.tensor_tensor(folded[:, :, :], ps_fold, own[:, :, :], ALU.mult))
            w_settle()
            w_step(nc.vector.tensor_reduce(foldsum[:, :], folded[:, :, :], AX.X, ALU.add))
            w_settle()
            nc.vector.tensor_tensor(b1[:, :], b1[:, :], foldsum[:, :], ALU.add).then_inc(ready, 1)

            def choose(n, step, settle):
                dve.wait_ge(logit_ps, n + 1)
                if later(n):
                    dve.wait_ge(pick_ps, n)
                for i in range(5):
                    ins = pick_step(nc, i, picked[:, :, :], ps_logit, order[:, :, :], peak[:, :], cand[:, :, :])
                    if i < 4:
                        step(ins)
                        settle()
                ins.then_inc(picked_done, 1)

            def mask(n, u):
                dve.wait_ge(mask_ps, n + 1)
                dve.wait_ge(h_sb, n + 1)
                if later(n, 2):
                    dve.wait_ge(y_ps, n - 1)
                for k in range(NHALF):
                    ins = nc.vector.tensor_tensor(masked[:, u, k, :], hid[:, u, k, :], ps_mask[:, k], ALU.mult)
                ins.then_inc(masked_done, 1)

            def finish(n, step, settle):
                dve.wait_ge(y_ps, n + 1)
                close(dve, n, step, settle, ps_y.rearrange("p (t d) -> p t d", t=BT))

            def unit(n, u):
                step, settle, steps = chain(dve, dve_chain, n * 6)
                choose(n + 1, step, settle)
                mask(n, u)
                if later(n):
                    finish(n - 1, step, settle)
                else:
                    dve.sem_inc(dve_chain, MEASURE_STEPS)
                assert steps() == (6 if later(n) else 4)

            choose(0, w_step, w_settle)
            each_pair(dve, blocks, unit)
            step, settle, steps = chain(dve, dve_chain, blocks * 6)
            finish(blocks - 1, step, settle)


FEATURE_EPS = 1e-6
DEN_EPS = 1e-6


def linear_attention_stage(c, w):
    nc = c["nc"]
    with nc.cleanup_on_exit(), ExitStack() as ctx:
        sb = lambda name, shape, dt=F32: ctx.enter_context(nc.sbuf_tensor("b_" + name, shape, dt))
        sem = lambda n: nc.alloc_semaphore("b_" + n)
        wq, wk, wv, wo, bv, bk_row, bo = (sb(n, [P, D]) for n in ("wq", "wk", "wv", "wo", "bv", "bk_row", "bo"))
        bqk, zero = sb("bqk", [P, 2]), sb("zero", [P, 2])
        own, causal = sb("own", [P, NH * VW]), sb("causal", [P, P])
        xh, xt = sb("xh", [P, TPB, D]), sb("xt", [P, 2, SEQ])
        raw = sb("raw", [P, 2, SEQ])
        qk = sb("qk", [P, 2, SEQ])
        late_q = sb("late_q", [P, 2, P])
        rest, parts = sb("rest", [P, 2, SEQ]), sb("parts", [P, 2, 3, 2, SEQ], BF16)
        stack = sb("stack", [P, 2, 2, NH, SEQ], BF16)
        kn = sb("kn", [P, D])
        kv = sb("kv", [P, 2, NH * VW])
        va = sb("va", [P, 2, TPB, NH, VW])
        am = sb("am", [P, 4, 2, TPB, P])
        ot = sb("ot", [P, NG, SEQ])
        rec, att, att_t, delta = sb("rec", [P, TPB * NH]), sb("att", [P, TPB, D]), sb("att_t", [P, SEQ]), sb("delta", [P, TPB, D])
        fresh, summed, added, add, measure, close = updater(c, ctx, "b_")
        ps_slot, ps_kv, ps_kn, ps_at, ps_o = c["psum"][:, 0:3], c["psum"][:, 2], c["psum"][:, 3, 0:P], c["psum"][:, 3, P:P + SEQ], c["psum"][:, 4:6]
        ps_qk, ps_xt, ps_v = c["psum"][:, 6], c["psum"][:, 7, 0:SEQ], c["psum"][:, 7, SEQ:2 * SEQ]
        ps_f, ps_y = c["psum"][:, 6:8], c["psum"][:, 7, 0:SEQ]

        weights, preset, cleared, rstd_done, centred, dve_chain, measure_chain, pool_chain, kept = (
            sem(n) for n in ("weights", "preset", "cleared", "rstd_done", "centred", "dve_chain", "measure_chain", "pool_chain", "kept"))
        xh_done, xt_ps, xt_sb, qk_ps, v_ps, raw_done, qk_sb, v_sb, kn_sum, kn_done, kv_ps, parts_done, stacked = (
            sem(n) for n in ("xh_done", "xt_ps", "xt_sb", "qk_ps", "v_ps", "raw_done", "qk_sb", "v_sb", "kn_sum", "kn_done",
                             "kv_ps", "parts_done", "stacked"))
        s_ready, m_done, av_done, o_done, f_ps, f_done, at_ps, at_sb, y_ps, y_used = (
            sem(n) for n in ("s_ready", "m_done", "av_done", "o_done", "f_ps", "f_done", "at_ps", "at_sb", "y_ps", "y_used"))
        n_weights = 16 * 10
        STACK = 16 * 2 * NTERM
        STEPS = NH // 2
        SLOTS = STEPS + 1
        take_roots, take_rstd = rstd_steps(c, "b_", double=False)
        block = ctx.enter_context(nc.Block())

        @block.sync
        def _(sp):
            for dst, src in ((wq, "wq"), (wk, "wk"), (wv, "wv"), (wo, "wo"), (bv, "bv"), (bk_row, "bk_row"), (bo, "bo"),
                             (bqk, "bqk"), (own, "own"), (causal, "causal")):
                sp.dma_start(dst[:, :], w[src]).then_inc(weights, 16)

            def stack_up(n, u):
                sp.wait_ge(parts_done, n + 1)
                for t in range(NTERM):
                    for side, part in ((0, Q_PART[t]), (1, K_PART[t])):
                        sp.dma_start(stack[t * DH:(t + 1) * DH, u, side], parts[:, u, part, side, :]).then_inc(stacked, 16)

            sp.wait_ge(cleared, 1)
            stack_up(0, 0)
            sp.wait_ge(preset, 4)
            stack_up(1, 1)
            each_pair(sp, c["batches"], lambda n, u: stack_up(n + 2, u))
            sp.wait_ge(stacked, STACK * (c["batches"] + 2))

        @block.gpsimd
        def _(pool):
            def norm(n):
                if later(n):
                    pool.wait_ge(xt_ps, n)
                normalise_by_pool(pool, nc, c, xh, n, c["rstd"], centred).then_inc(xh_done, 1)

            nc.gpsimd.memset(va[:, :, :, :, :], 0.0).then_inc(preset, 1)
            nc.gpsimd.memset(zero[:, :], 0.0).then_inc(preset, 1)
            pool.wait_ge(rstd_done, 1)
            norm(0)
            norm(1)
            nc.gpsimd.memset(stack[:, 1], 0.0).then_inc(preset, 1)
            pool.wait_ge(preset, 3)
            nc.gpsimd.memset(va[:, :, :, :, DH:DH + 1], 1.0).then_inc(preset, 1)

            def split(n, u):
                pool.wait_ge(qk_sb, n + 1)
                step, settle, steps = chain(pool, pool_chain, n * 2)
                hi, mid, lo = (parts[:, u, k] for k in range(3))
                step(nc.gpsimd.tensor_tensor(hi, qk[:, :, :], zero[:, :].rearrange("p (a o) -> p a o", o=1).broadcast_to([P, 2, SEQ]), ALU.add))
                settle()
                nc.gpsimd.tensor_tensor(rest[:, :, :], qk[:, :, :], hi, ALU.subtract)
                step(nc.gpsimd.tensor_tensor(mid, qk[:, :, :], hi, ALU.subtract))
                settle()
                if later(n):
                    pool.wait_ge(stacked, STACK * n)
                if later(n, 2):
                    pool.wait_ge(s_ready, STEPS * (n - 1))
                nc.gpsimd.tensor_tensor(lo, rest[:, :, :], mid, ALU.subtract).then_inc(parts_done, 1)

            split(0, 0)
            split(1, 1)

            def batch(n, u):
                norm(n + 2)
                split(n + 2, u)

            each_pair(pool, c["batches"], batch)

        @block.scalar
        def _(act):
            take_roots(act)
            def copy_xt(n, u):
                act.wait_ge(xt_ps, n + 1)
                if later(n, 2):
                    act.wait_ge(v_ps, n - 1)
                nc.scalar.activation(xt[:, u], ps_xt, ACT.Copy).then_inc(xt_sb, 1)

            def relu_qk(n):
                act.wait_ge(qk_ps, n + 1)
                if later(n):
                    act.wait_ge(qk_sb, n)
                nc.scalar.activation(raw[:, 0, :], ps_qk[:, 0:SEQ], ACT.Relu, bias=bqk[:, 0:1])
                nc.scalar.activation(raw[:, 1, :], ps_qk[:, SEQ:2 * SEQ], ACT.Relu, bias=bqk[:, 1:2]).then_inc(raw_done, 1)

            def keep(n, u):
                act.wait_ge(qk_sb, n + 1)
                if later(n, 2):
                    act.wait_ge(av_done, NG * (n - 1))
                nc.scalar.activation(late_q[:, u], qk[:, 0, P:SEQ], ACT.Copy).then_inc(kept, 1)

            def copy_out(n, g):
                act.wait_ge(av_done, n * NG + g + 1)
                if g == 0 and later(n):
                    act.wait_ge(f_ps, n)
                nc.scalar.activation(ot[:, g, :], ps_o[:, g % 2, (g // 2) * SEQ:(g // 2 + 1) * SEQ],
                                     ACT.Copy).then_inc(o_done, 1)

            def copy_att(n):
                act.wait_ge(at_ps, n + 1)
                if later(n):
                    act.wait_ge(y_ps, n)
                nc.scalar.activation(att_t[:, :], ps_at, ACT.Copy).then_inc(at_sb, 1)

            def batch(n, u):
                keep(n + 1, 1 - u)
                copy_xt(n + 2, u)
                copy_out(n, 0)
                relu_qk(n + 2)
                copy_out(n, 1)
                if later(n):
                    copy_att(n - 1)
                copy_out(n, 2)
                copy_out(n, 3)

            copy_xt(0, 0)
            act.wait_ge(weights, n_weights)
            relu_qk(0)
            keep(0, 0)
            copy_xt(1, 1)
            relu_qk(1)
            each_pair(act, c["batches"], batch)
            copy_att(c["batches"] - 1)

        @block.vector
        def _(dve):
            take_rstd(dve)
            dve.sem_inc(rstd_done, 1)
            by_head = lambda t: t.rearrange("p (o h d) -> p o h d", o=1, h=NH).broadcast_to([P, TPB, NH, DH])
            every_block = causal[:, :].rearrange("p (o q) -> p o q", o=1).broadcast_to([P, 2 * TPB, P])

            def features(n):
                dve.wait_ge(raw_done, n + 1)
                if later(n):
                    dve.wait_ge(parts_done, n)
                    dve.wait_ge(kept, n)
                nc.vector.tensor_scalar(qk[:, :, :], raw[:, :, :], FEATURE_EPS, None, ALU.add).then_inc(qk_sb, 1)

            def natural(n, u):
                dve.wait_ge(v_ps, n + 1)
                if later(n, 2):
                    dve.wait_ge(av_done, NG * (n - 1))
                nc.vector.tensor_tensor(va[:, u, :, :, 0:DH], ps_v.rearrange("p (t h d) -> p t h d", t=TPB, h=NH),
                                        by_head(bv[:, :]), ALU.add).then_inc(v_sb, 1)
                if later(n):
                    dve.wait_ge(kv_ps, n)
                nc.vector.tensor_tensor(kn[:, :], ps_kn, bk_row[:, :], ALU.add).then_inc(kn_sum, 1)
                dve.wait_ge(kn_sum, n + 1)
                nc.vector.tensor_scalar(kn[:, :], kn[:, :], 0.0, FEATURE_EPS, ALU.max, ALU.add).then_inc(kn_done, 1)

            def state(n, u):
                dve.wait_ge(kv_ps, n + 1)
                nc.vector.tensor_tensor(kv[:, u, :], ps_kv, own[:, :], ALU.mult).then_inc(m_done, 1)

            def mask(n, s):
                dve.wait_ge(s_ready, n * STEPS + s + 1)
                if s >= 4:
                    dve.wait_ge(av_done, n * NG + s // 2 - 1)
                elif s % 2 == 0 and later(n):
                    dve.wait_ge(av_done, n * NG + s // 2 - 1)
                nc.vector.tensor_tensor(am[:, s % 4].rearrange("p h t q -> p (h t) q"),
                                        ps_slot[:, s % 3].rearrange("p (b q) -> p b q", q=P), every_block, ALU.mult).then_inc(m_done, 1)

            def divide(n, step, settle):
                outs = ps_f.rearrange("p t (h v) -> p (t h) v", v=VW)
                dve.wait_ge(f_ps, n + 1)
                step(nc.vector.tensor_scalar(rec[:, :], outs[:, :, DH], DEN_EPS, None, ALU.max))
                settle()
                step(nc.vector.reciprocal(rec[:, :], rec[:, :]))
                settle()
                nc.vector.tensor_tensor(att[:, :, :].rearrange("p t (h d) -> p (t h) d", d=DH), outs[:, :, 0:DH],
                                        rec[:, :].rearrange("p (a o) -> p a o", o=1).broadcast_to([P, TPB * NH, DH]),
                                        ALU.mult).then_inc(f_done, 1)

            def divide_chain(n):
                return chain(dve, dve_chain, n * 2)[0:2]

            def measure_all(n):
                step, settle, steps = chain(dve, measure_chain, n * MEASURE_STEPS)
                dve.wait_ge(summed, n + 1)
                for part in range(3):
                    measure(dve, n, step, settle, part)
                assert steps() == MEASURE_STEPS

            def add_result(n):
                dve.wait_ge(y_ps, n + 1)
                nc.vector.tensor_tensor(delta[:, :, :], ps_y.rearrange("p (t d) -> p t d", t=TPB),
                                        bo[:, :].rearrange("p (o d) -> p o d", o=1).broadcast_to([P, TPB, D]), ALU.add).then_inc(y_used, 1)
                dve.wait_ge(y_used, n + 1)
                add(n, delta[:, :, :])

            def batch(n, u):
                for s in range(SLOTS):
                    mask(n, s) if s < STEPS else state(n + 1, 1 - u)
                    if s == 1 and later(n):
                        divide(n - 1, *divide_chain(n - 1))
                    if s == 2 and later(n, 2):
                        measure_all(n - 2)
                    if s == 4:
                        natural(n + 1, 1 - u)
                    if s == 5:
                        features(n + 2)
                    if s == STEPS and later(n):
                        add_result(n - 1)

            nc.vector.memset(stack[:, 0], 0.0).then_inc(cleared, 1)
            features(0)
            dve.wait_ge(weights, n_weights)
            dve.wait_ge(preset, 4)
            natural(0, 0)
            state(0, 0)
            features(1)
            each_pair(dve, c["batches"], batch)
            last = c["batches"] - 1
            measure_all(last - 1)
            divide(last, *divide_chain(last))
            add_result(last)
            measure_all(last)

        @block.tensor
        def _(pe):
            def transpose_x(n):
                pe.wait_ge(xh_done, n + 1)
                if later(n):
                    pe.wait_ge(xt_sb, n)
                    pe.wait_ge(v_sb, n - 1 if later(n, 2) else n)
                if later(n, 3):
                    pe.wait_ge(f_done, n - 2)
                for t in range(TPB):
                    ins = nc.tensor.transpose(ps_xt[:, t * P:(t + 1) * P], xh[:, t, :], c["ident"][:, :])
                ins.then_inc(xt_ps, 1)

            def project_qk(n, u):
                pe.wait_ge(xt_sb, n + 1)
                if later(n):
                    pe.wait_ge(raw_done, n)
                if later(n, 3):
                    pe.wait_ge(f_done, n - 2)
                nc.tensor.matmul(ps_qk[:, 0:SEQ], wq[:, :], xt[:, u], start=True, stop=True)
                nc.tensor.matmul(ps_qk[:, SEQ:2 * SEQ], wk[:, :], xt[:, u], start=True, stop=True).then_inc(qk_ps, 1)

            def project_v(n, u):
                if later(n):
                    pe.wait_ge(v_sb, n)
                    pe.wait_ge(kn_sum, n)
                    pe.wait_ge(xt_sb, n + 2)
                if later(n, 2):
                    pe.wait_ge(f_done, n - 1)
                if later(n, 3):
                    pe.wait_ge(at_sb, n - 2)
                for t in range(TPB):
                    nc.tensor.matmul(ps_v[:, t * P:(t + 1) * P], xt[:, u, t * P:(t + 1) * P], wv[:, :], start=True, stop=True)
                nc.tensor.matmul(ps_kn, xt[:, u, 0:P], wk[:, :], start=True, stop=True).then_inc(v_ps, 1)

            def state(n, u):
                pe.wait_ge(kn_done, n + 1)
                pe.wait_ge(v_sb, n + 1)
                if later(n):
                    pe.wait_ge(m_done, (n - 1) * SLOTS + SLOTS - 2)
                nc.tensor.matmul(ps_kv, kn[:, :], va[:, u, 0].rearrange("p h v -> p (h v)"), start=True, stop=True).then_inc(kv_ps, 1)

            def scores(n, u, s):
                if s == 0:
                    pe.wait_ge(stacked, STACK * (n + 1))
                if s >= 2 or later(n):
                    pe.wait_ge(m_done, n * SLOTS + s - 1)
                for j in range(2):
                    for t in range(TPB):
                        here = slice(t * P, (t + 1) * P)
                        at = (j * TPB + t) * P
                        ins = nc.tensor.matmul(ps_slot[:, s % 3, at:at + P], stack[:, u, 1, 2 * s + j, here],
                                               stack[:, u, 0, 2 * s + j, here], start=True, stop=True)
                ins.then_inc(s_ready, 1)

            def values(n, u, g):
                pe.wait_ge(m_done, n * SLOTS + 2 * (g + 1) + 1)
                if g == 0:
                    pe.wait_ge(kept, n + 1)
                if g >= 2:
                    pe.wait_ge(o_done, n * NG + g - 1)
                bank, off = ps_o[:, g % 2], (g // 2) * SEQ

                def within(t, start):
                    for j in range(GH):
                        ins = nc.tensor.matmul(bank[j * VW:(j + 1) * VW, off + t * P:off + (t + 1) * P], va[:, u, t, g * GH + j, :],
                                               am[:, (2 * g + j // 2) % 4, j % 2, t, :], start=start, stop=True, tile_position=(0, j * VW))
                    return ins

                within(0, True)
                nc.tensor.matmul(bank[:, off + P:off + SEQ], kv[:, u, g * P:(g + 1) * P], late_q[:, u], start=True, stop=False)
                within(1, False).then_inc(av_done, 1)

            def transpose_out(n):
                pe.wait_ge(o_done, NG * (n + 1))
                pe.wait_ge(xt_sb, n + 3)
                pe.wait_ge(raw_done, n + 3)
                if later(n):
                    pe.wait_ge(y_used, n)
                pe.wait_ge(v_sb, n + 2)
                for t in range(TPB):
                    for g in range(NG):
                        ins = nc.tensor.transpose(ps_f[:, t, g * P:(g + 1) * P], ot[:, g, t * P:(t + 1) * P], c["ident"][:, :])
                ins.then_inc(f_ps, 1)

            def transpose_att(n, keyed):
                pe.wait_ge(f_done, n + 1)
                pe.wait_ge(kn_sum, keyed)
                for t in range(TPB):
                    ins = nc.tensor.transpose(ps_at[:, t * P:(t + 1) * P], att[:, t, :], c["ident"][:, :])
                ins.then_inc(at_ps, 1)

            def project_out(n, projected):
                pe.wait_ge(at_sb, n + 1)
                pe.wait_ge(xt_sb, projected)
                for t in range(TPB):
                    ins = nc.tensor.matmul(ps_y[:, t * P:(t + 1) * P], att_t[:, t * P:(t + 1) * P], wo[:, :], start=True, stop=True)
                ins.then_inc(y_ps, 1)

            def batch(n, u):
                for s in range(SLOTS):
                    if s == 5:
                        if later(n):
                            transpose_att(n - 1, n + 2)
                        state(n + 1, 1 - u)
                    else:
                        scores(n, u, s + 3) if s < 5 else scores(n + 1, 1 - u, s - 6)
                    if s == 0 and later(n):
                        transpose_out(n - 1)
                    if s == 2:
                        transpose_x(n + 2)
                    if s == 3:
                        project_v(n + 1, 1 - u)
                    if s == 4:
                        project_qk(n + 2, u)
                    if s in (2, 4, 6, 8):
                        values(n, u, s // 2 - 1)
                    if s == 6 and later(n):
                        project_out(n - 1, n + 3)

            transpose_x(0)
            pe.wait_ge(weights, n_weights)
            project_qk(0, 0)
            project_v(0, 0)
            transpose_x(1)
            project_qk(1, 1)
            pe.wait_ge(preset, 4)
            state(0, 0)
            scores(0, 0, 0)
            scores(0, 0, 1)
            scores(0, 0, 2)
            each_pair(pe, c["batches"], batch)
            last = c["batches"] - 1
            transpose_out(last)
            transpose_att(last, last + 2)
            project_out(last, last + 3)


REL_CLIP = 128
UQ = P // NH // 2
NUNIT = P // UQ
REL_W = SEQ + P - 1


def attention_relative_stage(c, w):
    nc = c["nc"]
    scale = -1.0 / float(np.sqrt(DH))
    with nc.cleanup_on_exit(), ExitStack() as ctx:
        sb = lambda name, shape, dt=F32: ctx.enter_context(nc.sbuf_tensor("r_" + name, shape, dt))
        sem = lambda n: nc.alloc_semaphore("r_" + n)
        wq, wk, wv, wo, bv, bo = (sb(n, [P, D]) for n in ("wq", "wk", "wv", "wo", "bv", "bo"))
        bqk, own, part_of = sb("bqk", [P, 2]), sb("own", [P, NH]), sb("part_of", [P, 3])
        table = sb("table", [P, REL_W], BF16)
        xh, xt = sb("xh", [P, TPB, D]), sb("xt", [P, 2, SEQ])
        qt, kt = sb("qt", [P, SEQ]), sb("kt", [P, 2, SEQ])
        split_q = sb("split_q", [P, 2, SEQ])
        rest, parts = sb("rest", [P, 2, SEQ]), sb("parts", [P, 3, 2, SEQ], BF16)
        stack = sb("stack", [P, 2, NH, SEQ], BF16)
        spread = sb("spread", [P, 2, P, NH, TPB])
        va = sb("va", [P, 2, TPB, NH, VW])
        nmax = sb("nmax", [P, 2, 2])
        prob = sb("prob", [P, 2, 2, SEQ])
        pt = sb("pt", [P, TPB, NH * TPB, P])
        ot = sb("ot", [P, NG, SEQ])
        rec, att, att_t, delta = sb("rec", [P, TPB * NH]), sb("att", [P, TPB, D]), sb("att_t", [P, SEQ]), sb("delta", [P, TPB, D])
        fresh, summed, added, add, measure, close = updater(c, ctx, "r_")
        ps_s, ps_t, ps_o = c["psum"][:, 0:2], c["psum"][:, 2:4], c["psum"][:, 4:6]
        ps_qk, ps_xt, ps_v = c["psum"][:, 6], c["psum"][:, 7, 0:SEQ], c["psum"][:, 7, SEQ:2 * SEQ]
        ps_f, ps_at, ps_y = c["psum"][:, 6:8], c["psum"][:, 4, 0:SEQ], c["psum"][:, 4, SEQ:2 * SEQ]

        weights, preset, bq_ready, table_chain, table_done, pool_chain, dve_chain = (
            sem(n) for n in ("weights", "preset", "bq_ready", "table_chain", "table_done", "pool_chain", "dve_chain"))
        xh_done, xt_ps, xt_sb, qk_ps, v_ps, qk_sb, v_sb, parts_done, stacked, spread_done = (
            sem(n) for n in ("xh_done", "xt_ps", "xt_sb", "qk_ps", "v_ps", "qk_sb", "v_sb", "parts_done", "stacked", "spread_done"))
        s_ready, m_done, e_done, t_done, ce_done, co_done, av_done, o_done, f_ps, f_done, at_ps, at_sb, y_ps, y_used = (
            sem(n) for n in ("s_ready", "m_done", "e_done", "t_done", "ce_done", "co_done", "av_done", "o_done", "f_ps", "f_done",
                             "at_ps", "at_sb", "y_ps", "y_used"))
        n_weights = 16 * 10
        STACK = 16 * 2 * NTERM
        STEPS = NUNIT // 2
        table32, table_rest = (prob[:, k].rearrange("p i k -> p (i k)")[:, 0:REL_W] for k in range(2))
        table_parts = [stack[:, 1, 2 * k:2 * k + 2].rearrange("p h q -> p (h q)")[:, 0:REL_W] for k in range(3)]
        def to_pt(s):
            return pt[:, :, :, s * 2 * UQ:(s + 1) * 2 * UQ].rearrange("p k m q -> p k q m")

        def from_ps(s):
            return ps_t[:, s % 2].rearrange("p (k q m) -> p k q m", k=TPB, m=NH * TPB)

        take_roots, take_rstd = rstd_steps(c, "r_", double=False)
        block = ctx.enter_context(nc.Block())

        @block.sync
        def _(sp):
            for dst, src in ((wq, "wq"), (wk, "wk"), (wv, "wv"), (wo, "wo"), (bv, "bv"), (bo, "bo"), (bqk, "bqk"), (own, "own"),
                             (part_of, "part_of")):
                sp.dma_start(dst[:, :], w[src]).then_inc(weights, 16)
            sp.dma_start(table32, w["table"]).then_inc(weights, 16)

            def stack_up(n, u):
                sp.wait_ge(parts_done, n + 1)
                for t in range(NTERM):
                    for side in range(2):
                        row = side * P // 2 + t * DH
                        sp.dma_start(stack[row:row + DH, u], parts[:, Q_PART[t], side, :]).then_inc(stacked, 16)

            sp.wait_ge(preset, 5)
            stack_up(0, 0)
            sp.wait_ge(preset, 6)
            stack_up(1, 1)
            each_pair(sp, c["batches"], lambda n, u: stack_up(n + 2, u))
            sp.wait_ge(stacked, STACK * (c["batches"] + 2))

        @block.gpsimd
        def _(pool):
            nc.gpsimd.memset(split_q[:, :, :], 0.0).then_inc(preset, 1)
            nc.gpsimd.memset(parts[:, 0], 0.0).then_inc(preset, 1)
            nc.gpsimd.memset(va[:, :, :, :, :], 0.0).then_inc(preset, 1)
            nc.gpsimd.memset(stack[:, 0], 0.0).then_inc(preset, 1)
            pool.wait_ge(preset, 4)
            nc.gpsimd.memset(va[:, :, :, :, DH:DH + 1], 1.0).then_inc(preset, 1)

            def split(n, u):
                pool.wait_ge(qk_sb, n + 1)
                if later(n):
                    pool.wait_ge(stacked, STACK * n)
                if later(n, 2):
                    pool.wait_ge(s_ready, STEPS * (n - 1))
                step, settle, steps = chain(pool, pool_chain, n)
                hi, mid, lo = (parts[:, k] for k in range(3))
                nc.gpsimd.tensor_tensor(rest[:, :, :], split_q[:, :, :], hi, ALU.subtract)
                step(nc.gpsimd.tensor_tensor(mid, split_q[:, :, :], hi, ALU.subtract))
                settle()
                nc.gpsimd.tensor_tensor(lo, rest[:, :, :], mid, ALU.subtract).then_inc(parts_done, 1)
                nc.gpsimd.tensor_tensor(spread[:, u], qt[:, :].rearrange("p (t q o) -> p q o t", t=TPB, o=1).broadcast_to([P, P, NH, TPB]),
                                        own[:, :].rearrange("p (o h t) -> p o h t", o=1, t=1).broadcast_to([P, P, NH, TPB]),
                                        ALU.mult).then_inc(spread_done, 1)

            split(0, 0)
            pool.wait_ge(table_done, 1)
            nc.gpsimd.memset(stack[:, 1], 0.0).then_inc(preset, 1)
            split(1, 1)
            each_pair(pool, c["batches"], lambda n, u: split(n + 2, u))

        @block.scalar
        def _(act):
            take_roots(act)
            def copy_xt(n, u):
                act.wait_ge(xt_ps, n + 1)
                if later(n, 2):
                    act.wait_ge(v_ps, n - 1)
                nc.scalar.activation(xt[:, u], ps_xt, ACT.Copy).then_inc(xt_sb, 1)

            def copy_qk(n, u):
                act.wait_ge(qk_ps, n + 1)
                if later(n):
                    act.wait_ge(spread_done, n)
                    act.wait_ge(stacked, STACK * n)
                if later(n, 2):
                    act.wait_ge(s_ready, STEPS * (n - 1))
                nc.scalar.activation(kt[:, u, :], ps_qk[:, SEQ:2 * SEQ], ACT.Identity, bias=bqk[:, 1:2])
                nc.scalar.activation(qt[:, :], ps_qk[:, 0:SEQ], ACT.Identity, bias=bqk[:, 0:1], scale=scale)

            def copy_split_q(n):
                for dst in (split_q, parts[:, 0]):
                    for side in range(2):
                        own_tile = slice(side * P, (side + 1) * P)
                        ins = nc.scalar.activation(dst[:, side, own_tile], ps_qk[:, own_tile], ACT.Identity,
                                                   bias=bqk[:, 0:1], scale=scale)
                ins.then_inc(qk_sb, 1)

            def exps(n, s):
                h = n * STEPS + s
                act.wait_ge(m_done, h + 1)
                if s >= 2 or later(n):
                    act.wait_ge(t_done, h - 1)
                for i in range(2):
                    ins = nc.scalar.activation(prob[:, s % 2, i, :], ps_s[:, s % 2, i * SEQ:(i + 1) * SEQ], ACT.Exp,
                                               bias=nmax[:, s % 2, i:i + 1], scale=-1.0)
                ins.then_inc(e_done, 1)

            def copy_pt(n, s):
                act.wait_ge(t_done, n * STEPS + s + 1)
                if s == 1 and later(n):
                    act.wait_ge(av_done, n * NG)
                nc.scalar.activation(to_pt(s), from_ps(s), ACT.Copy).then_inc(co_done, 1)

            def copy_out(n, g):
                act.wait_ge(av_done, n * NG + g + 1)
                if g == 0 and later(n):
                    act.wait_ge(f_ps, n)
                nc.scalar.activation(ot[:, g, :], ps_o[:, g % 2, (g // 2) * SEQ:(g // 2 + 1) * SEQ],
                                     ACT.Copy).then_inc(o_done, 1)

            def copy_att(n):
                act.wait_ge(at_ps, n + 1)
                if later(n):
                    act.wait_ge(y_ps, n)
                nc.scalar.activation(att_t[:, :], ps_at, ACT.Copy).then_inc(at_sb, 1)

            def outputs(n):
                for g in range(NG):
                    copy_out(n, g)

            def batch(n, u):
                for s in range(STEPS):
                    if s == 0 and later(n):
                        copy_pt(n - 1, STEPS - 1)
                    exps(n, s + 1) if s + 1 < STEPS else exps(n + 1, 0)
                    if s == 0 and later(n):
                        outputs(n - 1)
                    if s == 1 and not later(n):
                        copy_qk(1, 1)
                        copy_split_q(1)
                    if s % 2 == 0 and s:
                        copy_pt(n, s - 1)
                    if s == 4 and later(n):
                        copy_att(n - 1)
                    if s == 10:
                        copy_xt(n + 2, u)
                    if s == STEPS - 2:
                        copy_qk(n + 2, u)
                    if s == STEPS - 1:
                        copy_split_q(n + 2)

            copy_xt(0, 0)
            act.wait_ge(weights, n_weights)
            nc.scalar.mul(bqk[:, 0:1], bqk[:, 0:1], scale).then_inc(bq_ready, 1)
            act.wait_ge(bq_ready, 1)
            act.wait_ge(preset, 5)
            copy_qk(0, 0)
            copy_split_q(0)
            copy_xt(1, 1)
            exps(0, 0)
            each_pair(act, c["batches"], batch)
            copy_pt(c["batches"] - 1, STEPS - 1)
            outputs(c["batches"] - 1)
            copy_att(c["batches"] - 1)

        @block.vector
        def _(dve):
            take_rstd(dve)
            bvb = bv[:, :].rearrange("p (o h d) -> p o h d", o=1, h=NH).broadcast_to([P, TPB, NH, DH])
            def norm(n):
                if later(n):
                    dve.wait_ge(xt_ps, n)
                normalise(nc.vector, c, xh, n, c["rstd"]).then_inc(xh_done, 1)

            def copy_v(n, u):
                dve.wait_ge(v_ps, n + 1)
                if later(n, 2):
                    dve.wait_ge(av_done, NG * (n - 1))
                nc.vector.tensor_tensor(va[:, u, :, :, 0:DH], ps_v.rearrange("p (t h d) -> p t h d", t=TPB, h=NH), bvb,
                                        ALU.add).then_inc(v_sb, 1)

            def maxima(n, s):
                h = n * STEPS + s
                dve.wait_ge(s_ready, h + 1)
                if s >= 2 or later(n):
                    dve.wait_ge(e_done, h - 1)
                nc.vector.tensor_reduce(nmax[:, s % 2, :], ps_s[:, s % 2].rearrange("p (i k) -> p i k", i=2), AX.X,
                                        ALU.min).then_inc(m_done, 1)

            def copy_pt(n, s):
                dve.wait_ge(t_done, n * STEPS + s + 1)
                if s == 0 and later(n):
                    dve.wait_ge(av_done, n * NG)
                nc.vector.tensor_copy(to_pt(s), from_ps(s)).then_inc(ce_done, 1)

            def divide(n, step, settle):
                outs = ps_f.rearrange("p t (h v) -> p (t h) v", v=VW)
                dve.wait_ge(f_ps, n + 1)
                step(nc.vector.reciprocal(rec[:, :], outs[:, :, DH]))
                settle()
                nc.vector.tensor_tensor(att[:, :, :].rearrange("p t (h d) -> p (t h) d", d=DH), outs[:, :, 0:DH],
                                        rec[:, :].rearrange("p (a o) -> p a o", o=1).broadcast_to([P, TPB * NH, DH]),
                                        ALU.mult).then_inc(f_done, 1)

            def add_result(n):
                dve.wait_ge(y_ps, n + 1)
                nc.vector.tensor_tensor(delta[:, :, :], ps_y.rearrange("p (t d) -> p t d", t=TPB),
                                        bo[:, :].rearrange("p (o d) -> p o d", o=1).broadcast_to([P, TPB, D]), ALU.add).then_inc(y_used, 1)
                dve.wait_ge(y_used, n + 1)
                add(n, delta[:, :, :])

            def batch(n, u):
                step, settle, steps = chain(dve, dve_chain, (n - 1) * 3)
                for s in range(STEPS):
                    maxima(n, s + 1) if s + 1 < STEPS else maxima(n + 1, 0)
                    if s % 2:
                        copy_pt(n, s - 1)
                    if s == 3 and later(n):
                        divide(n - 1, step, settle)
                    if s == 5:
                        norm(n + 2)
                    if s == 7 and later(n):
                        add_result(n - 1)
                    if s in (8, 9, 10) and later(n):
                        dve.wait_ge(summed, n)
                        measure(dve, n - 1, step, settle, s - 8)
                    if s == 12:
                        copy_v(n + 1, 1 - u)

            norm(0)
            norm(1)
            step, settle, steps = chain(dve, table_chain, 0)
            dve.wait_ge(weights, n_weights)
            hi, mid, lo = table_parts
            step(nc.vector.tensor_copy(hi, table32))
            settle()
            step(nc.vector.tensor_tensor(table_rest, table32, hi, ALU.subtract))
            settle()
            step(nc.vector.tensor_copy(mid, table_rest))
            settle()
            step(nc.vector.tensor_tensor(lo, table_rest, mid, ALU.subtract))
            step(nc.vector.tensor_scalar(table[:, :], hi, part_of[:, 0:1], None, ALU.mult))
            settle()
            step(nc.vector.scalar_tensor_tensor(table[:, :], mid, part_of[:, 1:2], table[:, :], ALU.mult, ALU.add))
            settle()
            nc.vector.scalar_tensor_tensor(table[:, :], lo, part_of[:, 2:3], table[:, :], ALU.mult, ALU.add).then_inc(table_done, 1)
            dve.wait_ge(preset, 5)
            copy_v(0, 0)
            maxima(0, 0)
            each_pair(dve, c["batches"], batch)
            last = c["batches"] - 1
            step, settle, steps = chain(dve, dve_chain, last * 3)
            divide(last, step, settle)
            add_result(last)
            dve.wait_ge(summed, last + 1)
            for part in range(3):
                measure(dve, last, step, settle, part)

        @block.tensor
        def _(pe):
            def transpose_x(n):
                pe.wait_ge(xh_done, n + 1)
                if later(n):
                    pe.wait_ge(xt_sb, n)
                    pe.wait_ge(v_sb, n - 1 if later(n, 2) else n)
                if later(n, 3):
                    pe.wait_ge(f_done, n - 2)
                for t in range(TPB):
                    ins = nc.tensor.transpose(ps_xt[:, t * P:(t + 1) * P], xh[:, t, :], c["ident"][:, :])
                ins.then_inc(xt_ps, 1)

            def project_qk(n, u):
                pe.wait_ge(xt_sb, n + 1)
                if later(n):
                    pe.wait_ge(qk_sb, n)
                nc.tensor.matmul(ps_qk[:, 0:SEQ], wq[:, :], xt[:, u], start=True, stop=True)
                nc.tensor.matmul(ps_qk[:, SEQ:2 * SEQ], wk[:, :], xt[:, u], start=True, stop=True).then_inc(qk_ps, 1)

            def project_v(n, u):
                if later(n):
                    pe.wait_ge(v_sb, n)
                    pe.wait_ge(xt_sb, n + 2)
                if later(n, 2):
                    pe.wait_ge(f_done, n - 1)
                for t in range(TPB):
                    ins = nc.tensor.matmul(ps_v[:, t * P:(t + 1) * P], xt[:, u, t * P:(t + 1) * P], wv[:, :], start=True, stop=True)
                ins.then_inc(v_ps, 1)

            def pair_stack(u, q):
                return stack[:, u].rearrange("p h (t q) -> p (h t) q", t=TPB)[:, :, q]

            def scores(n, u, s):
                h = n * STEPS + s
                if s == 0:
                    pe.wait_ge(stacked, STACK * (n + 1))
                    pe.wait_ge(spread_done, n + 1)
                if s >= 2 or later(n):
                    pe.wait_ge(e_done, h - 1)
                for i in range(2):
                    q0 = (2 * s + i) * UQ
                    nc.tensor.matmul(ps_s[:, s % 2, i * SEQ:(i + 1) * SEQ], spread[:, u, q0:q0 + UQ].rearrange("p q h t -> p (q h t)"),
                                     kt[:, u, :], start=True, stop=False)
                    for j in range(UQ):
                        both, at = pair_stack(u, q0 + j), P - 1 - (q0 + j)
                        row, width = j * NH * TPB, NH * TPB
                        ins = nc.tensor.matmul(ps_s[row:row + width, s % 2, i * SEQ:(i + 1) * SEQ], both, table[:, at:at + SEQ],
                                               start=False, stop=True, tile_position=(0, row))
                ins.then_inc(s_ready, 1)

            def transpose_p(n, s):
                pe.wait_ge(e_done, n * STEPS + s + 1)
                if s >= 2 or later(n):
                    pe.wait_ge(co_done if s % 2 else ce_done, n * (STEPS // 2) + s // 2)
                for i in range(2):
                    for k in range(TPB):
                        ins = nc.tensor.transpose(ps_t[:, s % 2, k * SEQ + i * P:k * SEQ + (i + 1) * P],
                                                  prob[:, s % 2, i, k * P:(k + 1) * P], c["ident"][:, :])
                ins.then_inc(t_done, 1)

            def values(n, u, g):
                if g == 0:
                    pe.wait_ge(ce_done, (n + 1) * (STEPS // 2))
                    pe.wait_ge(co_done, (n + 1) * (STEPS // 2))
                    pe.wait_ge(v_sb, n + 1)
                if g == 0 and later(n):
                    pe.wait_ge(y_used, n)
                if g >= 2:
                    pe.wait_ge(o_done, n * NG + g - 1)
                for k in range(TPB):
                    for j in range(GH):
                        ins = nc.tensor.matmul(ps_o[j * VW:(j + 1) * VW, g % 2, (g // 2) * SEQ:(g // 2 + 1) * SEQ],
                                               va[:, u, k, g * GH + j, :], pt[:, k, (g * GH + j) * TPB:(g * GH + j + 1) * TPB, :].rearrange("p t q -> p (t q)"),
                                               start=k == 0, stop=k == TPB - 1, tile_position=(0, j * VW))
                ins.then_inc(av_done, 1)

            def transpose_out(n):
                pe.wait_ge(o_done, NG * (n + 1))
                pe.wait_ge(xt_sb, n + 3)
                pe.wait_ge(qk_sb, n + 3)
                pe.wait_ge(v_sb, n + 2)
                for t in range(TPB):
                    for g in range(NG):
                        ins = nc.tensor.transpose(ps_f[:, t, g * P:(g + 1) * P], ot[:, g, t * P:(t + 1) * P], c["ident"][:, :])
                ins.then_inc(f_ps, 1)

            def transpose_att(n):
                pe.wait_ge(f_done, n + 1)
                for t in range(TPB):
                    ins = nc.tensor.transpose(ps_at[:, t * P:(t + 1) * P], att[:, t, :], c["ident"][:, :])
                ins.then_inc(at_ps, 1)

            def project_out(n):
                pe.wait_ge(at_sb, n + 1)
                for t in range(TPB):
                    ins = nc.tensor.matmul(ps_y[:, t * P:(t + 1) * P], att_t[:, t * P:(t + 1) * P], wo[:, :], start=True, stop=True)
                ins.then_inc(y_ps, 1)

            def batch(n, u):
                for s in range(STEPS):
                    scores(n, u, s + 2) if s + 2 < STEPS else scores(n + 1, 1 - u, s + 2 - STEPS)
                    if s == 0 and later(n):
                        for g in range(NG):
                            values(n - 1, 1 - u, g)
                    transpose_p(n, s)
                    if s == 2 and later(n):
                        transpose_out(n - 1)
                    if s == 4 and later(n):
                        transpose_att(n - 1)
                    if s == 6 and later(n):
                        project_out(n - 1)
                    if s == 9:
                        transpose_x(n + 2)
                    if s == 11:
                        project_qk(n + 2, u)
                        project_v(n + 1, 1 - u)

            transpose_x(0)
            pe.wait_ge(weights, n_weights)
            project_qk(0, 0)
            project_v(0, 0)
            transpose_x(1)
            project_qk(1, 1)
            pe.wait_ge(table_done, 1)
            scores(0, 0, 0)
            scores(0, 0, 1)
            each_pair(pe, c["batches"], batch)
            last = c["batches"] - 1
            for g in range(NG):
                values(last, last % 2, g)
            transpose_out(last)
            transpose_att(last)
            project_out(last)


def lay_out(inputs):
    a = {k: np.asarray(v) for k, v in inputs.items()}
    rows = lambda v: np.broadcast_to(v.reshape(1, -1), (P, v.size))
    by_width = lambda m: m.reshape(m.shape[0], NH, DH).transpose(0, 2, 1).reshape(m.shape[0], D)
    q, k = np.arange(SEQ)[:, None], np.arange(SEQ)[None, :]
    toeplitz = a["L0_attn_a_rel_emb"][:, q - k + SEQ - 1]
    of_expert = np.arange(NHALF * P).reshape(NHALF, P) // EH
    one_of = (of_expert[:, :, None] == np.arange(NE)).astype(np.float32)
    out = {
        "x": a["L0_attn_a_x"],
        "ident": np.eye(P, dtype=np.float32),
        "a_wq": by_width(a["L0_attn_a_Wq"]), "a_wk": by_width(a["L0_attn_a_Wk"]), "a_wv": a["L0_attn_a_Wv"],
        "a_bv": rows(a["L0_attn_a_bv"]),
        "a_bqk": np.stack([by_width(a["L0_attn_a_bq"][None])[0], by_width(a["L0_attn_a_bk"][None])[0]], 1),
        "a_bias": toeplitz.reshape(NH, TPB, P, SEQ).transpose(2, 0, 1, 3),
        "f_w1": a["L0_ffn_W1"].transpose(1, 0, 2), "f_b1": a["L0_ffn_b1"].reshape(NHALF, P).T,
        "f_lns": a["L0_ffn_ln_scale"].T, "f_lnb": a["L0_ffn_ln_bias"].T, "f_wg": a["L0_ffn_Wg"].T,
        "f_own": one_of.transpose(1, 0, 2), "f_spread": one_of.transpose(2, 0, 1),
        "f_w2": a["L0_ffn_W2"].reshape(NHALF, P, D).transpose(1, 0, 2), "f_b2": a["L0_ffn_b2"],
        "f_order": np.broadcast_to(np.arange(NE, 0, -1, dtype=np.float32), (P, BT, NE)),
    }
    qkv_w, qkv_b = a["L0_attn_b_qkv_w"].reshape(3, D, D), a["L0_attn_b_qkv_b"].reshape(3, D)
    head_of = np.arange(P) % NH
    out |= {
        "b_wq": by_width(qkv_w[0].T), "b_wk": by_width(qkv_w[1].T), "b_wv": qkv_w[2].T, "b_wo": a["L0_attn_b_out_w"].T,
        "b_bv": rows(qkv_b[2]), "b_bk_row": rows(by_width(qkv_b[1:2])[0]), "b_bo": rows(a["L0_attn_b_out_b"]),
        "b_bqk": np.stack([by_width(qkv_b[0:1])[0], by_width(qkv_b[1:2])[0]], 1),
        "b_own": (head_of[:, None] == np.arange(NH * VW) // VW).astype(np.float32),
        "b_causal": np.triu(np.ones((P, P), np.float32)),
    }
    rel = a["L1_attn_a_rel_emb"]
    table, part_of = np.zeros((P, REL_W), np.float32), np.zeros((P, 3), np.float32)
    for j in range(2):
        distance = np.clip(np.arange(REL_W) - (P - 1) - j * P, -REL_CLIP, REL_CLIP) + REL_CLIP
        for t in range(NTERM):
            at = j * P // 2 + t * DH
            table[at:at + DH] = rel[distance].T
            part_of[at:at + DH, K_PART[t]] = 1.0
    out |= {
        "r_wq": by_width(a["L1_attn_a_Wq"].T), "r_wk": by_width(a["L1_attn_a_Wk"].T), "r_wv": a["L1_attn_a_Wv"].T,
        "r_wo": a["L1_attn_a_Wo"].T, "r_bv": rows(a["L1_attn_a_bv"]), "r_bo": rows(a["L1_attn_a_bo"]),
        "r_bqk": np.stack([by_width(a["L1_attn_a_bq"][None])[0], by_width(a["L1_attn_a_bk"][None])[0]], 1),
        "r_own": (head_of[:, None] == np.arange(NH)).astype(np.float32), "r_table": table, "r_part_of": part_of,
    }
    w_qkv = a["L1_attn_b_w_qkv"].reshape(3, NH * CH, D)
    out |= {
        "c_wq": w_qkv[0].T, "c_wk": w_qkv[1].T, "c_wv": w_qkv[2].T,
        "c_wo": a["L1_attn_b_w_out"].T.reshape(NC, P, D).transpose(1, 0, 2),
        "c_mask": np.concatenate([np.zeros((P, P)), np.triu(np.full((P, P), BIG), 1)], 1).astype(np.float32),
    }
    shared, routed = a["L1_ffn_w_shared_in"], a["L1_ffn_w1_shared"]
    hidden = a["L1_ffn_w_shared_out"].shape[0]
    out |= {
        "g_in": np.stack([m.reshape(D, 2, hidden) for m in (shared, routed)], 1),
        "g_shared_out": a["L1_ffn_w_shared_out"], "g_w2": a["L1_ffn_w2"].transpose(1, 0, 2), "g_gate": a["L1_ffn_w_gate"],
        "g_gbias": np.broadcast_to(a["L1_ffn_gate_bias"], (P, BT, NE)), "g_order": out["f_order"],
    }
    return {k: np.ascontiguousarray(v) for k, v in out.items()}


def build(nc, w, out, stages=None):
    with ExitStack() as ctx:
        c = core(nc, ctx, w["x"].shape[0])
        sub = lambda p: {k[len(p):]: v for k, v in w.items() if k.startswith(p)}
        run = lambda k: stages is None or k in stages
        if run(1):
            attention_bias_stage(c, sub("a_"), w["x"], w["ident"])
        else:
            load_stage(c, w["x"], w["ident"])
        if run(2):
            expert_stage(c, sub("f_"), "f0_")
        if run(3):
            linear_attention_stage(c, sub("b_"))
        if run(4):
            expert_stage(c, sub("f_"), "f1_")
        if run(5):
            attention_relative_stage(c, sub("r_"))
        if run(6):
            gated_expert_stage(c, sub("g_"), "g0_")
        if run(7):
            causal_attention_stage(c, sub("c_"))
        if run(8):
            gated_expert_stage(c, sub("g_"), "g1_", out)
        else:
            store_stage(c, out)


def kernel(**inputs):
    import concourse.bacc as bacc
    from concourse.bass_utils import run_bass_kernel_spmd

    nc = bacc.Bacc("TRN2", target_bir_lowering=False, num_devices=1)
    arrays = lay_out(inputs)
    w = {k: nc.dram_tensor("in_" + k, v.shape, mybir.dt.from_np(v.dtype), kind="ExternalInput").ap() for k, v in arrays.items()}
    out = nc.dram_tensor("out", arrays["x"].shape, F32, kind="ExternalOutput").ap()
    build(nc, w, out)
    result = run_bass_kernel_spmd(nc, [{"in_" + k: v for k, v in arrays.items()}], core_ids=[0])
    return result.results[0]["out"]
```
